# Optimizing a Trainium2 kernel written in Bass

```python
import numpy as np
import jax
import jax.numpy as jnp

def _softmax(x, axis=-1):
    return jax.nn.softmax(x, axis=axis)

def _gelu(x):
    return jax.nn.gelu(x, approximate=True)

def _silu(x):
    return jax.nn.silu(x)

def _sigmoid(x):
    return jax.nn.sigmoid(x)

def _layernorm(x, axis=-1, eps=1e-05):
    m = jnp.mean(x, axis=axis, keepdims=True)
    v = jnp.var(x, axis=axis, keepdims=True)
    return (x - m) / jnp.sqrt(v + eps)

def _scatter_add(tgt, idx, src, axis=0):
    return tgt.at[idx].add(src)

def _segment_sum(src, seg, n):
    return jax.ops.segment_sum(src, seg, n)
kernel_name = 'mk_xattn_ffn_d4_seqx_r8_7c3b1a'

def setup_inputs(seed: int=0):
    np.random.seed(seed)
    _w = jnp.asarray

    def _rec_inputs():
        import jax
        import jax.numpy as jnp
        _rk = jax.random.key(seed)
        x = -0.0002928 + 1 * jax.random.normal(jax.random.fold_in(_rk, 1), (64, 64, 128), jnp.float32)
        _lenS = 64 - jax.random.randint(jax.random.fold_in(_rk, 7), (64,), 0, max(1, 64 // 4) + 1, jnp.int32)
        _lenS2 = 64 - jax.random.randint(jax.random.fold_in(_rk, 8), (64,), 0, max(1, 64 // 4) + 1, jnp.int32)
        _ctx_1024P = jax.random.normal(jax.random.fold_in(_rk, 11), (64, 16, 128), jnp.float32)
        _ctx_1024c = jax.random.dirichlet(jax.random.fold_in(_rk, 511), 0.3 * jnp.ones((16,), jnp.float32), (64, 64))
        _ctx_1024t = jnp.einsum('bsk,bkd->bsd', _ctx_1024c, _ctx_1024P)
        _ctx_1024t = _ctx_1024t * jax.lax.rsqrt(jnp.mean(jnp.square(_ctx_1024t)) + 1e-12) * 0.953939
        ctx_1024 = -1.39393e-06 + 0.999914 * (_ctx_1024t + 0.3 * jax.random.normal(jax.random.fold_in(_rk, 611), (64, 64, 128), jnp.float32))
        itok_BxS2_0_2047 = jax.random.randint(jax.random.fold_in(_rk, 14), (64, 64), 0, 256, jnp.int32)
        _validS = jnp.arange(64)[None, :] < _lenS[:, None]
        _validS2 = jnp.arange(64)[None, :] < _lenS2[:, None]
        _causal = jnp.tril(jnp.ones((64, 64), dtype=bool))
        mask_Bx16xSxS2_ff0 = jnp.where(jnp.ones((64, 16, 64, 64), dtype=bool), 0.0, -1000000000.0).astype(jnp.float32)
        mask_1x1xSxS2_ik1 = jnp.where(jnp.broadcast_to(_validS2[0:1, None, None, :], (1, 1, 64, 64)), 1, 0).astype(jnp.int32)
        return (x, ctx_1024, itok_BxS2_0_2047, mask_Bx16xSxS2_ff0, mask_1x1xSxS2_ik1)
    x, ctx_1024, itok_BxS2_0_2047, mask_Bx16xSxS2_ff0, mask_1x1xSxS2_ik1 = _rec_inputs()

    def _L0_xattn_setup():
        import jax, jax.numpy as jnp
        import numpy as np
        B, S, D = (2, 256, 128)
        H = 16
        DH = D // H
        LAMBDA_INIT = 0.8
        EPS = 1e-05
        SCALE = 1.0 / np.sqrt(DH)
        key = jax.random.key(seed)
        ks = jax.random.split(key, 13)
        inp = {'query': jax.random.normal(ks[0], (B, S, D), jnp.float32), 'key': jax.random.normal(ks[1], (B, S, D), jnp.float32), 'value': jax.random.normal(ks[2], (B, S, D), jnp.float32), 'attn_mask': jnp.zeros((B, H, S, S), jnp.float32), 'W_q': jax.random.normal(ks[3], (D, 2 * DH * H), jnp.float32) * 0.02, 'W_k': jax.random.normal(ks[4], (D, 2 * DH * H), jnp.float32) * 0.02, 'W_v': jax.random.normal(ks[5], (D, DH * H), jnp.float32) * 0.02, 'W_o': jax.random.normal(ks[6], (DH * H, D), jnp.float32) * 0.02, 'lambda_q1': jax.random.normal(ks[7], (H, DH), jnp.float32) * 0.1, 'lambda_k1': jax.random.normal(ks[8], (H, DH), jnp.float32) * 0.1, 'lambda_q2': jax.random.normal(ks[9], (H, DH), jnp.float32) * 0.1, 'lambda_k2': jax.random.normal(ks[10], (H, DH), jnp.float32) * 0.1, 'rms_scale': jnp.ones((DH,), jnp.float32)}
        return inp
    _L0_xattn_all = _L0_xattn_setup()
    _L0_xattn_in = {k: v for k, v in _L0_xattn_all.items() if k in ('W_q', 'W_k', 'W_v', 'W_o', 'lambda_q1', 'lambda_k1', 'lambda_q2', 'lambda_k2', 'rms_scale')}
    del _L0_xattn_all

    def _L0_ffn_setup():
        import jax, jax.numpy as jnp
        import numpy as np
        LN_EPS = 1e-05

        def layernorm(x, g, b):
            mu = jnp.mean(x, axis=-1, keepdims=True)
            var = jnp.mean((x - mu) ** 2, axis=-1, keepdims=True)
            return (x - mu) * jax.lax.rsqrt(var + LN_EPS) * g + b

        def act_quant_fake(x):
            scale = 127.0 / jnp.clip(jnp.max(jnp.abs(x), axis=-1, keepdims=True), 1e-05)
            return jnp.clip(jnp.round(x * scale), -128.0, 127.0) / scale

        def weight_quant_fake(w):
            scale = 1.0 / jnp.clip(jnp.mean(jnp.abs(w)), 1e-05)
            return jnp.clip(jnp.round(w * scale), -1.0, 1.0) / scale

        def bitlinear(x, w, b):
            dqx = act_quant_fake(x)
            dqw = weight_quant_fake(w)
            return jnp.einsum('btd,hd->bth', dqx, dqw) + b
        key = jax.random.key(seed)
        ks = jax.random.split(key, 5)
        B, T, D, H = (8, 512, 128, 512)
        return {'x': jax.random.normal(ks[0], (B, T, D), dtype=jnp.float32), 'ln1_g': jnp.ones((D,), jnp.float32), 'ln1_b': jnp.zeros((D,), jnp.float32), 'w1': jax.random.normal(ks[1], (H, D), dtype=jnp.float32) * (1.0 / np.sqrt(D)), 'b1': jax.random.normal(ks[2], (H,), dtype=jnp.float32) * 0.02, 'ln2_g': jnp.ones((H,), jnp.float32), 'ln2_b': jnp.zeros((H,), jnp.float32), 'w2': jax.random.normal(ks[3], (D, H), dtype=jnp.float32) * (1.0 / np.sqrt(H)), 'b2': jax.random.normal(ks[4], (D,), jnp.float32) * 0.02}
    _L0_ffn_all = _L0_ffn_setup()
    _L0_ffn_in = {k: v for k, v in _L0_ffn_all.items() if k in ('ln1_g', 'ln1_b', 'w1', 'b1', 'ln2_g', 'ln2_b', 'w2', 'b2')}
    del _L0_ffn_all

    def _L1_xattn_setup():
        import jax, jax.numpy as jnp
        import numpy as np
        B, S, H, NH = (2, 256, 128, 16)
        HD = H // NH
        NEG = -1000000.0

        def _split(t):
            b, s, h = t.shape
            return t.reshape(b, s, NH, h // NH).transpose(0, 2, 1, 3)
        key = jax.random.key(seed)
        ks = jax.random.split(key, 12)
        sc = 0.02
        inp = {'q': jax.random.normal(ks[0], (B, S, H), jnp.float32), 'k': jax.random.normal(ks[1], (B, S, H), jnp.float32), 'v': jax.random.normal(ks[2], (B, S, H), jnp.float32), 'mask': jax.random.randint(ks[3], (1, 1, S, S), 0, 2, jnp.int32), 'wq': jax.random.normal(ks[4], (H, H), jnp.float32) * sc, 'bq': jnp.zeros((H,), jnp.float32), 'wk': jax.random.normal(ks[5], (H, H), jnp.float32) * sc, 'bk': jnp.zeros((H,), jnp.float32), 'wv': jax.random.normal(ks[6], (H, H), jnp.float32) * sc, 'bv': jnp.zeros((H,), jnp.float32), 'wo': jax.random.normal(ks[7], (H, H), jnp.float32) * sc, 'bo': jnp.zeros((H,), jnp.float32)}
        return inp
    _L1_xattn_all = _L1_xattn_setup()
    _L1_xattn_in = {k: v for k, v in _L1_xattn_all.items() if k in ('wq', 'bq', 'wk', 'bk', 'wv', 'bv', 'wo', 'bo')}
    del _L1_xattn_all

    def _L1_ffn_setup():
        import jax, jax.numpy as jnp
        import numpy as np
        DIM = 128
        HID = 512
        E = 8
        TOPK = 2
        ALPHA = 2.0
        B, T = (1, 256)
        DOWN_SCALE = 0.01
        key = jax.random.key(seed)
        ks = jax.random.split(key, 8)
        s = 1.0 / np.sqrt(DIM)
        sh = 1.0 / np.sqrt(HID)
        return {'x': jax.random.normal(ks[0], (B, T, DIM), jnp.float32), 'w_router': jax.random.uniform(ks[1], (DIM, E), jnp.float32, -s, s), 'w_up': jax.random.uniform(ks[2], (E - 1, DIM, HID), jnp.float32, -s, s), 'w_gate': jax.random.uniform(ks[3], (E - 1, DIM, HID), jnp.float32, -s, s), 'w_down': jax.random.normal(ks[4], (E - 1, HID, DIM), jnp.float32) * DOWN_SCALE, 'ws_up': jax.random.uniform(ks[5], (DIM, HID), jnp.float32, -s, s), 'ws_gate': jax.random.uniform(ks[6], (DIM, HID), jnp.float32, -s, s), 'ws_down': jax.random.normal(ks[7], (HID, DIM), jnp.float32) * DOWN_SCALE}
    _L1_ffn_all = _L1_ffn_setup()
    _L1_ffn_in = {k: v for k, v in _L1_ffn_all.items() if k in ('w_router', 'w_up', 'w_gate', 'w_down', 'ws_up', 'ws_gate', 'ws_down')}
    del _L1_ffn_all

    def _L2_xattn_setup():
        import jax, jax.numpy as jnp
        import numpy as np
        D_MODEL = 128
        HEAD = 16
        key = jax.random.key(seed)
        ks = jax.random.split(key, 11)
        B, S, D = (2, 256, D_MODEL)
        s = 1.0 / np.sqrt(D)
        return {'query': jax.random.normal(ks[0], (B, S, D), jnp.float32), 'value': jax.random.normal(ks[1], (B, S, D), jnp.float32), 'key': jax.random.normal(ks[2], (B, S, D), jnp.float32), 'Wq_w': jax.random.normal(ks[3], (D, D), jnp.float32) * s, 'Wq_b': jnp.zeros((D,), jnp.float32), 'Wk_w': jax.random.normal(ks[4], (D, D), jnp.float32) * s, 'Wk_b': jnp.zeros((D,), jnp.float32), 'Wv_w': jax.random.normal(ks[5], (D, D), jnp.float32) * s, 'Wv_b': jnp.zeros((D,), jnp.float32), 'Wo_w': jax.random.normal(ks[6], (D, D), jnp.float32) * s, 'Wo_b': jnp.zeros((D,), jnp.float32)}
    _L2_xattn_all = _L2_xattn_setup()
    _L2_xattn_in = {k: v for k, v in _L2_xattn_all.items() if k in ('Wq_w', 'Wq_b', 'Wk_w', 'Wk_b', 'Wv_w', 'Wv_b', 'Wo_w', 'Wo_b')}
    del _L2_xattn_all

    def _L2_ffn_setup():
        import jax, jax.numpy as jnp
        import numpy as np
        B, L, D = (1, 256, 128)
        E, H, G, K = (64, 32, 64, 16)

        def _grouped_routing_scores(router_scores):
            T, En = router_scores.shape
            Tq = T // G
            budget = Tq * K
            order = jnp.argsort(-router_scores, axis=0)
            sorted_vals = jnp.take_along_axis(router_scores, order, axis=0)
            group_score = sorted_vals.reshape(Tq, G, En).sum(axis=1)
            _, top_flat = jax.lax.top_k(group_score.reshape(-1), budget)
            gmask = jnp.zeros((Tq * En,), bool).at[top_flat].set(True).reshape(Tq, En)
            mask_sorted = jnp.broadcast_to(gmask[:, None, :], (Tq, G, En)).reshape(T, En)
            mask = jnp.zeros((T, En), bool).at[order, jnp.arange(En)[None, :]].set(mask_sorted)
            fs = jnp.where(mask, router_scores, 0.0)
            return fs / (fs.sum(axis=-1, keepdims=True) + 1e-06)
        key = jax.random.key(seed)
        ks = jax.random.split(key, 6)
        s = lambda k, shape, scale: jax.random.normal(k, shape, jnp.float32) * scale
        return {'x': jax.random.normal(ks[0], (B, L, D), jnp.float32), 'Wr': s(ks[1], (D, E), D ** (-0.5)), 'br': jnp.zeros((E,), jnp.float32), 'Wup': s(ks[2], (E, D, H), D ** (-0.5)), 'bup': jnp.zeros((E, H), jnp.float32), 'Wgate': s(ks[3], (E, D, H), D ** (-0.5)), 'bgate': jnp.zeros((E, H), jnp.float32), 'Wdown': s(ks[4], (E, H, D), H ** (-0.5)), 'bdown': jnp.zeros((E, D), jnp.float32)}
    _L2_ffn_all = _L2_ffn_setup()
    _L2_ffn_in = {k: v for k, v in _L2_ffn_all.items() if k in ('Wr', 'br', 'Wup', 'bup', 'Wgate', 'bgate', 'Wdown', 'bdown')}
    del _L2_ffn_all

    def _L3_xattn_setup():
        import jax, jax.numpy as jnp
        import numpy as np
        DIM = 128
        HEADS = 16
        HEAD_DIM = DIM // HEADS
        SCALE = HEAD_DIM ** (-0.5)
        key = jax.random.key(seed)
        ks = jax.random.split(key, 13)
        B, Nq, Nk = (4, 256, 256)
        s = DIM ** (-0.5)
        return {'query': jax.random.normal(ks[0], (B, Nq, DIM), jnp.float32), 'key': jax.random.normal(ks[1], (B, Nk, DIM), jnp.float32), 'value': jax.random.normal(ks[2], (B, Nk, DIM), jnp.float32), 'qpos': jax.random.randint(ks[3], (B, Nq), 0, Nq), 'kpos': jax.random.randint(ks[4], (B, Nk), 0, Nk), 'Wq': jax.random.normal(ks[5], (DIM, DIM), jnp.float32) * s, 'bq': jnp.zeros((DIM,), jnp.float32), 'Wk': jax.random.normal(ks[6], (DIM, DIM), jnp.float32) * s, 'bk': jnp.zeros((DIM,), jnp.float32), 'Wv': jax.random.normal(ks[7], (DIM, DIM), jnp.float32) * s, 'bv': jnp.zeros((DIM,), jnp.float32), 'Wo': jax.random.normal(ks[8], (DIM, DIM), jnp.float32) * s, 'bo': jnp.zeros((DIM,), jnp.float32)}
    _L3_xattn_all = _L3_xattn_setup()
    _L3_xattn_in = {k: v for k, v in _L3_xattn_all.items() if k in ('Wq', 'bq', 'Wk', 'bk', 'Wv', 'bv', 'Wo', 'bo')}
    del _L3_xattn_all

    def _L3_ffn_setup():
        import jax, jax.numpy as jnp
        import numpy as np
        B, S, H, I = (2, 256, 128, 64)
        E, K, G, TG = (64, 8, 8, 4)
        SCALE = 2.5
        CAP = 128
        key = jax.random.key(seed)
        ks = jax.random.split(key, 6)
        hidden_states = jax.random.normal(ks[0], (B, S, H), jnp.float32)
        gate_w = jax.random.normal(ks[1], (E, H), jnp.float32) * 0.02
        gate_bias = jax.random.normal(ks[2], (E,), jnp.float32) * 0.02
        w_gate = jax.random.normal(ks[3], (E, H, I), jnp.float32) * (1.0 / np.sqrt(H))
        w_up = jax.random.normal(ks[4], (E, H, I), jnp.float32) * (1.0 / np.sqrt(H))
        w_down = jax.random.normal(ks[5], (E, I, H), jnp.float32) * (1.0 / np.sqrt(I))
        return {'hidden_states': hidden_states, 'gate_w': gate_w, 'gate_bias': gate_bias, 'w_gate': w_gate, 'w_up': w_up, 'w_down': w_down}
    _L3_ffn_all = _L3_ffn_setup()
    _L3_ffn_in = {k: v for k, v in _L3_ffn_all.items() if k in ('gate_w', 'gate_bias', 'w_gate', 'w_up', 'w_down')}
    del _L3_ffn_all
    return {'x': x, 'ctx_1024': ctx_1024, 'itok_BxS2_0_2047': itok_BxS2_0_2047, 'mask_Bx16xSxS2_ff0': mask_Bx16xSxS2_ff0, 'mask_1x1xSxS2_ik1': mask_1x1xSxS2_ik1, 'L0_xattn_W_q': _L0_xattn_in['W_q'], 'L0_xattn_W_k': _L0_xattn_in['W_k'], 'L0_xattn_W_v': _L0_xattn_in['W_v'], 'L0_xattn_W_o': _L0_xattn_in['W_o'], 'L0_xattn_lambda_q1': _L0_xattn_in['lambda_q1'], 'L0_xattn_lambda_k1': _L0_xattn_in['lambda_k1'], 'L0_xattn_lambda_q2': _L0_xattn_in['lambda_q2'], 'L0_xattn_lambda_k2': _L0_xattn_in['lambda_k2'], 'L0_xattn_rms_scale': _L0_xattn_in['rms_scale'], 'L0_ffn_ln1_g': _L0_ffn_in['ln1_g'], 'L0_ffn_ln1_b': _L0_ffn_in['ln1_b'], 'L0_ffn_w1': _L0_ffn_in['w1'], 'L0_ffn_b1': _L0_ffn_in['b1'], 'L0_ffn_ln2_g': _L0_ffn_in['ln2_g'], 'L0_ffn_ln2_b': _L0_ffn_in['ln2_b'], 'L0_ffn_w2': _L0_ffn_in['w2'], 'L0_ffn_b2': _L0_ffn_in['b2'], 'L1_xattn_wq': _L1_xattn_in['wq'], 'L1_xattn_bq': _L1_xattn_in['bq'], 'L1_xattn_wk': _L1_xattn_in['wk'], 'L1_xattn_bk': _L1_xattn_in['bk'], 'L1_xattn_wv': _L1_xattn_in['wv'], 'L1_xattn_bv': _L1_xattn_in['bv'], 'L1_xattn_wo': _L1_xattn_in['wo'], 'L1_xattn_bo': _L1_xattn_in['bo'], 'L1_ffn_w_router': _L1_ffn_in['w_router'], 'L1_ffn_w_up': _L1_ffn_in['w_up'], 'L1_ffn_w_gate': _L1_ffn_in['w_gate'], 'L1_ffn_w_down': _L1_ffn_in['w_down'], 'L1_ffn_ws_up': _L1_ffn_in['ws_up'], 'L1_ffn_ws_gate': _L1_ffn_in['ws_gate'], 'L1_ffn_ws_down': _L1_ffn_in['ws_down'], 'L2_xattn_Wq_w': _L2_xattn_in['Wq_w'], 'L2_xattn_Wq_b': _L2_xattn_in['Wq_b'], 'L2_xattn_Wk_w': _L2_xattn_in['Wk_w'], 'L2_xattn_Wk_b': _L2_xattn_in['Wk_b'], 'L2_xattn_Wv_w': _L2_xattn_in['Wv_w'], 'L2_xattn_Wv_b': _L2_xattn_in['Wv_b'], 'L2_xattn_Wo_w': _L2_xattn_in['Wo_w'], 'L2_xattn_Wo_b': _L2_xattn_in['Wo_b'], 'L2_ffn_Wr': _L2_ffn_in['Wr'], 'L2_ffn_br': _L2_ffn_in['br'], 'L2_ffn_Wup': _L2_ffn_in['Wup'], 'L2_ffn_bup': _L2_ffn_in['bup'], 'L2_ffn_Wgate': _L2_ffn_in['Wgate'], 'L2_ffn_bgate': _L2_ffn_in['bgate'], 'L2_ffn_Wdown': _L2_ffn_in['Wdown'], 'L2_ffn_bdown': _L2_ffn_in['bdown'], 'L3_xattn_Wq': _L3_xattn_in['Wq'], 'L3_xattn_bq': _L3_xattn_in['bq'], 'L3_xattn_Wk': _L3_xattn_in['Wk'], 'L3_xattn_bk': _L3_xattn_in['bk'], 'L3_xattn_Wv': _L3_xattn_in['Wv'], 'L3_xattn_bv': _L3_xattn_in['bv'], 'L3_xattn_Wo': _L3_xattn_in['Wo'], 'L3_xattn_bo': _L3_xattn_in['bo'], 'L3_ffn_gate_w': _L3_ffn_in['gate_w'], 'L3_ffn_gate_bias': _L3_ffn_in['gate_bias'], 'L3_ffn_w_gate': _L3_ffn_in['w_gate'], 'L3_ffn_w_up': _L3_ffn_in['w_up'], 'L3_ffn_w_down': _L3_ffn_in['w_down']}

def reference(x, ctx_1024, itok_BxS2_0_2047, mask_Bx16xSxS2_ff0, mask_1x1xSxS2_ik1, L0_xattn_W_q, L0_xattn_W_k, L0_xattn_W_v, L0_xattn_W_o, L0_xattn_lambda_q1, L0_xattn_lambda_k1, L0_xattn_lambda_q2, L0_xattn_lambda_k2, L0_xattn_rms_scale, L0_ffn_ln1_g, L0_ffn_ln1_b, L0_ffn_w1, L0_ffn_b1, L0_ffn_ln2_g, L0_ffn_ln2_b, L0_ffn_w2, L0_ffn_b2, L1_xattn_wq, L1_xattn_bq, L1_xattn_wk, L1_xattn_bk, L1_xattn_wv, L1_xattn_bv, L1_xattn_wo, L1_xattn_bo, L1_ffn_w_router, L1_ffn_w_up, L1_ffn_w_gate, L1_ffn_w_down, L1_ffn_ws_up, L1_ffn_ws_gate, L1_ffn_ws_down, L2_xattn_Wq_w, L2_xattn_Wq_b, L2_xattn_Wk_w, L2_xattn_Wk_b, L2_xattn_Wv_w, L2_xattn_Wv_b, L2_xattn_Wo_w, L2_xattn_Wo_b, L2_ffn_Wr, L2_ffn_br, L2_ffn_Wup, L2_ffn_bup, L2_ffn_Wgate, L2_ffn_bgate, L2_ffn_Wdown, L2_ffn_bdown, L3_xattn_Wq, L3_xattn_bq, L3_xattn_Wk, L3_xattn_bk, L3_xattn_Wv, L3_xattn_bv, L3_xattn_Wo, L3_xattn_bo, L3_ffn_gate_w, L3_ffn_gate_bias, L3_ffn_w_gate, L3_ffn_w_up, L3_ffn_w_down):
    import jax
    import jax.numpy as jnp

    def _L0_xattn_ref(query, key, value, attn_mask, W_q, W_k, W_v, W_o, lambda_q1, lambda_k1, lambda_q2, lambda_k2, rms_scale):
        import jax, jax.numpy as jnp
        import numpy as np
        B, S, D = (2, 256, 128)
        H = 16
        DH = D // H
        LAMBDA_INIT = 0.8
        EPS = 1e-05
        SCALE = 1.0 / np.sqrt(DH)
        b, s, _ = value.shape
        q = (query @ W_q).reshape(b, s, H, 2 * DH).transpose(0, 2, 1, 3)
        k = (key @ W_k).reshape(b, s, H, 2 * DH).transpose(0, 2, 1, 3)
        v = (value @ W_v).reshape(b, s, H, DH).transpose(0, 2, 1, 3)
        q1, q2 = (q[..., :DH], q[..., DH:])
        k1, k2 = (k[..., :DH], k[..., DH:])
        lam = jnp.exp(jnp.sum(lambda_q1 * lambda_k1, -1)) - jnp.exp(jnp.sum(lambda_q2 * lambda_k2, -1)) + LAMBDA_INIT
        lam = lam[None, :, None, None]
        s1 = jnp.einsum('bhqd,bhkd->bhqk', q1, k1) * SCALE + attn_mask
        s2 = jnp.einsum('bhqd,bhkd->bhqk', q2, k2) * SCALE + attn_mask
        attn = jax.nn.softmax(s1, axis=-1) - lam * jax.nn.softmax(s2, axis=-1)
        out = jnp.einsum('bhqk,bhkd->bhqd', attn, v)
        rms = jnp.sqrt(jnp.mean(out * out, axis=-1, keepdims=True) + EPS)
        out = out / rms * rms_scale
        out = out * (1.0 - LAMBDA_INIT)
        out = out.transpose(0, 2, 1, 3).reshape(b, s, H * DH)
        return out @ W_o

    def _L0_ffn_ref(x, ln1_g, ln1_b, w1, b1, ln2_g, ln2_b, w2, b2):
        import jax, jax.numpy as jnp
        import numpy as np
        LN_EPS = 1e-05

        def layernorm(x, g, b):
            mu = jnp.mean(x, axis=-1, keepdims=True)
            var = jnp.mean((x - mu) ** 2, axis=-1, keepdims=True)
            return (x - mu) * jax.lax.rsqrt(var + LN_EPS) * g + b

        def act_quant_fake(x):
            scale = 127.0 / jnp.clip(jnp.max(jnp.abs(x), axis=-1, keepdims=True), 1e-05)
            return jnp.clip(jnp.round(x * scale), -128.0, 127.0) / scale

        def weight_quant_fake(w):
            scale = 1.0 / jnp.clip(jnp.mean(jnp.abs(w)), 1e-05)
            return jnp.clip(jnp.round(w * scale), -1.0, 1.0) / scale

        def bitlinear(x, w, b):
            dqx = act_quant_fake(x)
            dqw = weight_quant_fake(w)
            return jnp.einsum('btd,hd->bth', dqx, dqw) + b
        h = layernorm(x, ln1_g, ln1_b)
        h = bitlinear(h, w1, b1)
        h = jax.nn.gelu(h, approximate=False)
        h = layernorm(h, ln2_g, ln2_b)
        h = bitlinear(h, w2, b2)
        return h

    def _L1_xattn_ref(q, k, v, mask, wq, bq, wk, bk, wv, bv, wo, bo):
        import jax, jax.numpy as jnp
        import numpy as np
        B, S, H, NH = (2, 256, 128, 16)
        HD = H // NH
        NEG = -1000000.0

        def _split(t):
            b, s, h = t.shape
            return t.reshape(b, s, NH, h // NH).transpose(0, 2, 1, 3)
        qh = _split(q @ wq + bq)
        kh = _split(k @ wk + bk)
        vh = _split(v @ wv + bv)
        scale = 1.0 / jnp.sqrt(jnp.asarray(HD, qh.dtype))
        score = jnp.einsum('bhqd,bhkd->bhqk', qh, kh) * scale
        score = jnp.where(mask == 0, jnp.asarray(NEG, score.dtype), score)
        attn = jax.nn.softmax(score, axis=-1)
        out = jnp.einsum('bhqk,bhkd->bhqd', attn, vh)
        out = out.transpose(0, 2, 1, 3).reshape(q.shape[0], q.shape[1], -1)
        return out @ wo + bo

    def _L1_ffn_ref(x, w_router, w_up, w_gate, w_down, ws_up, ws_gate, ws_down):
        import jax, jax.numpy as jnp
        import numpy as np
        DIM = 128
        HID = 512
        E = 8
        TOPK = 2
        ALPHA = 2.0
        B, T = (1, 256)
        DOWN_SCALE = 0.01
        logits = x @ w_router
        probs = jax.nn.softmax(logits.astype(jnp.float32), axis=-1).astype(logits.dtype)
        topk_vals, topk_idx = jax.lax.top_k(probs, TOPK)
        up = jnp.einsum('btd,edh->ebth', x, w_up)
        gate = jax.nn.silu(jnp.einsum('btd,edh->ebth', x, w_gate))
        exp_out = jnp.einsum('ebth,ehd->ebtd', up * gate, w_down)
        out = jnp.zeros_like(x)
        eids = jnp.arange(E - 1)
        for i in range(TOPK - 1):
            idx_i = topk_idx[..., i]
            sel = (idx_i[None, :, :] == eids[:, None, None]).astype(x.dtype)
            gathered = jnp.einsum('ebt,ebtd->btd', sel, exp_out)
            out = out + ALPHA * topk_vals[..., i:i + 1] * gathered
        shared = x @ ws_up * jax.nn.silu(x @ ws_gate) @ ws_down
        return out + shared

    def _L2_xattn_ref(query, value, key, Wq_w, Wq_b, Wk_w, Wk_b, Wv_w, Wv_b, Wo_w, Wo_b):
        import jax, jax.numpy as jnp
        import numpy as np
        D_MODEL = 128
        HEAD = 16
        B, S, D = query.shape
        H = HEAD
        kd = D // H
        Q = query @ Wq_w.T + Wq_b
        K = key @ Wk_w.T + Wk_b
        V = value @ Wv_w.T + Wv_b
        Q = Q.reshape(B, S, H, kd).transpose(0, 2, 1, 3)
        K = K.reshape(B, S, H, kd).transpose(0, 2, 1, 3)
        V = V.reshape(B, S, H, kd).transpose(0, 2, 1, 3)
        scale = 1.0 / jnp.sqrt(jnp.asarray(kd, query.dtype))
        score = jnp.einsum('bhqd,bhkd->bhqk', Q, K) * scale
        attn = jax.nn.softmax(score, axis=-1)
        x = jnp.einsum('bhqk,bhkd->bhqd', attn, V)
        x = x.transpose(0, 2, 1, 3).reshape(B, S, D)
        return x @ Wo_w.T + Wo_b

    def _L2_ffn_ref(x, Wr, br, Wup, bup, Wgate, bgate, Wdown, bdown):
        import jax, jax.numpy as jnp
        import numpy as np
        B, L, D = (1, 256, 128)
        E, H, G, K = (64, 32, 64, 16)

        def _grouped_routing_scores(router_scores):
            T, En = router_scores.shape
            Tq = T // G
            budget = Tq * K
            order = jnp.argsort(-router_scores, axis=0)
            sorted_vals = jnp.take_along_axis(router_scores, order, axis=0)
            group_score = sorted_vals.reshape(Tq, G, En).sum(axis=1)
            _, top_flat = jax.lax.top_k(group_score.reshape(-1), budget)
            gmask = jnp.zeros((Tq * En,), bool).at[top_flat].set(True).reshape(Tq, En)
            mask_sorted = jnp.broadcast_to(gmask[:, None, :], (Tq, G, En)).reshape(T, En)
            mask = jnp.zeros((T, En), bool).at[order, jnp.arange(En)[None, :]].set(mask_sorted)
            fs = jnp.where(mask, router_scores, 0.0)
            return fs / (fs.sum(axis=-1, keepdims=True) + 1e-06)
        Bx, Lx, Dx = x.shape
        xt = x.reshape(-1, Dx)
        router_scores = jax.nn.softmax(xt @ Wr + br, axis=-1)
        fs = _grouped_routing_scores(router_scores)
        up = jnp.einsum('td,edh->teh', xt, Wup) + bup
        gate = jnp.einsum('td,edh->teh', xt, Wgate) + bgate
        h = jax.nn.silu(up) * gate * fs[:, :, None]
        out = jnp.einsum('teh,ehd->td', h, Wdown) + fs @ bdown
        return out.reshape(Bx, Lx, Dx)

    def _L3_xattn_ref(query, key, value, qpos, kpos, Wq, bq, Wk, bk, Wv, bv, Wo, bo):
        import jax, jax.numpy as jnp
        import numpy as np
        DIM = 128
        HEADS = 16
        HEAD_DIM = DIM // HEADS
        SCALE = HEAD_DIM ** (-0.5)
        B, Nq, C = query.shape

        def split_heads(x):
            return x.reshape(x.shape[0], x.shape[1], HEADS, HEAD_DIM).transpose(0, 2, 1, 3)
        q = split_heads(query @ Wq + bq)
        k = split_heads(key @ Wk + bk)
        v = split_heads(value @ Wv + bv)
        attn = jnp.einsum('bhqd,bhkd->bhqk', q, k) * SCALE
        attn = jax.nn.softmax(attn, axis=-1)
        x = jnp.einsum('bhqk,bhkd->bhqd', attn, v)
        x = x.transpose(0, 2, 1, 3).reshape(B, Nq, C)
        return x @ Wo + bo

    def _L3_ffn_ref(hidden_states, gate_w, gate_bias, w_gate, w_up, w_down):
        import jax, jax.numpy as jnp
        import numpy as np
        B, S, H, I = (2, 256, 128, 64)
        E, K, G, TG = (64, 8, 8, 4)
        SCALE = 2.5
        CAP = 128
        b, s, h = hidden_states.shape
        x = hidden_states.reshape(-1, h)
        n = x.shape[0]
        logits = x.astype(jnp.float32) @ gate_w.astype(jnp.float32).T
        scores = jax.nn.sigmoid(logits)
        sfc = scores + gate_bias[None, :]
        group_scores = jax.lax.top_k(sfc.reshape(n, G, E // G), 2)[0].sum(-1)
        gidx = jax.lax.top_k(group_scores, TG)[1]
        gmask = jnp.zeros((n, G), bool).at[jnp.arange(n)[:, None], gidx].set(True)
        smask = jnp.repeat(gmask, E // G, axis=1)
        tmp = jnp.where(smask, sfc, -jnp.inf)
        topk_idx = jax.lax.top_k(tmp, K)[1]
        topk_w = jnp.take_along_axis(scores, topk_idx, axis=1)
        topk_w = topk_w / (topk_w.sum(-1, keepdims=True) + 1e-20)
        topk_w = topk_w * SCALE
        e = topk_idx.reshape(-1)
        token = jnp.repeat(jnp.arange(n), K)
        oh = jax.nn.one_hot(e, E, dtype=jnp.int32)
        pos = jnp.take_along_axis(jnp.cumsum(oh, 0) - 1, e[:, None], 1)[:, 0]
        valid = pos < CAP
        pos_c = jnp.where(valid, pos, CAP)
        buf = jnp.zeros((E, CAP + 1, h), x.dtype).at[e, pos_c].set(x[token])[:, :CAP]
        g = jnp.einsum('ech,ehi->eci', buf, w_gate)
        u = jnp.einsum('ech,ehi->eci', buf, w_up)
        y = jnp.einsum('eci,eih->ech', jax.nn.silu(g) * u, w_down)
        y_slots = y[e, jnp.minimum(pos, CAP - 1)]
        w_slot = topk_w.reshape(-1) * valid.astype(topk_w.dtype)
        out = jnp.zeros((n, h), jnp.float32).at[token].add(y_slots * w_slot[:, None])
        return out.reshape(b, s, h)
    x = x + _L0_xattn_ref(_layernorm(x, axis=-1), ctx_1024, ctx_1024, mask_Bx16xSxS2_ff0, L0_xattn_W_q, L0_xattn_W_k, L0_xattn_W_v, L0_xattn_W_o, L0_xattn_lambda_q1, L0_xattn_lambda_k1, L0_xattn_lambda_q2, L0_xattn_lambda_k2, L0_xattn_rms_scale)
    x = x + _L0_ffn_ref(_layernorm(x, axis=-1), L0_ffn_ln1_g, L0_ffn_ln1_b, L0_ffn_w1, L0_ffn_b1, L0_ffn_ln2_g, L0_ffn_ln2_b, L0_ffn_w2, L0_ffn_b2)
    x = x + _L1_xattn_ref(_layernorm(x, axis=-1), ctx_1024, ctx_1024, mask_1x1xSxS2_ik1, L1_xattn_wq, L1_xattn_bq, L1_xattn_wk, L1_xattn_bk, L1_xattn_wv, L1_xattn_bv, L1_xattn_wo, L1_xattn_bo)
    x = x + _L1_ffn_ref(_layernorm(x, axis=-1), L1_ffn_w_router, L1_ffn_w_up, L1_ffn_w_gate, L1_ffn_w_down, L1_ffn_ws_up, L1_ffn_ws_gate, L1_ffn_ws_down)
    x = x + _L2_xattn_ref(_layernorm(x, axis=-1), ctx_1024, ctx_1024, L2_xattn_Wq_w, L2_xattn_Wq_b, L2_xattn_Wk_w, L2_xattn_Wk_b, L2_xattn_Wv_w, L2_xattn_Wv_b, L2_xattn_Wo_w, L2_xattn_Wo_b)
    x = x + _L2_ffn_ref(_layernorm(x, axis=-1), L2_ffn_Wr, L2_ffn_br, L2_ffn_Wup, L2_ffn_bup, L2_ffn_Wgate, L2_ffn_bgate, L2_ffn_Wdown, L2_ffn_bdown)
    x = x + _L3_xattn_ref(_layernorm(x, axis=-1), ctx_1024, ctx_1024, itok_BxS2_0_2047, itok_BxS2_0_2047, L3_xattn_Wq, L3_xattn_bq, L3_xattn_Wk, L3_xattn_bk, L3_xattn_Wv, L3_xattn_bv, L3_xattn_Wo, L3_xattn_bo)
    x = x + _L3_ffn_ref(_layernorm(x, axis=-1), L3_ffn_gate_w, L3_ffn_gate_bias, L3_ffn_w_gate, L3_ffn_w_up, L3_ffn_w_down)
    return x

_drawn_inputs = setup_inputs


def setup_inputs(seed=0):
    import zlib

    import numpy as np

    out = dict(_drawn_inputs(seed))
    spreads = {'L0_xattn_rms_scale': (1.0, 0.2),
     'L0_ffn_ln1_g': (1.0, 0.2),
     'L0_ffn_ln1_b': (0.0, 0.1),
     'L0_ffn_ln2_g': (1.0, 0.2),
     'L0_ffn_ln2_b': (0.0, 0.1),
     'L1_xattn_bq': (0.0, 0.8),
     'L1_xattn_bk': (0.0, 0.8),
     'L1_xattn_bv': (0.0, 0.1),
     'L1_xattn_bo': (0.0, 0.1),
     'L2_xattn_Wq_b': (0.0, 0.1),
     'L2_xattn_Wk_b': (0.0, 0.8),
     'L2_xattn_Wv_b': (0.0, 0.1),
     'L2_xattn_Wo_b': (0.0, 0.1),
     'L2_ffn_br': (0.0, 0.1),
     'L2_ffn_bup': (0.0, 0.1),
     'L2_ffn_bgate': (0.0, 0.1),
     'L2_ffn_bdown': (0.0, 0.1),
     'L3_xattn_bq': (0.0, 0.1),
     'L3_xattn_bk': (0.0, 0.8),
     'L3_xattn_bv': (0.0, 0.1),
     'L3_xattn_bo': (0.0, 0.1)}
    factors = {'L0_xattn_lambda_k1': 2.692, 'L1_xattn_wq': 5.363, 'L1_xattn_wk': 7.582}
    for name, (base, spread) in spreads.items():
        noise = np.random.default_rng([zlib.crc32(name.encode()), seed]).standard_normal(out[name].shape)
        drawn = base * np.exp(spread * noise) if base else spread * noise
        out[name] = jnp.asarray(drawn.astype(out[name].dtype))
    for name, factor in factors.items():
        out[name] = (out[name] * factor).astype(out[name].dtype)
    return out
```

```python
from contextlib import ExitStack

import concourse.bass as bass
from concourse import mybir

ALU = mybir.AluOpType
ACT = mybir.ActivationFunctionType
AX = mybir.AxisListType
F32 = mybir.dt.float32
BF16 = mybir.dt.bfloat16
I32 = mybir.dt.int32
U32 = mybir.dt.uint32

P = 128
BATCH, SEQ, D = 64, 64, 128
TOK = BATCH * SEQ
NT = TOK // P
HEADS, DH = 16, 8
EPS = 1e-5
QK_SCALE = DH ** -0.5
MAGIC = 1.5 * 2.0 ** 23


class Memory:

    def __init__(self, nc, stack):
        self.nc, self.stack, self.part, self.sems = nc, stack, "", []
        sb = self.kept
        self.X = sb("X", [P, NT, D], F32)
        self.ctxT = sb("ctxT", [P, TOK], F32)
        self.xT = sb("xT", [P, TOK], F32)
        self.ident = sb("ident", [P, P], F32)
        self.identb = sb("identb", [P, P], BF16)
        self.fold = sb("fold", [P, SEQ], F32)
        self.head_mask = sb("head_mask", [P, 4], F32)
        self.half_mask = sb("half_mask", [P, 2], F32)
        self.mean = sb("mean", [P, NT], F32)
        self.rstd = sb("rstd", [P, NT], F32)

    def kept(self, name, shape, dt):
        return self.stack.enter_context(self.nc.sbuf_tensor("kept_" + name, shape, dt))

    def sem(self, name):
        self.sems.append(self.nc.alloc_semaphore(name=f"{self.part}_{name}"))
        return self.sems[-1]

    def free_sems(self):
        self.nc.clear_and_free_semaphores(self.sems)
        self.nc.all_engine_barrier()
        self.sems = []


class Chain:

    def __init__(self, eng, sem, base=0):
        self.eng, self.sem, self.base, self.n = eng, sem, base, 0

    def link(self, instruction):
        self.n += 1
        instruction.then_inc(self.sem, 1)
        self.eng.wait_ge(self.sem, self.base + self.n)


def wait_past(eng, sem, value):
    if not isinstance(value, int) or value > 0:
        eng.wait_ge(sem, value)


def in_pairs(eng, first, end, step):
    assert first % 2 == 0 and end % 2 == 0
    with eng.Fori(0, (end - first) // 2) as k:
        for u in range(2):
            step(2 * k + (first + u), u, k + first // 2)


def peeled(eng, end, step):
    step(0, 0, 0)
    step(1, 1, 0)
    in_pairs(eng, 2, end, step)


def pipelined(eng, units, stages, period=2):
    stages = [(lead, stage, *(more or (0,))) for lead, stage, *more in stages]
    leads = [lead for lead, _, _ in stages]
    first = -(-(period - min(leads)) // period) * period
    end = (units - max(leads)) // period * period
    assert first < end

    def plain(start, stop):
        for s in range(start, stop):
            for lead, stage, beyond in stages:
                if 0 <= s + lead < units + beyond:
                    stage(s + lead, (s + lead) % period, (s + lead) // period)

    plain(-max(leads), first)
    with eng.Fori(0, (end - first) // period) as k:
        for s in range(first, first + period):
            for lead, stage, _ in stages:
                stage(period * k + (s + lead), (s + lead) % period, k + (s + lead) // period)
    plain(end, units - min(leads))


def load_all(nc, m, t):
    m.part = "load"
    loaded, built = m.sem("loaded"), m.sem("built")
    with nc.Block() as block:
        @block.sync
        def _(sp):
            x = t["x"].rearrange("(b e) s d -> (e s) b d", e=P // SEQ)
            sp.dma_start(m.X[:, :, :], x).then_inc(loaded, 16)
            sp.dma_start(m.head_mask[:, :], t["c_head_mask"]).then_inc(loaded, 16)
            sp.dma_start(m.fold[:, :], t["c_fold"]).then_inc(loaded, 16)
            sp.wait_ge(loaded, 80)

        @block.scalar
        def _(act):
            act.dma_start(m.ctxT[:, :], t["ctxT"]).then_inc(loaded, 16)
            act.dma_start(m.ident[:, :], t["c_ident"]).then_inc(loaded, 16)

        @block.vector
        def _(dve):
            for h in range(2):
                dve.memset(m.half_mask[64 * h:64 * h + 64, h:h + 1], 1.0).then_inc(built, 1)
                dve.memset(m.half_mask[64 * h:64 * h + 64, 1 - h:2 - h], 0.0).then_inc(built, 1)
            dve.wait_ge(loaded, 80)
            dve.tensor_copy(m.identb[:, :], m.ident[:, :]).then_inc(built, 1)
            dve.wait_ge(built, 5)


def store_all(nc, m, t):
    m.part = "store"
    stored = m.sem("stored")
    with nc.Block() as block:
        @block.sync
        def _(sp):
            out = t["out"].rearrange("(b e) s d -> (e s) b d", e=P // SEQ)
            sp.dma_start(out, m.X[:, :, :]).then_inc(stored, 16)
            sp.wait_ge(stored, 16)


def layer_norm(nc, m, part, to_xT=True, router=None, rows=None):
    m.part = part
    with ExitStack() as own:
        stats = own.enter_context(nc.sbuf_tensor(part + "stats", [P, NT, 6], F32))
        a = own.enter_context(nc.sbuf_tensor(part + "a", [P, NT], F32))
        diff = own.enter_context(nc.sbuf_tensor(part + "diff", [P, NT], F32))
        var = own.enter_context(nc.sbuf_tensor(part + "var", [P, NT], F32))
        xh = own.enter_context(nc.sbuf_tensor(part + "xh", [P, 2, 4, D], F32))
        psT = own.enter_context(nc.psum_tensor(part + "psT", [P, 2, 512], F32))
        if router:
            wr, logits = router
            E = logits.shape[2]
            Wr = own.enter_context(nc.sbuf_tensor(part + "Wr", [P, E], F32))
            hatT = own.enter_context(nc.sbuf_tensor(part + "hatT", [P, 2, 512], F32))
            psL = own.enter_context(nc.psum_tensor(part + "psL", [P, 2, 512], F32))
            wr_loaded, routed, hatT_copied = m.sem("wr_loaded"), m.sem("routed"), m.sem("hatT_copied")
        rows_out = [m.sem(f"rows_out{u}") for u in range(2)] if rows is not None else None
        chained, var_ready, std_ready = m.sem("chained"), m.sem("var_ready"), m.sem("std_ready")
        hat_ready, hatT_ready, hatT_taken = m.sem("hat_ready"), m.sem("hatT_ready"), m.sem("hatT_taken")
        groups = NT // 4

        with nc.Block() as block:
            @block.sync
            def _(sp):
                if router:
                    sp.dma_start(Wr[:, :], wr).then_inc(wr_loaded, 16)
                if rows is not None:
                    def write(g, u, n):
                        sp.wait_ge(hat_ready, g + 1)
                        sp.dma_start(rows[bass.ds(4 * g, 4), :, :].rearrange("j p d -> p j d"), xh[:, u, :, :]).then_inc(rows_out[u], 16)
                    peeled(sp, groups, write)
                    for u in range(2):
                        sp.wait_ge(rows_out[u], 16 * groups // 2)

            @block.vector
            def _(dve):
                chain = Chain(dve, chained)
                with dve.Fori(0, groups) as g:
                    for j in range(4):
                        last = dve.bn_stats(stats[:, 4 * g + j, :], m.X[:, 4 * g + j, :])
                    last.then_inc(chained, 1)
                chain.n = groups
                dve.wait_ge(chained, groups)
                dve.tensor_tensor(a[:, :], stats[:, :, 1], stats[:, :, 4], ALU.add)
                dve.tensor_tensor(diff[:, :], stats[:, :, 1], stats[:, :, 4], ALU.subtract)
                chain.link(dve.tensor_tensor(var[:, :], stats[:, :, 2], stats[:, :, 5], ALU.add))
                dve.tensor_scalar(m.mean[:, :], a[:, :], 0.5, None, ALU.mult)
                dve.tensor_scalar(var[:, :], var[:, :], 1.0 / D, EPS, ALU.mult, ALU.add)
                chain.link(dve.scalar_tensor_tensor(diff[:, :], diff[:, :], 0.25, diff[:, :], ALU.mult, ALU.mult))
                dve.tensor_tensor(var[:, :], var[:, :], diff[:, :], ALU.add).then_inc(var_ready, 1)
                dve.wait_ge(std_ready, 1)
                chain.link(dve.reciprocal(m.rstd[:, :], a[:, :]))
                if not to_xT:
                    return

                def normalise(g, u, n):
                    wait_past(dve, hatT_ready, g - 1)
                    if rows is not None:
                        wait_past(dve, rows_out[u], 16 * n)
                    for j in range(4):
                        i = 4 * g + j
                        last = dve.tensor_scalar(xh[:, u, j, :], m.X[:, i, :], m.mean[:, bass.ds(i, 1)],
                                                 m.rstd[:, bass.ds(i, 1)], ALU.subtract, ALU.mult)
                    last.then_inc(hat_ready, 1)

                dve.wait_ge(chained, chain.n)
                if not router:
                    peeled(dve, groups, normalise)
                    return

                def take_logits(g, u, n):
                    dve.wait_ge(hatT_taken, g + 1)
                    dve.tensor_scalar(m.xT[:, bass.ds(512 * g, 512)], hatT[:, u, :], 1.0, None, ALU.mult).then_inc(hatT_copied, 1)
                    dve.wait_ge(routed, g + 1)
                    out = logits[:, bass.ds(4 * g, 4), :].rearrange("p j e -> p (j e)")
                    dve.tensor_scalar(out, psL[:, u, 0:4 * E], 1.0, None, ALU.mult).then_inc(hatT_copied, 1)

                pipelined(dve, groups, [(1, normalise), (0, take_logits)])

            @block.scalar
            def _(act):
                act.wait_ge(var_ready, 1)
                act.activation(a[:, :], var[:, :], ACT.Sqrt).then_inc(std_ready, 1)
                if not to_xT:
                    return

                def take(g, u, n):
                    act.wait_ge(hatT_ready, g + 1)
                    if router:
                        wait_past(act, hatT_copied, 2 * (g - 1))
                        act.activation(hatT[:, u, :], psT[:, u, :], ACT.Copy).then_inc(hatT_taken, 1)
                        return
                    act.activation(m.xT[:, bass.ds(512 * g, 512)], psT[:, u, :], ACT.Copy).then_inc(hatT_taken, 1)

                peeled(act, groups, take)

            @block.tensor
            def _(pe):
                if not to_xT:
                    return

                def turn(g, u, n):
                    pe.wait_ge(hat_ready, g + 1)
                    wait_past(pe, hatT_taken, g - 1)
                    for j in range(4):
                        last = pe.transpose(psT[:, u, j * D:(j + 1) * D], xh[:, u, j, :], m.ident[:, :])
                    last.then_inc(hatT_ready, 1)

                if not router:
                    peeled(pe, groups, turn)
                    return

                def route(g, u, n):
                    pe.wait_ge(hatT_taken, g + 1)
                    wait_past(pe, hatT_copied, 2 * (g - 1))
                    for j in range(4):
                        last = pe.matmul(psL[:, u, j * E:j * E + E], hatT[:, u, j * D:j * D + D], Wr[:, :], start=True, stop=True)
                    last.then_inc(routed, 1)

                pe.wait_ge(wr_loaded, 16)
                pipelined(pe, groups, [(1, turn), (0, route)])
HV = 16
LAMBDA_INIT = 0.8
WIDTH = 64
REGIONS = 8


def attention(nc, m, part, wq, wk, wv, wo=None, bq=None, bk=None, bv=None, bo=None,
              keep_mask=None, add_mask=None, lams=None, Oall=None):
    m.part = part
    diff = lams is not None
    CH = 2 if diff else 1
    M = NT * CH
    VW = D // CH
    W = VW // (2 * REGIONS // 2)
    LS = 2 if diff else 1
    LP = LS + 1
    with ExitStack() as own:
        def sb(name, shape, dt=F32):
            return own.enter_context(nc.sbuf_tensor(f"{part}_{name}", shape, dt))

        def pb(name, shape, dt=F32):
            return own.enter_context(nc.psum_tensor(f"{part}_{name}", shape, dt))

        Wq, Wk, Wv = sb("Wq", [P, CH * P]), sb("Wk", [P, CH * P]), sb("Wv", [P, D])
        qmask = sb("qmask", [P, 2])
        cst = sb("cst", [P, 2, 2, 2, SEQ])
        QM = sb("QM", [P, 2, 2, 2, SEQ])
        KM = sb("KM", [P, 2, 2, 2, SEQ])
        RW = 2 * (W + 1)
        WIDE = max(RW, WIDTH)
        VZ = sb("VZ", [P, 2, REGIONS * RW + WIDE - RW])
        regions = lambda par: VZ[:, par, 0:REGIONS * RW].rearrange("p (r j w) -> p r j w", j=2, w=W + 1)
        E = sb("E", [P, 2, 2, 512])
        PT = sb("PT", [P, 2, REGIONS, P])
        mx, rs, spare = sb("mx", [P, HV]), sb("rs", [P, HV]), sb("spare", [P, 1])
        On = sb("On", [P, 2 * HV // 2, W])
        psS = pb("psS", [P, 4, 512])
        psT = pb("psT", [P, 2, 512])
        psP = pb("psP", [P, 512])
        psO = pb("psO", [P, 512])
        SUMS = (REGIONS - 1) * RW + WIDE
        O_ = psO[:, 0:REGIONS * RW].rearrange("p (r w) -> p r w", w=W + 1)
        OTP = slice(SUMS, SUMS + P) if not diff else slice(SUMS, SUMS + VW)
        if diff:
            lam, coef = sb("lam", [P, HEADS]), sb("coef", [P, CH, 2, HEADS // 2])
            lamv = sb("lamv", [P, 4, HEADS * DH])
            amask = sb("amask", [P, 4, 2, HEADS // 2, SEQ])
            Z = sb("Z", [P, 2, 2, 512])
            mx2 = sb("mx2", [P, 2, HV])
        else:
            Wo, OT = sb("Wo", [P, D]), sb("OT", [P, P])
            bqc, bkc, bvc = sb("bq", [P, 1]), sb("bk", [P, 1]), sb("bv", [P, 1])
            bvm, bias = sb("bvm", [P, P]), sb("bias", [P, D])
            inv = sb("inv", [P, HV, 2])
        if keep_mask is not None:
            keep, drop, neg, carrier = sb("keep", [P, SEQ], I32), sb("drop", [P, SEQ], I32), sb("neg", [P, 1]), sb("carrier", [P, 2])

        loaded, chained, prepared = m.sem("loaded"), m.sem("chained"), m.sem("prepared")
        staged, carried, qk_done, qk_taken, v_done, v_taken = (m.sem(n) for n in (
            "staged", "carried", "qk_done", "qk_taken", "v_done", "v_taken"))
        scored, s_taken, shifted, exped, turned, pt_ready = (m.sem(n) for n in (
            "scored", "s_taken", "shifted", "exped", "turned", "pt_ready"))
        maxed, summed, inverted, normed, folded, ot_taken = (m.sem(n) for n in (
            "maxed", "summed", "inverted", "normed", "folded", "ot_taken"))
        biased, y_ready, x_added = m.sem("biased"), m.sem("y_ready"), m.sem("x_added")
        dots_ready, lam_exps, mask_in = m.sem("dots_ready"), m.sem("lam_exps"), [m.sem(f"mask_in{u}") for u in range(4)]
        o_free = ot_taken if diff else x_added
        s_free = s_taken if diff else shifted
        LOADS = 16 * (7 if diff else 8 + (2 if keep_mask is not None else 0))
        PERIOD = 4
        run = lambda eng, stages: pipelined(eng, M, stages, period=PERIOD)
        at_most = lambda v: min(v, M) if isinstance(v, int) else v

        def tile_of(s, n):
            return PERIOD // CH * n + s // CH

        with nc.Block() as block:
            @block.sync
            def _(sp):
                sp.dma_start(Wq[:, :], wq).then_inc(loaded, 16)
                sp.dma_start(Wk[:, :], wk).then_inc(loaded, 16)
                sp.dma_start(Wv[:, :], wv).then_inc(loaded, 16)
                if not diff:
                    sp.dma_start(Wo[:, :], wo).then_inc(loaded, 16)
                    for column, b in ((bqc, bq), (bkc, bk), (bvc, bv)):
                        sp.dma_start(column[:, :], b.rearrange("(p a) -> p a", a=1)).then_inc(loaded, 16)
                    sp.dma_start(bias[:, :], bo.partition_broadcast(P)).then_inc(loaded, 16)
                if keep_mask is not None:
                    for h in range(2):
                        sp.dma_start(keep[64 * h:64 * h + 64, :], keep_mask[0, 0]).then_inc(loaded, 16)
                if diff:
                    for n, v in enumerate(lams):
                        sp.dma_start(lamv[:, n, :], v.rearrange("h d -> (h d)").partition_broadcast(P)).then_inc(loaded, 16)

                    def masks(i, s, n):
                        wait_past(sp, s_taken, 2 * (i - 3))
                        c = s % 2
                        for b in range(2):
                            src = add_mask[bass.ds(2 * tile_of(s, n) + b, 1), 8 * c:8 * c + 8, :, :]
                            for h in range(2):
                                sp.dma_start(amask[64 * h:64 * h + 64, s, b, :, :],
                                             src.rearrange("a h q k -> (a q) h k")).then_inc(mask_in[s], 16)
                    run(sp, [(0, masks)])

            @block.gpsimd
            def _(pool):
                pool.memset(spare[:, :], 0.0).then_inc(carried, 1)
                pool.wait_ge(carried, 1)
                pool.wait_ge(prepared, 2)

                def stage_ctx(i, s, n):
                    wait_past(pool, v_done, i - 1)
                    wait_past(pool, carried, i + 1)
                    pool.tensor_tensor(spare[:, :], spare[:, :], spare[:, :], ALU.add).then_inc(carried, 1)
                    tokens = m.ctxT[:, bass.ds(P * tile_of(s, n), P)].rearrange("p (b k) -> p b k", b=2)
                    pool.tensor_copy(cst[:, s % 2, :, :, :], tokens.unsqueeze(2).broadcast_to([P, 2, 2, SEQ])).then_inc(staged, 1)
                    if not diff:
                        mine = m.X[:, bass.ds(i, 1), :].rearrange("p a d -> p (a d)")
                        pool.tensor_tensor(mine, mine, bias[:, :], ALU.add).then_inc(biased, 1)

                def shift_masked(i, s, n):
                    for a in range(2):
                        pool.wait_ge(maxed, 2 * i + a + 1)
                        wait_past(pool, turned, 2 * i - 3 + a)
                        pool.tensor_tensor(E[:, s % 2, a, :].rearrange("p (v k) -> p v k", k=SEQ), Z[:, s % 2, a, :].rearrange("p (v k) -> p v k", k=SEQ),
                                           mx2[:, s % 2, 8 * a:8 * a + 8].unsqueeze(2).broadcast_to([P, 8, SEQ]), ALU.subtract).then_inc(shifted, 1)

                run(pool, [(1, stage_ctx)] + ([(1, shift_masked)] if diff else []))

            @block.tensor
            def _(pe):
                if not diff:
                    pe.wait_ge(prepared, 1)
                    pe.matmul(psO[:, 0:D], bvm[:, :], Wo[:, :], start=True, stop=True).then_inc(dots_ready, 1)
                pe.wait_ge(prepared, 2)

                def project_qk(i, s, n):
                    wait_past(pe, qk_taken, i)
                    wait_past(pe, v_taken, i - LP)
                    c = s % CH
                    x, ctx = m.xT[:, bass.ds(P * tile_of(s, n), P)], m.ctxT[:, bass.ds(P * tile_of(s, n), P)]
                    pe.matmul(psP[:, 0:P], Wq[:, c * P:c * P + P], x, start=True, stop=True)
                    pe.matmul(psP[:, P:2 * P], Wk[:, c * P:c * P + P], ctx, start=True, stop=True).then_inc(qk_done, 1)

                def project_v(i, s, n):
                    pe.wait_ge(staged, i + 1)
                    wait_past(pe, v_taken, i)
                    wait_past(pe, qk_taken, at_most(i + LP))
                    c = s % CH
                    for b in range(2):
                        last = pe.matmul(psP[:, 2 * P + b * VW:2 * P + b * VW + VW],
                                         cst[:, s % 2, b, :, :].rearrange("p t k -> p (t k)"), Wv[:, c * VW:c * VW + VW],
                                         start=True, stop=True)
                    last.then_inc(v_done, 1)

                def score(i, s, n):
                    pe.wait_ge(qk_taken, i + 1)
                    for a in range(2):
                        wait_past(pe, s_free, 2 * i - 1 + a)
                        for g in (2 * a, 2 * a + 1):
                            rows = slice(32 * g, 32 * g + 32)
                            for b in range(2):
                                last = pe.matmul(psS[:, g, b * P:b * P + P], QM[rows, s % 2, b, :, :].rearrange("p h q -> p (h q)"),
                                                 KM[rows, s % 2, b, :, :].rearrange("p j k -> p (j k)"), start=True, stop=True)
                        last.then_inc(scored, 1)

                def turn(i, s, n):
                    for a in range(2):
                        pe.wait_ge(exped, 2 * i + a + 1)
                        wait_past(pe, pt_ready, 2 * i - 1 + a)
                        for r in range(4):
                            last = pe.transpose(psT[:, a, r * P:r * P + P], E[:, s % 2, a, r * P:r * P + P], m.ident[:, :])
                        last.then_inc(turned, 1)

                def weigh(i, s, n):
                    pe.wait_ge(pt_ready, 2 * i + 2)
                    pe.wait_ge(v_taken, i + 1)
                    wait_past(pe, o_free, i)
                    for r in range(REGIONS):
                        last = pe.matmul(psO[:, r * RW:r * RW + WIDE], PT[:, s % 2, 2 * (r % 4) + r // 4, :],
                                         VZ[:, s % 2, r * RW:r * RW + WIDE], start=True, stop=True)
                    last.then_inc(summed, 1)

                def fold(i, s, n):
                    pe.wait_ge(normed, i + 1)
                    for b in range(2):
                        mine = On[:, 8 * b:8 * b + 8, :].rearrange("p r w -> p (r w)")
                        if diff:
                            last = pe.matmul(psO[64 * b:64 * b + 64, OTP], m.fold[:, :], mine, start=True, stop=True)
                        else:
                            last = pe.matmul(psO[:, SUMS + 64 * b:SUMS + 64 * b + 64], mine, m.fold[:, :], start=True, stop=True)
                    last.then_inc(folded, 1)

                def project_out(i, s, n):
                    pe.wait_ge(ot_taken, i + 1)
                    pe.matmul(psO[:, 0:D], OT[:, :], Wo[:, :], start=True, stop=True).then_inc(y_ready, 1)

                if diff:
                    run(pe, [(LS, score), (-2, fold), (LP, project_qk), (0, turn), (0, project_v), (-1, weigh)])
                else:
                    run(pe, [(LS, score), (-2, fold), (LP, project_qk), (-2, project_out), (0, turn), (0, project_v), (-1, weigh)])

            @block.scalar
            def _(act):
                if diff:
                    act.wait_ge(dots_ready, 1)
                    act.activation(lamv[:, 0, 0:HEADS], lamv[:, 1, 0:HEADS], ACT.Exp)
                    act.activation(lamv[:, 2, 0:HEADS], lamv[:, 3, 0:HEADS], ACT.Exp).then_inc(lam_exps, 1)

                def take_v(i, s, n):
                    act.wait_ge(v_done, i + 1)
                    act.wait_ge(qk_taken, at_most(i + LP + 1))
                    wait_past(act, summed, i - 1)
                    v = psP[:, 2 * P:2 * P + 2 * VW].rearrange("p (r j w) -> p r j w", r=REGIONS, w=W)
                    for j in range(2):
                        last = act.activation(regions(s % 2)[:, :, j, 0:W], v[:, :, j, :], ACT.Copy, scale=m.half_mask[:, j:j + 1])
                    last.then_inc(v_taken, 1)

                def exponent(i, s, n):
                    for a in range(2):
                        act.wait_ge(shifted, 2 * i + a + 1)
                        act.activation(E[:, s % 2, a, :], E[:, s % 2, a, :], ACT.Exp,
                                       scale=1.0 if diff else QK_SCALE).then_inc(exped, 1)

                def take_pt(i, s, n):
                    wait_past(act, summed, i - 1)
                    for a in range(2):
                        act.wait_ge(turned, 2 * i + a + 1)
                        act.activation(PT[:, s % 2, 4 * a:4 * a + 4, :].rearrange("p r q -> p (r q)"), psT[:, a, :], ACT.Copy).then_inc(pt_ready, 1)

                def take_o(i, s, n):
                    act.wait_ge(folded, i + 1)
                    if diff:
                        c = s % 2
                        act.activation(Oall[:, bass.ds(tile_of(s, n), 1), VW * c:VW * c + VW].rearrange("p a d -> p (a d)"), psO[:, OTP],
                                       ACT.Copy).then_inc(ot_taken, 1)
                        return
                    wait_past(act, y_ready, i)
                    act.activation(OT[:, :], psO[:, OTP], ACT.Copy).then_inc(ot_taken, 1)

                run(act, [(-2, take_o), (1, exponent), (0, take_pt), (0, take_v)])

            @block.vector
            def _(dve):
                chain = Chain(dve, chained)
                chain.link(dve.memset(VZ[:, :, :], 1.0))
                for par in range(2):
                    for j in range(2):
                        sums = regions(par)[:, :, j, W:W + 1]
                        dve.tensor_scalar(sums, sums, m.half_mask[:, j:j + 1], None, ALU.mult)
                if keep_mask is not None:
                    dve.memset(neg[:, :], -1e6 / QK_SCALE)
                chain.link(dve.tensor_scalar(qmask[:, :], m.head_mask[:, 0:2], QK_SCALE if diff else 1.0, None, ALU.mult))
                dve.wait_ge(loaded, LOADS)
                if keep_mask is not None:
                    chain.link(dve.tensor_scalar(drop[:, :], keep[:, :], 0, None, ALU.is_equal))
                if diff:
                    l0 = lamv[:, 0, :], lamv[:, 1, :], lamv[:, 2, :], lamv[:, 3, :]
                    dve.tensor_tensor(l0[0], l0[0], l0[1], ALU.mult)
                    chain.link(dve.tensor_tensor(l0[2], l0[2], l0[3], ALU.mult))
                    for n in (0, 2):
                        last = dve.tensor_reduce(lamv[:, n + 1, 0:HEADS], l0[n].rearrange("p (h d) -> p h d", d=DH), AX.X, ALU.add)
                    last.then_inc(dots_ready, 1)
                    dve.wait_ge(lam_exps, 1)
                    chain.link(dve.tensor_tensor(lam[:, :], lamv[:, 0, 0:HEADS], lamv[:, 2, 0:HEADS], ALU.subtract))
                    chain.link(dve.tensor_scalar(lam[:, :], lam[:, :], LAMBDA_INIT, -1.0, ALU.add, ALU.mult))
                    chain.link(dve.tensor_scalar(lam[:, :], lam[:, :], m.half_mask[:, 1:2], m.half_mask[:, 0:1], ALU.mult, ALU.add))
                    for b in range(2):
                        last = dve.tensor_copy(coef[:, :, b, :], lam[:, :].rearrange("p (c r) -> p c r", c=CH))
                    chain.link(last)
                    dve.memset(rs[:, :], 0.0).then_inc(prepared, 2)
                else:
                    chain.link(dve.memset(bvm[:, :], 1.0))
                    dve.tensor_scalar(bvm[:, :], bvm[:, :], bvc[:, 0:1], None, ALU.mult).then_inc(prepared, 1)
                    dve.wait_ge(dots_ready, 1)
                    dve.tensor_tensor(bias[:, :], bias[:, :], psO[:, 0:D], ALU.add).then_inc(prepared, 1)

                def take_qk(i, s, n):
                    dve.wait_ge(qk_done, i + 1)
                    wait_past(dve, v_done, i - LP + 1)
                    wait_past(dve, scored, 2 * (i - 1))
                    for out, src, mask, bc in ((QM, psP[:, 0:P], qmask[:, :], 0 if diff else bqc), (KM, psP[:, P:2 * P], m.head_mask[:, 2:4], 0 if diff else bkc)):
                        src = src.rearrange("p (b q) -> p b q", b=2)
                        for h in range(2):
                            if diff:
                                last = dve.tensor_scalar(out[:, s % 2, :, h, :], src, mask[:, h:h + 1], None, ALU.mult)
                            else:
                                last = dve.tensor_scalar(out[:, s % 2, :, h, :], src, bc[:, 0:1], mask[:, h:h + 1], ALU.add, ALU.mult)
                    last.then_inc(qk_taken, 1)

                def add_masks(i, s, n):
                    dve.wait_ge(mask_in[s], 64 * n + 64)
                    wait_past(dve, shifted, 2 * (i - 1))
                    for a in range(2):
                        dve.wait_ge(scored, 2 * i + a + 1)
                        by_batch = lambda v: v.rearrange("p g (b w) -> p g b w", b=2)
                        dve.tensor_tensor(by_batch(Z[:, s % 2, a, :].rearrange("p (g w) -> p g w", g=2)), by_batch(psS[:, 2 * a:2 * a + 2, 0:256]),
                                          amask[:, s, :, 4 * a:4 * a + 4, :].rearrange("p b (g j) k -> p g b (j k)", j=2),
                                          ALU.add).then_inc(s_taken, 1)
                    for a in range(2):
                        dve.wait_ge(s_taken, 2 * i + a + 1)
                        dve.tensor_reduce(mx2[:, s % 2, 8 * a:8 * a + 8], Z[:, s % 2, a, :].rearrange("p (v k) -> p v k", k=SEQ),
                                          AX.X, ALU.max).then_inc(maxed, 1)

                def shift(i, s, n):
                    banks = [psS[:, 2 * a:2 * a + 2, 0:256].rearrange("p g (v k) -> p g v k", k=SEQ) for a in range(2)]
                    tops = [mx[:, 8 * a:8 * a + 8].rearrange("p (g v) -> p g v", g=2) for a in range(2)]
                    passes = 4 if keep_mask is not None else 2
                    if keep_mask is not None:
                        m3 = drop[:, :].unsqueeze(1).unsqueeze(1).broadcast_to([P, 2, 4, SEQ])
                        n3 = neg[:, :].unsqueeze(1).unsqueeze(1).broadcast_to([P, 2, 4, SEQ])
                        for a in range(2):
                            dve.wait_ge(scored, 2 * i + a + 1)
                            dve.memset(carrier[:, a:a + 1], 0.0)
                            dve.copy_predicated(banks[a], m3, n3).then_inc(maxed, 1)
                    for a in range(2):
                        if keep_mask is not None:
                            dve.wait_ge(maxed, passes * i + a + 1)
                        else:
                            dve.wait_ge(scored, 2 * i + a + 1)
                            wait_past(dve, shifted, 2 * i)
                        dve.tensor_reduce(tops[a], banks[a], AX.X, ALU.max).then_inc(maxed, 1)
                    for a in range(2):
                        dve.wait_ge(maxed, passes * i + passes - 1 + a)
                        wait_past(dve, turned, 2 * i - 3 + a)
                        last = dve.tensor_tensor(E[:, s % 2, a, :].rearrange("p (g v k) -> p g v k", g=2, k=SEQ), banks[a],
                                                 tops[a].unsqueeze(3).broadcast_to([P, 2, 4, SEQ]), ALU.subtract)
                        last.then_inc(shifted, 1)

                def norm(i, s, n):
                    dve.wait_ge(summed, i + 1)
                    wait_past(dve, folded, i)
                    steps = 2
                    dve.reciprocal(rs[:, :], O_[:, :, W]).then_inc(inverted, 1)
                    dve.wait_ge(inverted, steps * i + 1)
                    if diff:
                        dve.tensor_tensor(rs[:, :], rs[:, :], coef[:, s % 2, :, :].rearrange("p b r -> p (b r)"), ALU.mult).then_inc(inverted, 1)
                        dve.wait_ge(inverted, steps * i + 2)
                        dve.tensor_tensor(On[:, :, :], O_[:, :, 0:W], rs[:, :].unsqueeze(2).broadcast_to([P, HV, W]), ALU.mult).then_inc(normed, 1)
                        return
                    dve.tensor_tensor(inv[:, :, :], rs[:, :].unsqueeze(2).broadcast_to([P, HV, 2]),
                                      m.half_mask[:, :].unsqueeze(1).broadcast_to([P, HV, 2]), ALU.mult).then_inc(inverted, 1)
                    dve.wait_ge(inverted, steps * i + 2)
                    dve.tensor_tensor(On[:, :, :].rearrange("p r (h d) -> p r h d", d=DH), O_[:, :, 0:W].rearrange("p r (h d) -> p r h d", d=DH),
                                      inv[:, :, :].unsqueeze(3).broadcast_to([P, HV, 2, DH]), ALU.mult).then_inc(normed, 1)

                def residual(i, s, n):
                    dve.wait_ge(y_ready, i + 1)
                    dve.wait_ge(biased, i + 1)
                    dve.tensor_tensor(m.X[:, i, :], m.X[:, i, :], psO[:, 0:D], ALU.add).then_inc(x_added, 1)

                if diff:
                    run(dve, [(-2, norm), (LS, add_masks), (LP, take_qk)])
                else:
                    run(dve, [(-2, norm), (1, shift), (-2, residual), (LP, take_qk)])


def differential_out(nc, m, part, Oall, wo, rms_scale):
    m.part = part
    with ExitStack() as own:
        def sb(name, shape, dt=F32):
            return own.enter_context(nc.sbuf_tensor(f"{part}_{name}", shape, dt))

        Wo, sc = sb("Wo", [P, D]), sb("sc", [P, 1])
        sq, inv = sb("sq", [P, NT * D]), sb("inv", [P, NT * HEADS])
        On, OT = sb("On", [P, 2, HEADS, DH]), sb("OT", [P, 2, P])
        psT = own.enter_context(nc.psum_tensor(part + "_psT", [P, 2, 512], F32))
        psY = own.enter_context(nc.psum_tensor(part + "_psY", [P, 2, 512], F32))
        loaded, chained, ms_ready, rms_ready = m.sem("loaded"), m.sem("chained"), m.sem("ms_ready"), m.sem("rms_ready")
        normed, turned, ot_ready, y_ready, x_added = (m.sem(n) for n in ("normed", "turned", "ot_ready", "y_ready", "x_added"))
        wo_scaled = m.sem("wo_scaled")

        with nc.Block() as block:
            @block.sync
            def _(sp):
                sp.dma_start(Wo[:, :], wo).then_inc(loaded, 16)
                sp.dma_start(sc[:, :], rms_scale).then_inc(loaded, 16)

            @block.vector
            def _(dve):
                chain = Chain(dve, chained)
                flat = Oall[:, :, :].rearrange("p n d -> p (n d)")
                chain.link(dve.tensor_tensor(sq[:, :], flat, flat, ALU.mult))
                chain.link(dve.tensor_reduce(inv[:, :], sq[:, :].rearrange("p (n d) -> p n d", d=DH), AX.X, ALU.add))
                dve.tensor_scalar(inv[:, :], inv[:, :], 1.0 / DH, EPS, ALU.mult, ALU.add).then_inc(ms_ready, 1)
                dve.wait_ge(loaded, 32)
                dve.tensor_scalar(Wo[:, :], Wo[:, :], sc[:, 0:1], 1.0 - LAMBDA_INIT, ALU.mult, ALU.mult).then_inc(wo_scaled, 1)
                dve.wait_ge(rms_ready, 1)
                chain.link(dve.reciprocal(inv[:, :], sq[:, 0:NT * HEADS]))

                def norm(i, u, n=None):
                    wait_past(dve, turned, i - 1)
                    dve.tensor_tensor(On[:, u, :, :], Oall[:, bass.ds(i, 1), :].rearrange("p a (h w) -> p (a h) w", w=DH),
                                      inv[:, bass.ds(HEADS * i, HEADS)].unsqueeze(2).broadcast_to([P, HEADS, DH]),
                                      ALU.mult).then_inc(normed, 1)

                def residual(i, u, n=None):
                    dve.wait_ge(y_ready, i + 1)
                    dve.tensor_tensor(m.X[:, i, :], m.X[:, i, :], psY[:, u, 0:D], ALU.add).then_inc(x_added, 1)

                def step(i, u, n=None):
                    norm(i, u)
                    residual(i - 1, 1 - u)

                norm(0, 0)
                step(1, 1)
                in_pairs(dve, 2, NT, step)
                residual(NT - 1, 1)

            @block.scalar
            def _(act):
                act.wait_ge(ms_ready, 1)
                act.activation(sq[:, 0:NT * HEADS], inv[:, :], ACT.Sqrt).then_inc(rms_ready, 1)

                def take(i, u, n=None):
                    act.wait_ge(turned, i + 1)
                    wait_past(act, y_ready, i - 1)
                    act.activation(OT[:, u, :], psT[:, u, 0:P], ACT.Copy).then_inc(ot_ready, 1)
                peeled(act, NT, take)

            @block.tensor
            def _(pe):
                pe.wait_ge(wo_scaled, 1)

                def turn(i, u, n=None):
                    pe.wait_ge(normed, i + 1)
                    wait_past(pe, ot_ready, i - 1)
                    pe.transpose(psT[:, u, 0:P], On[:, u, :, :].rearrange("p h w -> p (h w)"), m.ident[:, :]).then_inc(turned, 1)

                def project(i, u, n=None):
                    pe.wait_ge(ot_ready, i + 1)
                    wait_past(pe, x_added, i - 1)
                    pe.matmul(psY[:, u, 0:D], OT[:, u, :], Wo[:, :], start=True, stop=True).then_inc(y_ready, 1)

                def step(i, u, n=None):
                    turn(i, u)
                    project(i - 1, 1 - u)
                turn(0, 0)
                step(1, 1)
                in_pairs(pe, 2, NT, step)
                project(NT - 1, 1)


def norm_of_stats(dve, chain, stats, width, mean, var_eps, tmp):
    dve.tensor_tensor(mean, stats[:, :, 1], stats[:, :, 4], ALU.add)
    dve.tensor_tensor(tmp, stats[:, :, 1], stats[:, :, 4], ALU.subtract)
    chain.link(dve.tensor_tensor(var_eps, stats[:, :, 2], stats[:, :, 5], ALU.add))
    dve.tensor_scalar(mean, mean, 0.5, None, ALU.mult)
    dve.tensor_scalar(var_eps, var_eps, 1.0 / width, EPS, ALU.mult, ALU.add)
    chain.link(dve.scalar_tensor_tensor(tmp, tmp, 0.25, tmp, ALU.mult, ALU.mult))
    return dve.tensor_tensor(var_eps, var_eps, tmp, ALU.add)


HID0 = 512


def bit_ffn(nc, m, t):
    layer_norm(nc, m, "ln1", to_xT=False)
    m.part = "bit"
    C = HID0 // P
    G = NT // 4
    with ExitStack() as own:
        def sb(name, shape, dt=F32):
            return own.enter_context(nc.sbuf_tensor(f"bit_{name}", shape, dt))

        def pb(name, shape, dt=F32):
            return own.enter_context(nc.psum_tensor(f"bit_{name}", shape, dt))

        w1, w2 = sb("w1", [P, C, D]), sb("w2", [P, HID0])
        w1q, w2q = sb("w1q", [P, C, D], BF16), sb("w2q", [P, HID0], BF16)
        w1T, w2T = sb("w1T", [P, HID0], BF16), sb("w2T", [P, C, D], BF16)
        ones = sb("ones", [P, P])
        wsum, wmean, winv = sb("wsum", [P, 2]), sb("wmean", [P, 2]), sb("winv", [P, 2])
        g1, b1n, b2 = sb("g1", [P, D]), sb("b1n", [P, D]), sb("b2", [P, D])
        b1, g2, b2n = sb("b1", [P, HID0]), sb("g2", [P, HID0]), sb("b2n", [P, HID0])
        R, tmp = sb("R", [P, NT]), sb("tmp", [P, NT])
        mean2, rstd2, shift2 = sb("mean2", [P, NT]), sb("rstd2", [P, NT]), sb("shift2", [P, NT])
        stats = sb("stats", [P, NT, 6])
        H = sb("H", [P, NT, HID0])
        xh, xq, xqT = sb("xh", [P, 4, D]), sb("xq", [P, 2, 4 * D], BF16), sb("xqT", [P, 2, 4 * D], BF16)
        amax, scale, undo = sb("amax", [P, 4]), sb("scale", [P, 4]), sb("undo", [P, 2, 4])
        hn, hq, hqT = sb("hn", [P, 2, HID0]), sb("hq", [P, 2, HID0], BF16), sb("hqT", [P, 2, HID0], BF16)
        y = sb("y", [P, 2, D])
        psT = pb("psT", [P, 2, 1024], BF16)
        psH = pb("psH", [P, 4, HID0])
        psY = pb("psY", [P, 2, 512])
        loaded, chained, wsum_ready, wtot_ready, wq_ready, wT_turned, wT_ready = (m.sem(n) for n in (
            "loaded", "chained", "wsum_ready", "wtot_ready", "wq_ready", "wT_turned", "wT_ready"))
        r_in, r_out = m.sem("r_in"), m.sem("r_out")
        xq_ready, xq_turned, xqT_ready, up_ready, biased, gelued = (m.sem(n) for n in (
            "xq_ready", "xq_turned", "xqT_ready", "up_ready", "biased", "gelued"))
        n_ready, hq_ready, hq_turned, hqT_ready, down_ready, x_added = (m.sem(n) for n in (
            "n_ready", "hq_ready", "hq_turned", "hqT_ready", "down_ready", "x_added"))
        LOADS = 16 * 8

        with nc.Block() as block:
            @block.sync
            def _(sp):
                sp.dma_start(w1[:, :, :], t["L0_ffn_w1"].rearrange("(c p) d -> p c d", p=P)).then_inc(loaded, 16)
                sp.dma_start(w2[:, :], t["L0_ffn_w2"]).then_inc(loaded, 16)
                for dst, name in ((g1, "ln1_g"), (b1n, "ln1_b"), (b2, "b2"), (b1, "b1"), (g2, "ln2_g"), (b2n, "ln2_b")):
                    sp.dma_start(dst[:, :], t["L0_ffn_" + name].partition_broadcast(P)).then_inc(loaded, 16)

            @block.vector
            def _(dve):
                chain = Chain(dve, chained)
                dve.memset(ones[:, :], 1.0)
                chain.link(dve.tensor_tensor(tmp[:, :], m.rstd[:, :], m.rstd[:, :], ALU.mult))
                dve.tensor_scalar(tmp[:, :], tmp[:, :], -EPS, 1.0 + EPS, ALU.mult, ALU.add).then_inc(r_in, 1)
                dve.wait_ge(loaded, LOADS)
                dve.tensor_reduce(wsum[:, 0:1], w1[:, :, :], AX.XY, ALU.add, apply_absolute_value=True)
                dve.tensor_reduce(wsum[:, 1:2], w2[:, :], AX.X, ALU.add, apply_absolute_value=True).then_inc(wsum_ready, 1)
                dve.wait_ge(r_out, 1)
                chain.link(dve.reciprocal(tmp[:, :], R[:, :]))
                chain.link(dve.tensor_tensor(R[:, :], m.rstd[:, :], tmp[:, :], ALU.mult))
                dve.wait_ge(wtot_ready, 1)
                chain.link(dve.tensor_scalar(wmean[:, :], psY[:, 0, 0:2], 1.0 / (HID0 * D), EPS, ALU.mult, ALU.max))
                chain.link(dve.reciprocal(winv[:, :], wmean[:, :]))
                dve.tensor_scalar(w1[:, :, :], w1[:, :, :], winv[:, 0:1], 1.0, ALU.mult, ALU.min)
                chain.link(dve.tensor_scalar(w2[:, :], w2[:, :], winv[:, 1:2], 1.0, ALU.mult, ALU.min))
                dve.tensor_scalar(w1[:, :, :], w1[:, :, :], -1.0, MAGIC, ALU.max, ALU.add)
                chain.link(dve.tensor_scalar(w2[:, :], w2[:, :], -1.0, MAGIC, ALU.max, ALU.add))
                dve.tensor_scalar(w1q[:, :, :], w1[:, :, :], MAGIC, None, ALU.subtract)
                dve.tensor_scalar(w2q[:, :], w2[:, :], MAGIC, None, ALU.subtract).then_inc(wq_ready, 1)
                dve.wait_ge(wT_turned, 1)
                dve.tensor_copy(w1T[:, :], psT[:, 0, 0:HID0])
                dve.tensor_copy(w2T[:, :, :], psT[:, 1, 0:HID0].rearrange("p (c d) -> p c d", c=C)).then_inc(wT_ready, 1)
                before = chain.n
                A_LINKS = 8

                def quantise(g, u, n):
                    wait_past(dve, xq_turned, g - 1)
                    wait_past(dve, xq_ready, g)
                    c = Chain(dve, chained, before + A_LINKS * g)
                    for j in range(4):
                        i = 4 * g + j
                        last = dve.tensor_scalar(xh[:, j, :], m.X[:, i, :], m.mean[:, bass.ds(i, 1)],
                                                 R[:, bass.ds(i, 1)], ALU.subtract, ALU.mult)
                    c.link(last)
                    row = lambda v: v[:, :].unsqueeze(1).broadcast_to([P, 4, D])
                    c.link(dve.tensor_tensor(xh[:, :, :], xh[:, :, :], row(g1), ALU.mult))
                    c.link(dve.tensor_tensor(xh[:, :, :], xh[:, :, :], row(b1n), ALU.add))
                    c.link(dve.tensor_reduce(amax[:, :], xh[:, :, :], AX.X, ALU.max, apply_absolute_value=True))
                    c.link(dve.tensor_scalar(amax[:, :], amax[:, :], EPS, 1.0 / 127.0, ALU.max, ALU.mult))
                    dve.tensor_scalar(undo[:, u, :], amax[:, :], wmean[:, 0:1], None, ALU.mult)
                    c.link(dve.reciprocal(scale[:, :], amax[:, :]))
                    for j in range(4):
                        last = dve.tensor_scalar(xh[:, j, :], xh[:, j, :], scale[:, j:j + 1], 127.0, ALU.mult, ALU.min)
                    c.link(last)
                    c.link(dve.tensor_scalar(xh[:, :, :], xh[:, :, :], -128.0, MAGIC, ALU.max, ALU.add))
                    assert c.n == A_LINKS
                    dve.tensor_scalar(xq[:, u, :], xh[:, :, :].rearrange("p j d -> p (j d)"), MAGIC, None, ALU.subtract).then_inc(xq_ready, 1)

                def bias(g, u, n):
                    for j in range(4):
                        i = 4 * g + j
                        dve.wait_ge(up_ready, i + 1)
                        dve.scalar_tensor_tensor(H[:, bass.ds(i, 1), :].rearrange("p a h -> p (a h)"), psH[:, j, :], undo[:, u, j:j + 1], b1[:, :],
                                                 ALU.mult, ALU.add).then_inc(biased, 1)

                def measure(g, u, n):
                    dve.wait_ge(gelued, 4 * g + 4)
                    for j in range(4):
                        dve.bn_stats(stats[:, 4 * g + j, :], H[:, 4 * g + j, :])

                pipelined(dve, G, [(1, quantise), (0, bias), (-1, measure)])
                c = Chain(dve, chained, before + A_LINKS * G)
                c.link(dve.memset(y[:, 0, 0:1], 0.0))
                norm_of_stats(dve, c, stats, HID0, mean2[:, :], R[:, :], tmp[:, :]).then_inc(r_in, 1)
                dve.wait_ge(r_out, 2)
                c.link(dve.reciprocal(rstd2[:, :], tmp[:, :]))
                c.link(dve.scalar_tensor_tensor(shift2[:, :], mean2[:, :], -1.0, rstd2[:, :], ALU.mult, ALU.mult))
                dve.memset(y[:, 0, 0:1], 0.0).then_inc(r_in, 1)
                before_b = c.base + c.n
                B_LINKS = 7

                def quantise_h(i, u, n):
                    dve.wait_ge(n_ready, i + 1)
                    wait_past(dve, hq_turned, i - 1)
                    c = Chain(dve, chained, before_b + B_LINKS * i)
                    h = hn[:, u, :]
                    c.link(dve.tensor_tensor(h, h, g2[:, :], ALU.mult))
                    c.link(dve.tensor_tensor(h, h, b2n[:, :], ALU.add))
                    c.link(dve.tensor_reduce(amax[:, 0:1], h, AX.X, ALU.max, apply_absolute_value=True))
                    c.link(dve.tensor_scalar(amax[:, 0:1], amax[:, 0:1], EPS, 1.0 / 127.0, ALU.max, ALU.mult))
                    dve.tensor_scalar(undo[:, u, 0:1], amax[:, 0:1], wmean[:, 1:2], None, ALU.mult)
                    c.link(dve.reciprocal(scale[:, 0:1], amax[:, 0:1]))
                    c.link(dve.tensor_scalar(h, h, scale[:, 0:1], 127.0, ALU.mult, ALU.min))
                    c.link(dve.tensor_scalar(h, h, -128.0, MAGIC, ALU.max, ALU.add))
                    dve.tensor_scalar(hq[:, u, :], h, MAGIC, None, ALU.subtract).then_inc(hq_ready, 1)

                def residual(i, u, n):
                    dve.wait_ge(down_ready, i + 1)
                    dve.scalar_tensor_tensor(y[:, u, :], psY[:, u, 0:D], undo[:, u, 0:1], b2[:, :], ALU.mult, ALU.add).then_inc(x_added, 1)
                    dve.wait_ge(x_added, 2 * i + 1)
                    dve.tensor_tensor(m.X[:, i, :], m.X[:, i, :], y[:, u, :], ALU.add).then_inc(x_added, 1)

                pipelined(dve, NT, [(-1, residual), (1, quantise_h)])

            @block.scalar
            def _(act):
                act.wait_ge(r_in, 1)
                act.activation(R[:, :], tmp[:, :], ACT.Sqrt).then_inc(r_out, 1)

                def take(g, u, n):
                    act.wait_ge(xq_turned, g + 1)
                    wait_past(act, up_ready, 4 * (g - 1))
                    act.activation(xqT[:, u, :], psT[:, u, 0:4 * D], ACT.Copy).then_inc(xqT_ready, 1)

                def gelu(g, u, n):
                    for j in range(4):
                        i = 4 * g + j
                        act.wait_ge(biased, i + 1)
                        act.activation(H[:, i, :], H[:, i, :], ACT.Gelu).then_inc(gelued, 1)

                act.wait_ge(wT_ready, 1)
                pipelined(act, G, [(1, take), (0, gelu)])
                act.wait_ge(r_in, 2)
                act.activation(tmp[:, :], R[:, :], ACT.Sqrt).then_inc(r_out, 1)
                act.wait_ge(r_in, 3)

                def normalise(i, u, n):
                    wait_past(act, hq_ready, i - 1)
                    act.activation(hn[:, u, :], H[:, i, :], ACT.Identity, bias=shift2[:, bass.ds(i, 1)],
                                   scale=rstd2[:, bass.ds(i, 1)]).then_inc(n_ready, 1)

                def take_h(i, u, n):
                    act.wait_ge(hq_turned, i + 1)
                    wait_past(act, down_ready, i - 1)
                    act.activation(hqT[:, u, :], psT[:, u, 0:HID0], ACT.Copy).then_inc(hqT_ready, 1)

                pipelined(act, NT, [(2, normalise), (0, take_h)])

            @block.tensor
            def _(pe):
                pe.wait_ge(wsum_ready, 1)
                pe.matmul(psY[:, 0, 0:2], ones[:, :], wsum[:, :], start=True, stop=True).then_inc(wtot_ready, 1)
                pe.wait_ge(wq_ready, 1)
                for c in range(C):
                    pe.transpose(psT[:, 0, c * P:c * P + P], w1q[:, c, :], m.identb[:, :])
                for c in range(C):
                    last = pe.transpose(psT[:, 1, c * P:c * P + P], w2q[:, c * P:c * P + P], m.identb[:, :])
                last.then_inc(wT_turned, 1)
                pe.wait_ge(wT_ready, 1)

                def turn(g, u, n):
                    pe.wait_ge(xq_ready, g + 1)
                    wait_past(pe, xqT_ready, g - 1)
                    for j in range(4):
                        last = pe.transpose(psT[:, u, j * D:j * D + D], xq[:, u, j * D:j * D + D], m.identb[:, :])
                    last.then_inc(xq_turned, 1)

                def up(g, u, n):
                    pe.wait_ge(xqT_ready, g + 1)
                    for j in range(4):
                        wait_past(pe, biased, 4 * g + (j - 3))
                        pe.matmul(psH[:, j, :], xqT[:, u, j * D:j * D + D], w1T[:, :], start=True, stop=True).then_inc(up_ready, 1)

                pipelined(pe, G, [(0, up), (1, turn)])

                def turn_h(i, u, n):
                    pe.wait_ge(hq_ready, i + 1)
                    wait_past(pe, hqT_ready, i - 1)
                    for c in range(C):
                        last = pe.transpose(psT[:, u, c * P:c * P + P], hq[:, u, c * P:c * P + P], m.identb[:, :])
                    last.then_inc(hq_turned, 1)

                def down(i, u, n):
                    pe.wait_ge(hqT_ready, i + 1)
                    wait_past(pe, x_added, 2 * (i - 1))
                    for c in range(C):
                        last = pe.matmul(psY[:, u, 0:D], hqT[:, u, c * P:c * P + P], w2T[:, c, :],
                                         start=(c == 0), stop=(c == C - 1))
                    last.then_inc(down_ready, 1)

                pipelined(pe, NT, [(0, turn_h), (0, down)])


HID1, EXP1 = 512, 8
TOP1_SCALE = 2.0
BLOCKS = (TOK + EXP1 * (P - 1)) // P


def expert_ffn(nc, m, t):
    C, G = HID1 // P, NT // 4
    EARLY = 6
    xs = nc.dram_tensor("ex_xs", (BLOCKS * P, D), F32, kind="Internal").ap()
    ys = nc.dram_tensor("ex_ys", (BLOCKS * P, D), F32, kind="Internal").ap()
    with ExitStack() as own:
        def sb(name, shape, dt=F32):
            return own.enter_context(nc.sbuf_tensor(f"ex_{name}", shape, dt))

        def pb(name, shape, dt=F32):
            return own.enter_context(nc.psum_tensor(f"ex_{name}", shape, dt))

        prob = sb("prob", [P, NT, EXP1])
        layer_norm(nc, m, "ln3", router=(t["L1_ffn_w_router"], prob))
        m.part = "ex"
        wu, wg = sb("wu", [P, EXP1, HID1]), sb("wg", [P, EXP1, HID1])
        wd = sb("wd", [P, EXP1, C, D])
        order = sb("order", [P, EXP1])
        upto, uptob, onesb = sb("upto", [P, P]), sb("uptob", [P, P], BF16), sb("onesb", [P, P], BF16)
        number = sb("number", [1, BLOCKS])
        eq = sb("eq", [P, NT, EXP1])
        M, inc, fresh = (sb(n, [P, EXP1, NT]) for n in ("M", "inc", "fresh"))
        Mb, incb, excb = (sb(n, [P, EXP1, NT], BF16) for n in ("Mb", "incb", "excb"))
        top, total, weight = sb("top", [P, NT]), sb("total", [P, NT]), sb("weight", [P, NT])
        count, whole, ends, one8 = (sb(n, [P, EXP1]) for n in ("count", "whole", "ends", "one8"))
        pos = sb("pos", [P, NT], I32)
        over = sb("over", [1, BLOCKS, EXP1 - 1])
        ids = sb("ids", [1, BLOCKS], I32)
        sg, h, upc = sb("sg", [P, 2, 512]), sb("h", [P, 2, 512]), sb("upc", [P, 2, 512])
        S = sb("S", [P, NT, D])
        idx = sb("idx", [P, 4], I32)
        row = sb("row", [P, 4, D])
        out = sb("out", [P, 4, D])
        GT, hT = sb("GT", [P, 2, P]), sb("hT", [P, 2, 512])
        zero, spare = sb("zero", [P, D]), sb("spare", [P, 1])
        psU, psG, psH = pb("psU", [P, 2, 512]), pb("psG", [P, 2, 512]), pb("psH", [P, 2, 512])
        psX, psY = pb("psX", [P, 512]), pb("psY", [P, 512])
        loaded, w_loaded, chained, shifted, exped = (m.sem(n) for n in ("loaded", "w_loaded", "chained", "shifted", "exped"))
        zeroed, z_out, counting, counted, given, carried = (m.sem(n) for n in (
            "zeroed", "z_out", "counting", "counted", "given", "carried"))
        up_ready, gated, h_ready, down_done, s_written = (m.sem(n) for n in ("up_ready", "gated", "h_ready", "down_done", "s_written"))
        experts_in, up_taken = m.sem("experts_in"), m.sem("up_taken")
        scattered = [m.sem(f"scattered{s}") for s in range(4)]

        def shared_up(pe, q, c, g):
            wait_past(pe, h_ready, q - 1)
            x = m.xT[:, bass.ds(512 * g, 512)]
            pe.matmul(psU[:, c % 2, :], wu[:, EXP1 - 1, c * P:c * P + P], x, start=True, stop=True)
            pe.matmul(psG[:, c % 2, :], wg[:, EXP1 - 1, c * P:c * P + P], x, start=True, stop=True).then_inc(up_ready, 1)

        def shared_down(pe, q, c, g, half):
            pe.wait_ge(h_ready, q + 1)
            if c == 0:
                wait_past(pe, s_written, g - 1)
            for j in range(4):
                last = pe.matmul(psH[:, half, j * D:j * D + D], h[:, c % 2, j * P:j * P + P], wd[:, EXP1 - 1, c, :],
                                 start=(c == 0 and j == 0), stop=(c == C - 1), skip_group_check=True)
            last.then_inc(down_done, 1)

        def shared_silu(act, q, u):
            act.wait_ge(up_ready, q + 1)
            wait_past(act, h_ready, q - 1)
            act.activation(sg[:, u, :], psG[:, u, :], ACT.Silu).then_inc(gated, 1)

        def shared_take(act, g, half):
            act.wait_ge(down_done, C * g + C)
            act.activation(S[:, bass.ds(4 * g, 4), :].rearrange("p j d -> p (j d)"), psH[:, half, :], ACT.Copy).then_inc(s_written, 1)

        def shared_product(eng, q, u, up=psU):
            eng.wait_ge(gated, q + 1)
            wait_past(eng, down_done, q - 1)
            eng.tensor_tensor(h[:, u, :], up[:, u, :], sg[:, u, :], ALU.mult).then_inc(h_ready, 1)

        ON_POOL = 8
        UNITS = EARLY * C
        with nc.Block() as block:
            @block.sync
            def _(sp):
                sp.dma_start(wu[:, EXP1 - 1, :], t["L1_ffn_ws_up"]).then_inc(w_loaded, 16)
                sp.dma_start(wg[:, EXP1 - 1, :], t["L1_ffn_ws_gate"]).then_inc(w_loaded, 16)
                sp.dma_start(wd[:, EXP1 - 1, :, :], t["L1_ffn_ws_down"].rearrange("(c p) d -> p c d", p=P)).then_inc(w_loaded, 16)
                sp.dma_start(order[:, :], t["c_order"].partition_broadcast(P)).then_inc(loaded, 16)
                sp.dma_start(upto[:, :], t["c_upto"]).then_inc(loaded, 16)
                sp.dma_start(number[:, :], t["c_blocks"].rearrange("(a b) -> a b", a=1)).then_inc(loaded, 16)
                sp.wait_ge(zeroed, 1)
                sp.dma_start(xs.rearrange("(b p) d -> p b d", p=P), zero[:, :].unsqueeze(1).broadcast_to([P, BLOCKS, D])).then_inc(z_out, 16)
                sp.dma_start(wu[:, 0:EXP1 - 1, :], t["L1_ffn_w_up"].rearrange("e d h -> d e h")).then_inc(experts_in, 16)
                sp.dma_start(wg[:, 0:EXP1 - 1, :], t["L1_ffn_w_gate"].rearrange("e d h -> d e h")).then_inc(experts_in, 16)
                sp.dma_start(wd[:, 0:EXP1 - 1, :, :], t["L1_ffn_w_down"].rearrange("e (c p) d -> p e c d", p=P)).then_inc(experts_in, 16)
                sp.wait_ge(experts_in, 48)

            @block.gpsimd
            def _(pool):
                pool.memset(zero[:, :], 0.0).then_inc(zeroed, 1)
                for q in range(ON_POOL):
                    pool.wait_ge(up_taken, q + 1)
                    shared_product(pool, q, q % 2, up=upc)
                pool.wait_ge(z_out, 16)

                def scatter(i, s, n):
                    pool.wait_ge(given, i + 1)
                    wait_past(pool, carried, i)
                    pool.tensor_tensor(spare[:, :], zero[:, 0:1], zero[:, 0:1], ALU.add).then_inc(carried, 1)
                    pool.indirect_dma_start(xs, bass.IndirectOffsetOnAxis(ap=idx[:, s:s + 1], axis=0), row[:, s, :], None).then_inc(scattered[s], 16)

                pipelined(pool, NT, [(0, scatter)], period=4)
                for s in range(4):
                    pool.wait_ge(scattered[s], 16 * NT // 4)

            @block.scalar
            def _(act):
                act.wait_ge(shifted, 1)
                act.activation(prob[:, :, :], prob[:, :, :], ACT.Exp).then_inc(exped, 1)

                def silu(q, s, n):
                    if isinstance(q, int) and q < ON_POOL:
                        act.wait_ge(up_ready, q + 1)
                        wait_past(act, h_ready, q - 1)
                        act.activation(upc[:, s % 2, :], psU[:, s % 2, :], ACT.Copy).then_inc(up_taken, 1)
                    shared_silu(act, q, s % 2)

                def take(q, s, n):
                    if s % C == C - 1:
                        shared_take(act, 2 * n + s // C, s // C)

                pipelined(act, UNITS, [(0, silu), (-1, take)], period=2 * C)

            @block.tensor
            def _(pe):
                def up(q, s, n):
                    shared_up(pe, q, s % C, 2 * n + s // C)

                def down(q, s, n):
                    shared_down(pe, q, s % C, 2 * n + s // C, s // C)

                pe.wait_ge(w_loaded, 48)
                for q in range(ON_POOL):
                    up(q, q, 0)
                    if q:
                        down(q - 1, q - 1, 0)
                pe.wait_ge(counting, 1)
                flat = lambda v: v[:, :, :].rearrange("p e n -> p (e n)")
                pe.matmul(psX[:, 0:EXP1 * NT], uptob[:, :], flat(Mb), start=True, stop=False)
                pe.matmul(psX[:, 0:EXP1 * NT], onesb[:, :], flat(excb), start=False, stop=True)
                pe.matmul(psY[:, 0:EXP1], onesb[:, :], incb[:, :, NT - 1], start=True, stop=True).then_inc(counted, 1)
                down(ON_POOL - 1, ON_POOL - 1, 0)
                with pe.Fori(1, UNITS // ON_POOL) as k:
                    for s in range(ON_POOL):
                        up(ON_POOL * k + s, s, k)
                        if s:
                            down(ON_POOL * k + s - 1, s - 1, k)
                    down(ON_POOL * k + ON_POOL - 1, ON_POOL - 1, k)

            @block.vector
            def _(dve):
                chain = Chain(dve, chained)
                wide = lambda v: v[:, :].unsqueeze(2).broadcast_to([P, NT, EXP1])
                flat = lambda v: v[:, :, :].rearrange("p e n -> p (e n)")
                chain.link(dve.tensor_reduce(top[:, :], prob[:, :, :], AX.X, ALU.max))
                dve.tensor_tensor(prob[:, :, :], prob[:, :, :], wide(top), ALU.subtract).then_inc(shifted, 1)
                dve.memset(onesb[:, :], 1.0)
                dve.memset(one8[:, :], 1.0)
                chain.link(dve.memset(fresh[:, :, :], 1.0))
                dve.memset(fresh[:, :, 0:1], 0.0)
                dve.wait_ge(loaded, 48)
                dve.tensor_copy(uptob[:, :], upto[:, :])
                dve.wait_ge(exped, 1)
                chain.link(dve.tensor_reduce(total[:, :], prob[:, :, :], AX.X, ALU.add))
                chain.link(dve.reciprocal(total[:, :], total[:, :]))
                chain.link(dve.tensor_tensor(prob[:, :, :], prob[:, :, :], wide(total), ALU.mult))
                chain.link(dve.tensor_reduce(top[:, :], prob[:, :, :], AX.X, ALU.max))
                chain.link(dve.tensor_tensor(eq[:, :, :], prob[:, :, :], wide(top), ALU.is_equal))
                chain.link(dve.tensor_tensor(eq[:, :, :], eq[:, :, :], order[:, :].unsqueeze(1).broadcast_to([P, NT, EXP1]), ALU.mult))
                chain.link(dve.tensor_reduce(total[:, :], eq[:, :, :], AX.X, ALU.max))
                by_token = M[:, :, :].rearrange("p e n -> p n e")
                chain.link(dve.tensor_tensor(by_token, eq[:, :, :], wide(total), ALU.is_equal))
                dve.tensor_copy(Mb[:, :, :], M[:, :, :])
                chain.link(dve.tensor_tensor_scan(flat(inc), flat(fresh), flat(M), 0.0, ALU.mult, ALU.add))
                dve.tensor_copy(incb[:, :, :], inc[:, :, :])
                dve.tensor_tensor(excb[:, :, :], inc[:, :, :], M[:, :, :], ALU.subtract).then_inc(counting, 1)
                chain.link(dve.tensor_scalar(weight[:, :], M[:, EXP1 - 1, :], -TOP1_SCALE, TOP1_SCALE, ALU.mult, ALU.add))
                dve.tensor_tensor(weight[:, :], weight[:, :], top[:, :], ALU.mult)
                dve.wait_ge(counted, 1)
                chain.link(dve.tensor_scalar(count[:, :], psY[:, 0:EXP1], (P - 1) / 2, 1.0 / P, ALU.add, ALU.mult))
                chain.link(dve.tensor_scalar(whole[:, :], count[:, :], MAGIC, -MAGIC, ALU.add, ALU.add))
                chain.link(dve.tensor_tensor_scan(ends[:, :], one8[:, :], whole[:, :], 0.0, ALU.mult, ALU.add))
                chain.link(dve.tensor_tensor(count[:, :], ends[:, :], whole[:, :], ALU.subtract))
                chain.link(dve.tensor_scalar(count[:, :], count[:, :], float(P), -1.0, ALU.mult, ALU.add))
                chain.link(dve.tensor_tensor(inc[:, :, :], psX[:, 0:EXP1 * NT].rearrange("p (e n) -> p e n", n=NT),
                                             count[:, :].unsqueeze(2).broadcast_to([P, EXP1, NT]), ALU.add))
                chain.link(dve.tensor_tensor(inc[:, :, :], inc[:, :, :], M[:, :, :], ALU.mult))
                chain.link(dve.tensor_reduce(total[:, :], inc[:, :, :].rearrange("p e n -> p n e"), AX.X, ALU.add))
                dve.tensor_copy(pos[:, :], total[:, :])
                full = [1, BLOCKS, EXP1 - 1]
                chain.link(dve.tensor_tensor(over[:, :, :], ends[0:1, 0:EXP1 - 1].unsqueeze(1).broadcast_to(full),
                                             number[:, :].unsqueeze(2).broadcast_to(full), ALU.is_le))
                chain.link(dve.tensor_reduce(inc[0:1, 0:2, :].rearrange("p e n -> p (e n)")[:, 0:BLOCKS], over[:, :, :], AX.X, ALU.add))
                chain.link(dve.tensor_copy(ids[:, :], inc[0:1, 0:2, :].rearrange("p e n -> p (e n)")[:, 0:BLOCKS]))
                dve.wait_ge(h_ready, ON_POOL)

                def give(i, s, n):
                    wait_past(dve, scattered[s % 4], 16 * (2 * n + s // 4))
                    dve.tensor_copy(idx[:, s % 4:s % 4 + 1], pos[:, bass.ds(i, 1)])
                    dve.tensor_scalar(row[:, s % 4, :], m.X[:, bass.ds(i, 1), :].rearrange("p a d -> p (a d)"), m.mean[:, bass.ds(i, 1)],
                                      m.rstd[:, bass.ds(i, 1)], ALU.subtract, ALU.mult).then_inc(given, 1)

                def step(k, i0, q0):
                    for s in range(8):
                        give(i0 + s, s, k)
                        if s % 2:
                            shared_product(dve, q0 + s // 2, s // 2 % 2)
                step(0, 0, ON_POOL)
                with dve.Fori(1, NT // 8) as k:
                    step(k, 8 * k, ON_POOL + 4 * k)

        m.part = "exb"
        x_in, y_out = ([m.sem(f"{n}{s}") for s in range(4)] for n in ("x_in", "y_out"))
        turned, gt_ready, ug_ready, silued, hb_ready = (m.sem(n) for n in ("turned", "gt_ready", "ug_ready", "silued", "hb_ready"))
        h_turned, ht_ready, y_ready, y_taken = (m.sem(n) for n in ("h_turned", "ht_ready", "y_ready", "y_taken"))
        run = lambda eng, stages: pipelined(eng, BLOCKS, stages, period=4)
        with nc.Block() as block:
            @block.sync
            def _(sp):
                def load(b, s, n):
                    wait_past(sp, turned, b - 3)
                    sp.dma_start(row[:, s, :], xs[bass.ds(P * b, P), :]).then_inc(x_in[s], 16)

                def store(b, s, n):
                    sp.wait_ge(y_taken, b + 1)
                    sp.dma_start(ys[bass.ds(P * b, P), :], out[:, s, :]).then_inc(y_out[s], 16)

                run(sp, [(4, load), (-2, store)])
                for s in range(4):
                    sp.wait_ge(y_out[s], 16 * len(range(s, BLOCKS, 4)))

            @block.tensor
            def _(pe):
                def turn(b, s, n):
                    pe.wait_ge(x_in[s], 16 * n + 16)
                    wait_past(pe, gt_ready, b)
                    pe.transpose(psX[:, 0:P], row[:, s, :], m.ident[:, :]).then_inc(turned, 1)

                def expert_of(b):
                    return pe.value_load(ids[0:1, bass.ds(b, 1)], min_val=0, max_val=EXP1 - 1)

                def up(b, s, n):
                    e = expert_of(b)
                    pe.wait_ge(gt_ready, b + 1)
                    wait_past(pe, hb_ready, b - 1)
                    pe.matmul(psU[:, s % 2, :], GT[:, s % 2, :], wu[:, bass.ds(e, 1), :].rearrange("p a h -> p (a h)"), start=True, stop=True)
                    pe.matmul(psG[:, s % 2, :], GT[:, s % 2, :], wg[:, bass.ds(e, 1), :].rearrange("p a h -> p (a h)"), start=True, stop=True).then_inc(ug_ready, 1)

                def turn_h(b, s, n):
                    pe.wait_ge(hb_ready, b + 1)
                    wait_past(pe, ht_ready, b - 1)
                    for c in range(C):
                        last = pe.transpose(psH[:, s % 2, c * P:c * P + P], h[:, s % 2, c * P:c * P + P], m.ident[:, :])
                    last.then_inc(h_turned, 1)

                def down(b, s, n):
                    e = expert_of(b)
                    pe.wait_ge(ht_ready, b + 1)
                    wait_past(pe, y_taken, b)
                    for c in range(C):
                        last = pe.matmul(psY[:, 0:D], hT[:, s % 2, c * P:c * P + P], wd[:, bass.ds(e, 1), c, :].rearrange("p a d -> p (a d)"),
                                         start=(c == 0), stop=(c == C - 1))
                    last.then_inc(y_ready, 1)

                run(pe, [(1, turn), (0, up), (-1, turn_h), (-2, down)])

            @block.scalar
            def _(act):
                def take_x(b, s, n):
                    act.wait_ge(turned, b + 1)
                    wait_past(act, ug_ready, b - 1)
                    act.activation(GT[:, s % 2, :], psX[:, 0:P], ACT.Copy).then_inc(gt_ready, 1)

                def silu(b, s, n):
                    act.wait_ge(ug_ready, b + 1)
                    wait_past(act, hb_ready, b - 1)
                    act.activation(sg[:, s % 2, :], psG[:, s % 2, :], ACT.Silu).then_inc(silued, 1)

                def take_y(b, s, n):
                    act.wait_ge(y_ready, b + 1)
                    wait_past(act, y_out[s], 16 * n)
                    act.activation(out[:, s, :], psY[:, 0:D], ACT.Copy).then_inc(y_taken, 1)

                run(act, [(1, take_x), (0, silu), (-2, take_y)])

            @block.vector
            def _(dve):
                def product(b, s, n):
                    dve.wait_ge(silued, b + 1)
                    wait_past(dve, h_turned, b - 1)
                    dve.tensor_tensor(h[:, s % 2, :], psU[:, s % 2, :], sg[:, s % 2, :], ALU.mult).then_inc(hb_ready, 1)

                def take_h(b, s, n):
                    dve.wait_ge(h_turned, b + 1)
                    wait_past(dve, y_ready, b - 1)
                    dve.tensor_scalar(hT[:, s % 2, :], psH[:, s % 2, :], 1.0, None, ALU.mult).then_inc(ht_ready, 1)

                run(dve, [(0, product), (-1, take_h)])

        m.part = "exg"
        asked, gathered, carried, combined, x_added = m.sem("asked"), [m.sem(f"gathered{s}") for s in range(4)], *(
            m.sem(n) for n in ("carried", "combined", "x_added"))
        LATE = range(UNITS, G * C)
        with nc.Block() as block:
            @block.gpsimd
            def _(pool):
                def gather(i, s, n):
                    pool.wait_ge(asked, i + 1)
                    wait_past(pool, combined, i - 3)
                    wait_past(pool, carried, i)
                    pool.tensor_tensor(spare[:, :], zero[:, 0:1], zero[:, 0:1], ALU.add).then_inc(carried, 1)
                    pool.indirect_dma_start(row[:, s, :], None, ys, bass.IndirectOffsetOnAxis(ap=idx[:, s:s + 1], axis=0)).then_inc(gathered[s], 16)

                pipelined(pool, NT, [(0, gather)], period=4)

            @block.tensor
            def _(pe):
                for q in LATE:
                    shared_up(pe, q, q % C, q // C)
                    if q > UNITS:
                        shared_down(pe, q - 1, (q - 1) % C, (q - 1) // C, (q - 1) // C % 2)
                shared_down(pe, LATE[-1], C - 1, G - 1, (G - 1) % 2)

            @block.scalar
            def _(act):
                for q in LATE:
                    shared_silu(act, q, q % 2)
                    if q % C == 0 and q > UNITS:
                        shared_take(act, q // C - 1, (q // C - 1) % 2)
                shared_take(act, G - 1, (G - 1) % 2)

            @block.vector
            def _(dve):
                def ask(i, s, n):
                    wait_past(dve, gathered[s % 4], 16 * (2 * n + s // 4))
                    dve.tensor_copy(idx[:, s % 4:s % 4 + 1], pos[:, bass.ds(i, 1)]).then_inc(asked, 1)

                def product(i, s, n):
                    if s % 4 == 0:
                        shared_product(dve, UNITS + 2 * n + s // 4, s // 4)

                def combine(i, s, n):
                    dve.wait_ge(gathered[s % 4], 16 * (2 * n + s // 4) + 16)
                    if isinstance(i, int) and i >= 4 * EARLY:
                        dve.wait_ge(s_written, i // 4 + 1)
                    mine = S[:, bass.ds(i, 1), :].rearrange("p a d -> p (a d)")
                    dve.scalar_tensor_tensor(mine, row[:, s % 4, :], weight[:, bass.ds(i, 1)], mine, ALU.mult, ALU.add).then_inc(combined, 1)

                def residual(i, s, n):
                    dve.wait_ge(combined, i + 1)
                    mine = m.X[:, bass.ds(i, 1), :]
                    dve.tensor_tensor(mine, mine, S[:, bass.ds(i, 1), :], ALU.add).then_inc(x_added, 1)

                pipelined(dve, NT, [(3, ask), (0, product), (0, combine), (-1, residual)], period=8)


HID2, EXP2 = 32, 64
GROUP = 64
BUDGET = TOK // GROUP * 16
HALF = TOK // 2
NG = HALF // GROUP


def sort_levels():
    run = 2
    while run <= HALF:
        dist = run // 2
        while dist:
            yield run, dist
            dist //= 2
        run *= 2


def compare(dve, src, dst, run, dist):
    if run >= HALF:
        s = src.rearrange("p (b two d) -> p b two d", two=2, d=dist)
        o = dst.rearrange("p (b two d) -> p b two d", two=2, d=dist)
        dve.tensor_tensor(o[:, :, 0, :], s[:, :, 0, :], s[:, :, 1, :], ALU.max)
        return dve.tensor_tensor(o[:, :, 1, :], s[:, :, 0, :], s[:, :, 1, :], ALU.min)
    s = src.rearrange("p (r way b two d) -> p r way b two d", way=2, b=run // 2 // dist, two=2, d=dist)
    o = dst.rearrange("p (r way b two d) -> p r way b two d", way=2, b=run // 2 // dist, two=2, d=dist)
    for way in range(2):
        a, b = s[:, :, way, :, 0, :], s[:, :, way, :, 1, :]
        dve.tensor_tensor(o[:, :, way, :, way, :], a, b, ALU.max)
        last = dve.tensor_tensor(o[:, :, way, :, 1 - way, :], a, b, ALU.min)
    return last


def grouped_ffn(nc, m, t):
    C = EXP2 * HID2 // P
    EC = EXP2 // C
    with ExitStack() as own:
        def sb(name, shape, dt=F32, on=own):
            return on.enter_context(nc.sbuf_tensor(f"gr_{name}", shape, dt))

        def pb(name, shape, dt=F32, on=own):
            return on.enter_context(nc.psum_tensor(f"gr_{name}", shape, dt))

        V = sb("V", [P, HALF])
        wu, wg, wd = sb("wu", [P, EXP2, HID2]), sb("wg", [P, EXP2, HID2]), sb("wd", [P, C, D])
        bu, bg = sb("bu", [P, C]), sb("bg", [P, C])
        bd = sb("bd", [P, D])
        pick = sb("pick", [P, P, HID2])
        w_loaded = None
        with ExitStack() as routing:
            S = sb("S", [P, NT, EXP2], on=routing)
            layer_norm(nc, m, "ln5", router=(t["L2_ffn_Wr"], S))
            m.part = "gr"
            w_loaded = m.sem("w_loaded")
            A, B = sb("A", [P, HALF], on=routing), sb("B", [P, HALF], on=routing)
            br = sb("br", [P, EXP2], on=routing)
            sgn = sb("sgn", [P, 1], on=routing)
            mats = sb("mats", [P, 7, P], on=routing)
            ALL, SAME_HALF, SAME_EXP, LOW_UP, EARLIER, SWAP, LOW_UP_EXP = range(7)
            top, total = sb("top", [P, NT], on=routing), sb("total", [P, NT], on=routing)
            gsum, gmin = sb("gsum", [P, NG], on=routing), sb("gmin", [P, NG], on=routing)
            eq, sel, rank, excl = (sb(n, [P, NG], on=routing) for n in ("eq", "sel", "rank", "excl"))
            ones = sb("ones", [P, HALF], on=routing)
            count, cols = sb("count", [P, 4], on=routing), sb("cols", [P, 8], on=routing)
            cur, cand, bit, flag = (sb(n, [P, 1], I32, on=routing) for n in ("cur", "cand", "bit", "flag"))
            psV = pb("psV", [P, 4, 512], on=routing)
            psC = pb("psC", [P, 512], on=routing)
            psR = pb("psR", [P, 512], on=routing)
            loaded, chained, shifted, exped, s_ready, turned, v_taken, swapped, swap_in = (m.sem(n) for n in (
                "loaded", "chained", "shifted", "exped", "s_ready", "turned", "v_taken", "swapped", "swap_in"))
            picked, counted, total_ready, asked, answered, kept, summed = (m.sem(n) for n in (
                "picked", "counted", "total_ready", "asked", "answered", "kept", "summed"))
            BITS = 31

            with nc.Block() as block:
                @block.sync
                def _(sp):
                    sp.dma_start(br[:, :], t["L2_ffn_br"].partition_broadcast(P)).then_inc(loaded, 16)
                    sp.dma_start(mats[:, :, :], t["c_mats"]).then_inc(loaded, 16)
                    sp.dma_start(sgn[:, :], t["c_sign"]).then_inc(loaded, 16)
                    sp.dma_start(wu[:, :, :], t["L2_ffn_Wup"].rearrange("e d h -> d e h")).then_inc(w_loaded, 16)
                    sp.dma_start(wg[:, :, :], t["L2_ffn_Wgate"].rearrange("e d h -> d e h")).then_inc(w_loaded, 16)
                    sp.dma_start(wd[:, :, :], t["L2_ffn_Wdown"].rearrange("(c e) h d -> (e h) c d", e=EC)).then_inc(w_loaded, 16)
                    sp.dma_start(bu[:, :], t["bup_cols"]).then_inc(w_loaded, 16)
                    sp.dma_start(bg[:, :], t["bgate_cols"]).then_inc(w_loaded, 16)
                    for hf in range(2):
                        sp.dma_start(bd[EXP2 * hf:EXP2 * hf + EXP2, :], t["L2_ffn_bdown"]).then_inc(w_loaded, 16)
                    sp.wait_ge(swapped, 1)
                    for hf in range(2):
                        sp.dma_start(B[EXP2 * hf:EXP2 * hf + EXP2, :], A[EXP2 * (1 - hf):EXP2 * (1 - hf) + EXP2, :]).then_inc(swap_in, 16)
                    sp.wait_ge(w_loaded, 16 * 7)

                @block.gpsimd
                def _(pool):
                    pool.tensor_copy(pick[:, :, :], m.ident[:, :].unsqueeze(2).broadcast_to([P, P, HID2])).then_inc(picked, 1)
                    pool.wait_ge(picked, 1)

                @block.scalar
                def _(act):
                    act.wait_ge(shifted, 1)
                    act.activation(S[:, :, :], S[:, :, :], ACT.Exp).then_inc(exped, 1)
                    act.wait_ge(turned, 1)
                    act.activation(V[:, :], psV[:, :, :].rearrange("p a b -> p (a b)"), ACT.Copy).then_inc(v_taken, 1)

                @block.vector
                def _(dve):
                    chain = Chain(dve, chained)
                    dve.memset(ones[:, :], 1.0)
                    dve.memset(cur[:, :], 0)
                    dve.memset(bit[:, :], 1 << (BITS - 1))
                    wide = lambda v: v[:, :].unsqueeze(2).broadcast_to([P, NT, EXP2])
                    dve.wait_ge(loaded, 48)
                    chain.link(dve.tensor_tensor(S[:, :, :], S[:, :, :], br[:, :].unsqueeze(1).broadcast_to([P, NT, EXP2]), ALU.add))
                    chain.link(dve.tensor_reduce(top[:, :], S[:, :, :], AX.X, ALU.max))
                    dve.tensor_tensor(S[:, :, :], S[:, :, :], wide(top), ALU.subtract).then_inc(shifted, 1)
                    dve.wait_ge(exped, 1)
                    chain.link(dve.tensor_reduce(total[:, :], S[:, :, :], AX.X, ALU.add))
                    chain.link(dve.reciprocal(total[:, :], total[:, :]))
                    dve.tensor_tensor(B[:, :].rearrange("p (i h e) -> p h i e", h=2, e=EXP2), S[:, :, :].rearrange("p (h i) e -> p h i e", h=2),
                                      wide(total).rearrange("p (h i) e -> p h i e", h=2), ALU.mult).then_inc(s_ready, 1)
                    dve.wait_ge(v_taken, 1)
                    chain.link(dve.tensor_scalar(A[:, :], V[:, :], sgn[:, 0:1], None, ALU.mult))
                    here, there = A, B
                    for run, dist in sort_levels():
                        last = compare(dve, here[:, :], there[:, :], run, dist)
                        here, there = there, here
                        if (run, dist) != (HALF, 1):
                            chain.link(last)
                    assert here is A
                    last.then_inc(swapped, 1)
                    dve.wait_ge(swap_in, 32)
                    chain.link(dve.scalar_tensor_tensor(B[:, :], B[:, :], -1.0, A[:, :], ALU.mult, ALU.max))
                    chain.link(dve.tensor_scalar(A[:, :], B[:, :], sgn[:, 0:1], None, ALU.mult))
                    here, there = A, B
                    dist = HALF // 2
                    while dist >= GROUP:
                        chain.link(compare(dve, here[:, :], there[:, :], HALF, dist))
                        here, there = there, here
                        dist //= 2
                    by_group = here[:, :].rearrange("p (c g) -> p c g", g=GROUP)
                    dve.tensor_reduce(gmin[:, :], by_group, AX.X, ALU.min)
                    chain.link(dve.tensor_reduce(gsum[:, :], by_group, AX.X, ALU.add))
                    before, LINKS = chain.n, 3
                    with dve.Fori(0, BITS) as k:
                        c = Chain(dve, chained, before + LINKS * k)
                        c.link(dve.tensor_tensor(cand[:, :], cur[:, :], bit[:, :], ALU.bitwise_or))
                        dve.tensor_scalar(eq[:, :], gsum[:, :], cand[:, :].bitcast(F32), None, ALU.is_ge, ALU.add,
                                          accum_out=count[:, 0:1]).then_inc(counted, 1)
                        dve.wait_ge(total_ready, k + 1)
                        c.link(dve.tensor_scalar(flag[:, :], psC[:, 0:1], float(BUDGET), -1.0, ALU.is_ge, ALU.mult))
                        dve.scalar_tensor_tensor(cur[:, :], flag[:, :], bit[:, 0:1], cur[:, :], ALU.bitwise_and, ALU.bitwise_or)
                        c.link(dve.tensor_scalar(bit[:, :], bit[:, :], 1, None, ALU.logical_shift_right))
                        assert c.n == LINKS
                    chain.n = before + LINKS * BITS
                    tau = cur[:, :].bitcast(F32)
                    dve.tensor_scalar(sel[:, :], gsum[:, :], tau, None, ALU.is_gt, ALU.add, accum_out=cols[:, 0:1])
                    dve.tensor_scalar(eq[:, :], gsum[:, :], tau, None, ALU.is_equal, ALU.add, accum_out=cols[:, 1:2]).then_inc(asked, 1)
                    dve.wait_ge(answered, 1)
                    dve.tensor_scalar(cols[:, 2:3], psR[:, 0:1], -1.0, float(BUDGET), ALU.mult, ALU.add)
                    chain.link(dve.tensor_copy(excl[:, :], psR[:, 64:64 + NG]))
                    chain.link(dve.tensor_tensor_scan(rank[:, :], ones[:, 0:NG], excl[:, :], 0.0, ALU.mult, ALU.add))
                    chain.link(dve.tensor_tensor(rank[:, :], rank[:, :], excl[:, :], ALU.subtract))
                    chain.link(dve.tensor_tensor(rank[:, :], rank[:, :], psR[:, 128:128 + NG], ALU.add))
                    chain.link(dve.tensor_scalar(rank[:, :], rank[:, :], psR[:, 1:2], None, ALU.add))
                    chain.link(dve.tensor_scalar(rank[:, :], rank[:, :], cols[:, 2:3], None, ALU.is_lt))
                    chain.link(dve.tensor_tensor(rank[:, :], rank[:, :], eq[:, :], ALU.mult))
                    chain.link(dve.tensor_tensor(sel[:, :], sel[:, :], rank[:, :], ALU.add))
                    dve.tensor_reduce(cols[:, 3:4], sel[:, :], AX.X, ALU.add)
                    dve.tensor_scalar(eq[:, :], sel[:, :], -2.0, 2.0, ALU.mult, ALU.add)
                    chain.link(dve.tensor_tensor(gmin[:, :], gmin[:, :], sel[:, :], ALU.mult))
                    chain.link(dve.tensor_tensor(gmin[:, :], gmin[:, :], eq[:, :], ALU.add))
                    dve.tensor_reduce(cols[:, 4:5], gmin[:, :], AX.X, ALU.min).then_inc(asked, 1)
                    dve.wait_ge(answered, 2)
                    dve.tensor_scalar(cols[:, 5:6], psR[:, 2:3], float(GROUP), None, ALU.mult)
                    chain.link(dve.tensor_tensor(cols[:, 6:7], psR[:, 3:4], cols[:, 4:5], ALU.min))
                    chain.link(dve.tensor_scalar(A[:, :], V[:, :], cols[:, 6:7], None, ALU.is_gt, ALU.add, accum_out=count[:, 0:1]))
                    dve.tensor_scalar(B[:, :], V[:, :], cols[:, 6:7], None, ALU.is_equal, ALU.add, accum_out=count[:, 1:2]).then_inc(asked, 1)
                    dve.wait_ge(answered, 3)
                    chain.link(dve.tensor_tensor(cols[:, 7:8], cols[:, 5:6], psR[:, 4:5], ALU.subtract))
                    chain.link(dve.tensor_tensor(cols[:, 7:8], cols[:, 7:8], psR[:, 5:6], ALU.subtract))
                    T = S[:, :, :].rearrange("p n e -> p (n e)")
                    chain.link(dve.tensor_tensor_scan(T, ones[:, :], B[:, :], 0.0, ALU.mult, ALU.add))
                    chain.link(dve.scalar_tensor_tensor(B[:, :], T, cols[:, 7:8], B[:, :], ALU.is_le, ALU.mult))
                    chain.link(dve.tensor_tensor(A[:, :], A[:, :], B[:, :], ALU.add))
                    dve.tensor_tensor(V[:, :], V[:, :], A[:, :], ALU.mult).then_inc(kept, 1)
                    dve.wait_ge(summed, 1)
                    chain.link(dve.tensor_scalar(A[:, :], psV[:, :, :].rearrange("p a b -> p (a b)"), 1e-6, None, ALU.add))
                    chain.link(dve.reciprocal(A[:, :], A[:, :]))
                    chain.link(dve.tensor_tensor(V[:, :], V[:, :], A[:, :], ALU.mult))

                @block.tensor
                def _(pe):
                    pe.wait_ge(s_ready, 1)
                    for i in range(NT // 2):
                        last = pe.transpose(psV[:, i // 4, i % 4 * P:i % 4 * P + P], B[:, i * P:i * P + P], m.ident[:, :])
                    last.then_inc(turned, 1)
                    with pe.Fori(0, BITS) as k:
                        pe.wait_ge(counted, k + 1)
                        pe.matmul(psC[:, 0:1], mats[:, ALL, :], count[:, 0:1], start=True, stop=True).then_inc(total_ready, 1)
                    pe.wait_ge(asked, 1)
                    pe.matmul(psR[:, 0:1], mats[:, ALL, :], cols[:, 0:1], start=True, stop=True)
                    pe.matmul(psR[:, 1:2], mats[:, LOW_UP, :], cols[:, 1:2], start=True, stop=True)
                    pe.matmul(psR[:, 64:64 + NG], mats[:, SAME_HALF, :], eq[:, :], start=True, stop=True)
                    pe.matmul(psR[:, 128:128 + NG], mats[:, EARLIER, :], eq[:, :], start=True, stop=True).then_inc(answered, 1)
                    pe.wait_ge(asked, 2)
                    pe.matmul(psR[:, 2:3], mats[:, SAME_EXP, :], cols[:, 3:4], start=True, stop=True)
                    pe.matmul(psR[:, 3:4], mats[:, SWAP, :], cols[:, 4:5], start=True, stop=True).then_inc(answered, 1)
                    pe.wait_ge(asked, 3)
                    pe.matmul(psR[:, 4:5], mats[:, SAME_EXP, :], count[:, 0:1], start=True, stop=True)
                    pe.matmul(psR[:, 5:6], mats[:, LOW_UP_EXP, :], count[:, 1:2], start=True, stop=True).then_inc(answered, 1)
                    pe.wait_ge(kept, 1)
                    for b in range(4):
                        last = pe.matmul(psV[:, b, :], mats[:, SAME_HALF, :], V[:, 512 * b:512 * b + 512], start=True, stop=True)
                    last.then_inc(summed, 1)

        m.part = "gf"
        with ExitStack() as second:
            fst = sb("fst", [P, 512], on=second)
            su, tg, h = sb("su", [P, 2, 512], on=second), sb("tg", [P, 2, 512], on=second), sb("h", [P, 2, 512], on=second)
            psU, psG, psF = (pb(n, [P, 2, 512], on=second) for n in ("psU", "psG", "psF"))
            psY = pb("psY", [P, 4, D], on=second)
            staged, up_ready, silued, gated, h_ready, down_done, x_added = (m.sem(n) for n in (
                "staged", "up_ready", "silued", "gated", "h_ready", "down_done", "x_added"))
            G = NT // 4

            def groups(eng, body):
                for hf in range(2):
                    with eng.Fori(0, G // 2) as k:
                        body(k + hf * (G // 2), k, hf)

            with nc.Block() as block:
                @block.scalar
                def _(act):
                    def group(g, k, hf):
                        for n in range(C):
                            q = C * g + n
                            act.wait_ge(up_ready, q + 1)
                            act.wait_ge(gated, q - 1 if n > 0 else q)
                            act.activation(su[:, n % 2, :], psU[:, n % 2, :], ACT.Silu, bias=bu[:, n:n + 1]).then_inc(silued, 1)
                    groups(act, group)

                @block.vector
                def _(dve):
                    def group(g, k, hf):
                        dve.wait_ge(down_done, (C + 1) * g)
                        dve.tensor_scalar(fst[:, :], V[:, bass.ds(512 * k, 512)], 1.0, None, ALU.mult).then_inc(staged, 1)
                        for n in range(C):
                            q = C * g + n
                            dve.wait_ge(silued, q + 1)
                            dve.scalar_tensor_tensor(tg[:, n % 2, :], psG[:, n % 2, :], bg[:, n:n + 1], su[:, n % 2, :],
                                                     ALU.add, ALU.mult).then_inc(gated, 1)
                            dve.wait_ge(gated, q + 1)
                            dve.wait_ge(down_done, (C + 1) * g + n)
                            dve.tensor_tensor(h[:, n % 2, :], psF[:, n % 2, :], tg[:, n % 2, :], ALU.mult).then_inc(h_ready, 1)
                        dve.wait_ge(down_done, (C + 1) * g + C + 1)
                        tiles = m.X[:, bass.ds(4 * g, 4), :]
                        dve.tensor_tensor(tiles, tiles, psY[:, :, :], ALU.add).then_inc(x_added, 1)
                    groups(dve, group)

                @block.tensor
                def _(pe):
                    def group(g, k, hf):
                        def down(n):
                            pe.wait_ge(h_ready, C * g + n + 1)
                            for j in range(4):
                                last = pe.matmul(psY[:, j, :], h[:, n % 2, j * P:j * P + P], wd[:, n, :],
                                                 start=False, stop=(n == C - 1), skip_group_check=True)
                            last.then_inc(down_done, 1)

                        pe.wait_ge(staged, g + 1)
                        pe.wait_ge(x_added, g)
                        rows = slice(EXP2 * hf, EXP2 * hf + EXP2)
                        for j in range(4):
                            last = pe.matmul(psY[:, j, :], fst[rows, j * P:j * P + P], bd[rows, :],
                                             start=(j == 0), stop=False, skip_group_check=True)
                        last.then_inc(down_done, 1)
                        x = m.xT[:, bass.ds(512 * g, 512)]
                        for n in range(C):
                            q = C * g + n
                            pe.wait_ge(h_ready, q - 1 if n > 0 else q)
                            pe.matmul(psU[:, n % 2, :], wu[:, EC * n:EC * n + EC, :].rearrange("p e h -> p (e h)"), x, start=True, stop=True)
                            pe.matmul(psG[:, n % 2, :], wg[:, EC * n:EC * n + EC, :].rearrange("p e h -> p (e h)"), x, start=True, stop=True)
                            e = EXP2 * hf + EC * n
                            pe.matmul(psF[:, n % 2, :], pick[:, e:e + EC, :].rearrange("p e h -> p (e h)"), fst[:, :], start=True, stop=True).then_inc(up_ready, 1)
                            if n > 0:
                                down(n - 1)
                        down(C - 1)
                    groups(pe, group)


HID3, EXP3 = 64, 64
GROUPS3, TOP_GROUPS = 8, 4
TOP3, CAP = 8, 128
OUT_SCALE = 2.5
ROW = D + EXP3
ACCS = 4
FAR = -1e30


def capacity_ffn(nc, m, t):
    GE = EXP3 // GROUPS3
    rows = nc.dram_tensor("cap_rows", (TOK + P, ROW), F32, kind="Internal").ap()
    counts = nc.dram_tensor("cap_counts", (EXP3 * NT, P), F32, kind="Internal").ap()
    accs = [nc.dram_tensor(f"cap_acc{n}", (TOK + P, D), F32, kind="Internal").ap() for n in range(ACCS)]
    tiles_of = lambda table: table[0:TOK, :].rearrange("(n p) d -> n p d", p=P)
    with ExitStack() as own:
        def sb(name, shape, dt=F32, on=own):
            return on.enter_context(nc.sbuf_tensor(f"cap_{name}", shape, dt))

        def pb(name, shape, dt=F32, on=own):
            return on.enter_context(nc.psum_tensor(f"cap_{name}", shape, dt))

        row0 = sb("row0", [P, EXP3])
        slot = sb("slot", [P, 1])
        base = sb("base", [P, EXP3])
        row_of = sb("row_of", [P, EXP3], I32)
        with ExitStack() as first:
            L = sb("L", [P, NT, EXP3], on=first)
            layer_norm(nc, m, "ln7", router=(t["gate_wT"], L), rows=tiles_of(rows)[:, :, 0:D])
            m.part = "cap"
            F = sb("F", [P, NT, EXP3], on=first)
            bias, tri = sb("bias", [P, EXP3], on=first), sb("tri", [P, GROUPS3, GROUPS3], on=first)
            hi, lo, a = (sb(n, [P, NT, GROUPS3, GE // 2], on=first) for n in ("hi", "lo", "a"))
            gt, eq = (sb(n, [P, NT, GROUPS3, GROUPS3], on=first) for n in ("gt", "eq"))
            score, pen = sb("score", [P, NT, GROUPS3], on=first), sb("pen", [P, NT, GROUPS3], on=first)
            st, rp, t8 = sb("st", [P, 4, EXP3], on=first), sb("rp", [P, 4, EXP3], on=first), sb("t8", [P, 4, 8], on=first)
            M = sb("M", [P, EXP3, NT], on=first)
            fresh = sb("fresh", [P, EXP3, NT], on=first)
            inc = sb("inc", [P, EXP3, NT], on=first)
            Mb, incb, excb = (sb(n, [P, EXP3, NT], BF16, on=first) for n in ("Mb", "incb", "excb"))
            upto, onesb = sb("upto", [P, P], on=first), sb("onesb", [P, P], BF16, on=first)
            uptob = sb("uptob", [P, P], BF16, on=first)
            total, spare = sb("total", [P, NT], on=first), sb("spare", [P, 1], on=first)
            zero = sb("zero", [P, (NT + 1) * D], on=first)
            cT = sb("cT", [P, EXP3 * NT // P, P], on=first)
            psC, psE = pb("psC", [P, 4, 512], on=first), pb("psE", [P, 4, 512], on=first)
            loaded, zeroed, chained, sigmoided, w_ready, w_out, z_out = (m.sem(n) for n in (
                "loaded", "zeroed", "chained", "sigmoided", "w_ready", "w_out", "z_out"))
            bits_ready, counted, ends_ready, inc_ready, inc_turned, inc_taken, c_out = (m.sem(n) for n in (
                "bits_ready", "counted", "ends_ready", "inc_ready", "inc_turned", "inc_taken", "c_out"))

            with nc.Block() as block:
                @block.sync
                def _(sp):
                    sp.dma_start(bias[:, :], t["L3_ffn_gate_bias"].partition_broadcast(P)).then_inc(loaded, 16)
                    sp.dma_start(tri[:, :, :], t["c_tri8"].partition_broadcast(P)).then_inc(loaded, 16)
                    sp.dma_start(slot[:, :], t["c_slot"]).then_inc(loaded, 16)
                    sp.dma_start(upto[:, :], t["c_upto"]).then_inc(loaded, 16)
                    sp.dma_start(row0[:, :], t["c_row0"].partition_broadcast(P)).then_inc(loaded, 16)
                    sp.wait_ge(zeroed, 1)
                    for acc in accs:
                        sp.dma_start(acc.rearrange("(n p) d -> p n d", p=P), zero[:, :].rearrange("p (n d) -> p n d", d=D)).then_inc(z_out, 16)
                    sp.dma_start(rows[TOK:TOK + P, :], zero[:, 0:ROW]).then_inc(z_out, 16)
                    sp.wait_ge(w_ready, 1)
                    sp.dma_start(tiles_of(rows)[:, :, D:ROW].rearrange("n p e -> p n e"), L[:, :, :]).then_inc(w_out, 16)
                    for half in range(2):
                        sp.wait_ge(inc_taken, half + 1)
                        b = slice(8 * half, 8 * half + 8)
                        sp.dma_start(counts.rearrange("(b q) p -> q b p", q=P)[:, b, :], cT[:, b, :]).then_inc(c_out, 16)
                    sp.wait_ge(z_out, 16 * (ACCS + 1))
                    sp.wait_ge(w_out, 16)
                    sp.wait_ge(c_out, 32)

                @block.gpsimd
                def _(pool):
                    pool.memset(zero[:, :], 0.0).then_inc(zeroed, 1)

                @block.scalar
                def _(act):
                    act.activation(L[:, :, :], L[:, :, :], ACT.Sigmoid).then_inc(sigmoided, 1)
                    for half in range(2):
                        act.wait_ge(inc_turned, half + 1)
                        act.activation(cT[:, 8 * half:8 * half + 8, :], psE[:, 2 * half:2 * half + 2, :].rearrange("p a (b q) -> p (a b) q", q=P),
                                       ACT.Copy).then_inc(inc_taken, 1)

                @block.vector
                def _(dve):
                    chain = Chain(dve, chained)
                    dve.memset(fresh[:, :, :], 1.0)
                    chain.link(dve.memset(onesb[:, :], 1.0))
                    dve.memset(fresh[:, :, 0:1], 0.0)
                    dve.wait_ge(loaded, 80)
                    dve.tensor_copy(uptob[:, :], upto[:, :])
                    dve.wait_ge(sigmoided, 1)
                    chain.link(dve.tensor_tensor(F[:, :, :], L[:, :, :], bias[:, :].unsqueeze(1).broadcast_to([P, NT, EXP3]), ALU.add))
                    by_group = F[:, :, :].rearrange("p n (g e) -> p n g e", e=GE)
                    w = GE // 2
                    dve.tensor_tensor(hi[:, :, :, :], by_group[:, :, :, 0:w], by_group[:, :, :, w:GE], ALU.max)
                    chain.link(dve.tensor_tensor(lo[:, :, :, :], by_group[:, :, :, 0:w], by_group[:, :, :, w:GE], ALU.min))
                    while w > 1:
                        v = w // 2
                        chain.link(dve.tensor_tensor(a[:, :, :, 0:v], hi[:, :, :, 0:v], hi[:, :, :, v:w], ALU.min))
                        dve.tensor_tensor(a[:, :, :, v:w], lo[:, :, :, 0:v], lo[:, :, :, v:w], ALU.max)
                        chain.link(dve.tensor_tensor(hi[:, :, :, 0:v], hi[:, :, :, 0:v], hi[:, :, :, v:w], ALU.max))
                        chain.link(dve.tensor_tensor(lo[:, :, :, 0:v], a[:, :, :, 0:v], a[:, :, :, v:w], ALU.max))
                        w = v
                    chain.link(dve.tensor_tensor(score[:, :, :], hi[:, :, :, 0], lo[:, :, :, 0], ALU.add))
                    full = [P, NT, GROUPS3, GROUPS3]
                    own_score = score[:, :, :].unsqueeze(3).broadcast_to(full)
                    others = score[:, :, :].unsqueeze(2).broadcast_to(full)
                    dve.tensor_tensor(gt[:, :, :, :], others, own_score, ALU.is_gt)
                    chain.link(dve.tensor_tensor(eq[:, :, :, :], others, own_score, ALU.is_equal))
                    eqf = eq[:, :, :, :].rearrange("p n g h -> p n (g h)")
                    earlier = tri[:, :, :].rearrange("p g h -> p (g h)").unsqueeze(1).broadcast_to([P, NT, GROUPS3 * GROUPS3])
                    chain.link(dve.tensor_tensor(eqf, eqf, earlier, ALU.mult))
                    chain.link(dve.tensor_tensor(gt[:, :, :, :], gt[:, :, :, :], eq[:, :, :, :], ALU.add))
                    chain.link(dve.tensor_reduce(score[:, :, :], gt[:, :, :, :], AX.X, ALU.add))
                    chain.link(dve.tensor_scalar(pen[:, :, :], score[:, :, :], float(TOP_GROUPS), FAR, ALU.is_ge, ALU.mult))
                    before, LINKS = chain.n, 4
                    with dve.Fori(0, NT // 4) as k:
                        c = Chain(dve, chained, before + LINKS * k)
                        c.link(dve.tensor_tensor(st[:, :, :].rearrange("p j (g e) -> p j g e", e=GE),
                                                 F[:, bass.ds(4 * k, 4), :].rearrange("p j (g e) -> p j g e", e=GE),
                                                 pen[:, bass.ds(4 * k, 4), :].unsqueeze(3).broadcast_to([P, 4, GROUPS3, GE]), ALU.add))
                        dve.memset(spare[:, :], 0.0)
                        for j in range(4):
                            last = dve.max(t8[:, j, :], st[:, j, :])
                        c.link(last)
                        dve.memset(spare[:, :], 0.0)
                        for j in range(4):
                            last = dve.match_replace(rp[:, j, :], t8[:, j, :], st[:, j, :], 3 * FAR)
                        c.link(last)
                        c.link(dve.tensor_tensor(M[:, :, bass.ds(4 * k, 4)].rearrange("p e j -> p j e"), rp[:, :, :], st[:, :, :], ALU.not_equal))
                    chain.n = before + LINKS * (NT // 4)
                    dve.tensor_copy(Mb[:, :, :], M[:, :, :])
                    flat = lambda v: v[:, :, :].rearrange("p e n -> p (e n)")
                    chain.link(dve.tensor_tensor_scan(flat(inc), flat(fresh), flat(M), 0.0, ALU.mult, ALU.add))
                    dve.tensor_copy(incb[:, :, :], inc[:, :, :])
                    dve.tensor_tensor(excb[:, :, :], inc[:, :, :], M[:, :, :], ALU.subtract).then_inc(bits_ready, 1)
                    Mt = M[:, :, :].rearrange("p e n -> p n e")
                    chain.link(dve.tensor_tensor(L[:, :, :], L[:, :, :], Mt, ALU.mult))
                    chain.link(dve.tensor_reduce(total[:, :], L[:, :, :], AX.X, ALU.add))
                    chain.link(dve.tensor_scalar(total[:, :], total[:, :], 1e-20, None, ALU.add))
                    chain.link(dve.reciprocal(total[:, :], total[:, :]))
                    chain.link(dve.tensor_scalar(total[:, :], total[:, :], OUT_SCALE, None, ALU.mult))
                    dve.tensor_tensor(L[:, :, :], L[:, :, :], total[:, :].unsqueeze(2).broadcast_to([P, NT, EXP3]), ALU.mult).then_inc(w_ready, 1)
                    dve.wait_ge(counted, 1)
                    dve.tensor_copy(flat(inc), psC[:, :, :].rearrange("p a b -> p (a b)")).then_inc(inc_ready, 1)
                    dve.wait_ge(ends_ready, 1)
                    flatF = F[:, :, :].rearrange("p n e -> p (n e)")
                    dve.tensor_scalar(flatF, psE[:, :, :].rearrange("p a b -> p (a b)"), slot[:, 0:1], None, ALU.is_le).then_inc(inc_ready, 1)
                    dve.wait_ge(inc_ready, 2)
                    chain.link(dve.tensor_reduce(base[:, :], flatF.rearrange("p (e n) -> p e n", n=NT), AX.X, ALU.add))
                    chain.link(dve.tensor_scalar(base[:, :], base[:, :], float(NT - 1), None, ALU.min))
                    chain.link(dve.tensor_tensor(row_of[:, :], base[:, :], row0[:, :], ALU.add))
                    chain.link(dve.tensor_scalar(base[:, :], base[:, :], float(P), None, ALU.mult))

                @block.tensor
                def _(pe):
                    pe.wait_ge(bits_ready, 1)
                    fl = lambda v: v[:, :, :].rearrange("p e n -> p (e n)")
                    for b in range(4):
                        cols = slice(512 * b, 512 * b + 512)
                        pe.matmul(psC[:, b, :], uptob[:, :], fl(Mb)[:, cols], start=True, stop=False)
                        last = pe.matmul(psC[:, b, :], onesb[:, :], fl(excb)[:, cols], start=False, stop=True)
                    last.then_inc(counted, 1)
                    for b in range(4):
                        last = pe.matmul(psE[:, b, :], onesb[:, :], fl(incb)[:, 512 * b:512 * b + 512], start=True, stop=True)
                    last.then_inc(ends_ready, 1)
                    pe.wait_ge(inc_ready, 2)
                    for b in range(EXP3 * NT // P):
                        last = pe.transpose(psE[:, b // 4, b % 4 * P:b % 4 * P + P], fl(inc)[:, b * P:b * P + P], m.ident[:, :])
                        if b % 8 == 7:
                            last.then_inc(inc_turned, 1)

        m.part = "capx"
        with ExitStack() as second:
            GI, GX = sb("GI", [P, 4, P], on=second), sb("GX", [P, 4, ROW], on=second)
            idx1, idx2 = sb("idx1", [P, 8], I32, on=second), sb("idx2", [P, 8], I32, on=second)
            spare, nought = sb("spare2", [P, 3], on=second), sb("nought", [P, 1], on=second)
            le, cnt, tok, past = sb("le", [P, P], on=second), sb("cnt", [P, 1], on=second), sb("tok", [P, 1], on=second), sb("past", [P, 1], on=second)
            wgu, wdn = sb("wgu", [P, 4, 2, HID3], on=second), sb("wdn", [HID3, 4, D], on=second)
            GT, sg, h = sb("GT", [P, 2, P], on=second), sb("sg", [HID3, 2, P], on=second), sb("h", [HID3, 2, P], on=second)
            Y = sb("Y", [P, 4, D], on=second)
            psT, psU, psY = pb("psT", [P, 2, 512], on=second), pb("psU", [P, 2, 512], on=second), pb("psY", [P, 2, 512], on=second)
            asked, found, chained, turned, gt_ready, up_ready, silued, h_ready, down_ready, y_ready = (m.sem(n) for n in (
                "asked", "found", "chained", "turned", "gt_ready", "up_ready", "silued", "h_ready", "down_ready", "y_ready"))
            cleared, carried = m.sem("cleared"), [m.sem(f"carried{k}") for k in range(3)]
            gi_in, gx_in, w_in, added = ([m.sem(f"{n}{u}") for u in range(4)] for n in ("gi_in", "gx_in", "w_in", "added"))
            turn_of = lambda s, n: 2 * n + s // 4
            run = lambda eng, stages: pipelined(eng, EXP3, stages, period=8)

            with nc.Block() as block:
                @block.sync
                def _(sp):
                    def weights(e, s, n):
                        q = s % 4
                        wait_past(sp, down_ready, e - 3)
                        sp.dma_start(wgu[:, q, 0, :], t["L3_ffn_w_gate"][bass.ds(e, 1), :, :].rearrange("a d i -> (a d) i")).then_inc(w_in[q], 16)
                        sp.dma_start(wgu[:, q, 1, :], t["L3_ffn_w_up"][bass.ds(e, 1), :, :].rearrange("a d i -> (a d) i")).then_inc(w_in[q], 16)
                        sp.dma_start(wdn[:, q, :], t["L3_ffn_w_down"][bass.ds(e, 1), :, :].rearrange("a i d -> (a i) d")).then_inc(w_in[q], 16)
                    run(sp, [(0, weights)])

                @block.gpsimd
                def _(pool):
                    def carry(k, e):
                        wait_past(pool, carried[k], e)
                        pool.tensor_tensor(spare[:, k:k + 1], nought[:, :], nought[:, :], ALU.add).then_inc(carried[k], 1)

                    def gather_counts(e, s, n):
                        pool.wait_ge(asked, e + 1)
                        wait_past(pool, found, e - 3)
                        carry(0, e)
                        pool.indirect_dma_start(GI[:, s % 4, :], None, counts, bass.IndirectOffsetOnAxis(ap=idx1[:, s:s + 1], axis=0)).then_inc(gi_in[s % 4], 16)

                    def gather_rows(e, s, n):
                        pool.wait_ge(found, e + 1)
                        wait_past(pool, y_ready, e - 3)
                        carry(1, e)
                        pool.indirect_dma_start(GX[:, s % 4, :], None, rows, bass.IndirectOffsetOnAxis(ap=idx2[:, s:s + 1], axis=0)).then_inc(gx_in[s % 4], 16)

                    def add(e, s, n):
                        pool.wait_ge(y_ready, e + 1)
                        wait_past(pool, added[s % 4], 16 * turn_of(s, n))
                        carry(2, e)
                        pool.indirect_dma_start(accs[s % 4], bass.IndirectOffsetOnAxis(ap=idx2[:, s:s + 1], axis=0), Y[:, s % 4, :], None,
                                                compute_op=ALU.add).then_inc(added[s % 4], 16)

                    pool.memset(nought[:, :], 0.0).then_inc(cleared, 1)
                    pool.wait_ge(cleared, 1)
                    run(pool, [(6, gather_counts), (3, gather_rows), (-1, add)])
                    for s in range(4):
                        pool.wait_ge(added[s], 16 * EXP3 // 4)

                @block.vector
                def _(dve):
                    def ask(e, s, n):
                        wait_past(dve, found, e - 7)
                        dve.tensor_scalar(idx1[:, s:s + 1], row_of[:, bass.ds(e, 1)], 0, None, ALU.add).then_inc(asked, 1)

                    def find(e, s, n):
                        dve.wait_ge(gi_in[s % 4], 16 * turn_of(s, n) + 16)
                        wait_past(dve, added[s % 4], 16 * (turn_of(s, n) - 1))
                        wait_past(dve, found, e)
                        c = Chain(dve, chained, 3 * e)
                        c.link(dve.tensor_scalar(le[:, :], GI[:, s % 4, :], slot[:, 0:1], None, ALU.is_le, ALU.add, accum_out=cnt[:, :]))
                        c.link(dve.tensor_tensor(tok[:, :], cnt[:, :], base[:, bass.ds(e, 1)], ALU.add))
                        c.link(dve.scalar_tensor_tensor(past[:, :], tok[:, :], float(TOK), slot[:, :], ALU.is_ge, ALU.mult))
                        dve.tensor_tensor(idx2[:, s:s + 1], tok[:, :], past[:, :], ALU.add).then_inc(found, 1)

                    def product(e, s, n):
                        u = s % 2
                        dve.wait_ge(silued, e + 1)
                        wait_past(dve, down_ready, e - 1)
                        dve.tensor_tensor(h[:, u, :], psU[0:HID3, u, P:2 * P], sg[:, u, :], ALU.mult).then_inc(h_ready, 1)

                    run(dve, [(6, ask), (3, find), (0, product)])

                @block.scalar
                def _(act):
                    def take(e, s, n):
                        act.wait_ge(turned, e + 1)
                        wait_past(act, up_ready, e - 1)
                        act.activation(GT[:, s % 2, :], psT[:, s % 2, 0:P], ACT.Copy).then_inc(gt_ready, 1)

                    def silu(e, s, n):
                        act.wait_ge(up_ready, e + 1)
                        wait_past(act, h_ready, e - 1)
                        act.activation(sg[:, s % 2, :], psU[0:HID3, s % 2, 0:P], ACT.Silu).then_inc(silued, 1)

                    def weigh(e, s, n):
                        act.wait_ge(down_ready, e + 1)
                        wait_past(act, added[s % 4], 16 * turn_of(s, n))
                        act.activation(Y[:, s % 4, :], psY[:, s % 2, 0:D], ACT.Copy, scale=GX[:, s % 4, bass.ds(D + e, 1)]).then_inc(y_ready, 1)

                    run(act, [(1, take), (0, silu), (-1, weigh)])

                @block.tensor
                def _(pe):
                    def turn(e, s, n):
                        pe.wait_ge(gx_in[s % 4], 16 * turn_of(s, n) + 16)
                        wait_past(pe, gt_ready, e - 1)
                        pe.transpose(psT[:, s % 2, 0:P], GX[:, s % 4, 0:D], m.ident[:, :]).then_inc(turned, 1)

                    def up(e, s, n):
                        pe.wait_ge(gt_ready, e + 1)
                        pe.wait_ge(w_in[s % 4], 48 * turn_of(s, n) + 48)
                        wait_past(pe, h_ready, e - 1)
                        pe.matmul(psU[0:HID3, s % 2, 0:P], wgu[:, s % 4, 0, :], GT[:, s % 2, :], start=True, stop=True)
                        pe.matmul(psU[0:HID3, s % 2, P:2 * P], wgu[:, s % 4, 1, :], GT[:, s % 2, :], start=True, stop=True).then_inc(up_ready, 1)

                    def down(e, s, n):
                        pe.wait_ge(h_ready, e + 1)
                        wait_past(pe, y_ready, e - 1)
                        pe.matmul(psY[:, s % 2, 0:D], h[:, s % 2, :], wdn[:, s % 4, :], start=True, stop=True).then_inc(down_ready, 1)

                    run(pe, [(1, turn), (0, up), (-1, down)])

        m.part = "capy"
        with ExitStack() as third:
            S = sb("sums", [P, ACCS, NT, D], on=third)
            in_ = [m.sem(f"in{n}") for n in range(ACCS)]
            x_added = m.sem("x_added")
            with nc.Block() as block:
                @block.sync
                def _(sp):
                    for n in range(ACCS):
                        sp.dma_start(S[:, n, :, :], tiles_of(accs[n]).rearrange("n p d -> p n d")).then_inc(in_[n], 16)

                @block.vector
                def _(dve):
                    for n in range(ACCS):
                        dve.wait_ge(in_[n], 16)
                        if n:
                            dve.wait_ge(x_added, n)
                        dve.tensor_tensor(m.X[:, :, :], m.X[:, :, :], S[:, n, :, :], ALU.add).then_inc(x_added, 1)


def program(nc, t, first=0, last=8):
    with ExitStack() as stack:
        m = Memory(nc, stack)
        load_all(nc, m, t)
        for part in range(first, last):
            if part == 0:
                layer_norm(nc, m, "ln0")
                with nc.sbuf_tensor("kept_Oall", [P, NT, D], F32) as Oall:
                    attention(nc, m, "at0", t["L0_xattn_W_q"], t["L0_xattn_W_k"], t["L0_xattn_W_v"], t["L0_xattn_W_o"],
                              add_mask=t["mask_Bx16xSxS2_ff0"], Oall=Oall,
                              lams=[t["L0_xattn_lambda_" + n] for n in ("q1", "k1", "q2", "k2")])
                    differential_out(nc, m, "do0", Oall, t["L0_xattn_W_o"], t["rms_scale_col"])
            if part == 2:
                layer_norm(nc, m, "ln2")
                attention(nc, m, "at1", *(t["L1_xattn_" + n] for n in ("wq", "wk", "wv", "wo", "bq", "bk", "bv", "bo")),
                          keep_mask=t["mask_1x1xSxS2_ik1"])
            if part == 4:
                layer_norm(nc, m, "ln4")
                attention(nc, m, "at2", *(t["L2_xattn_" + n] for n in ("WqT", "WkT", "WvT", "WoT", "Wq_b", "Wk_b", "Wv_b", "Wo_b")))
            if part == 6:
                layer_norm(nc, m, "ln6")
                attention(nc, m, "at3", *(t["L3_xattn_" + n] for n in ("Wq", "Wk", "Wv", "Wo", "bq", "bk", "bv", "bo")))
            if part == 1:
                bit_ffn(nc, m, t)
            if part == 3:
                expert_ffn(nc, m, t)
            if part == 5:
                grouped_ffn(nc, m, t)
            if part == 7:
                capacity_ffn(nc, m, t)
            m.free_sems()
        store_all(nc, m, t)


def lay_out(inputs):
    import numpy as np

    t = {k: np.asarray(v) for k, v in inputs.items() if k != "itok_BxS2_0_2047"}
    t["ctxT"] = np.ascontiguousarray(t.pop("ctx_1024").reshape(TOK, D).T)
    for n in "qkvo":
        t[f"L2_xattn_W{n}T"] = np.ascontiguousarray(t.pop(f"L2_xattn_W{n}_w").T)
    t["rms_scale_col"] = np.ascontiguousarray(np.tile(t.pop("L0_xattn_rms_scale"), HEADS).reshape(P, 1))
    t["c_ident"] = np.eye(P, dtype=np.float32)
    t["c_order"] = np.arange(EXP1, 0, -1).astype(np.float32)
    t["bup_cols"] = np.ascontiguousarray(t.pop("L2_ffn_bup").reshape(-1, P).T)
    t["bgate_cols"] = np.ascontiguousarray(t.pop("L2_ffn_bgate").reshape(-1, P).T)
    p = np.arange(P)
    half, exp = p // EXP2, p % EXP2
    pairs = [np.ones((P, P), bool), half[:, None] == half, exp[:, None] == exp, half[:, None] < half,
             (half[:, None] == half) & (exp[:, None] < exp), (half[:, None] != half) & (exp[:, None] == exp),
             (half[:, None] < half) & (exp[:, None] == exp)]
    t["c_mats"] = np.ascontiguousarray(np.stack(pairs, 1).astype(np.float32))
    t["c_sign"] = (1.0 - 2.0 * half[:, None]).astype(np.float32)
    t["c_head_mask"] = np.stack([p // DH % 2 == 0, p // DH % 2 == 1, p // DH % 4 < 2, p // DH % 4 > 1], 1).astype(np.float32)
    t["c_fold"] = (p[:, None] % SEQ == np.arange(SEQ)).astype(np.float32)
    t["gate_wT"] = np.ascontiguousarray(t.pop("L3_ffn_gate_w").T)
    g = np.arange(GROUPS3)
    t["c_tri8"] = (g[None, :] < g[:, None]).astype(np.float32)
    t["c_slot"] = p.astype(np.float32)[:, None]
    t["c_blocks"] = np.arange(BLOCKS).astype(np.float32)
    t["c_upto"] = (p[:, None] <= p[None, :]).astype(np.float32)
    t["c_row0"] = (NT * np.arange(EXP3)).astype(np.float32)
    return t


def kernel(**inputs):
    import concourse.bacc as bacc
    from concourse.bass_utils import run_bass_kernel_spmd

    nc = bacc.Bacc("TRN2", target_bir_lowering=False, num_devices=1)
    arrays = lay_out(inputs)
    t = {name: nc.dram_tensor(name, a.shape, mybir.dt.from_np(a.dtype), kind="ExternalInput").ap() for name, a in arrays.items()}
    t["out"] = nc.dram_tensor("out", (BATCH, SEQ, D), F32, kind="ExternalOutput").ap()
    program(nc, t)
    result = run_bass_kernel_spmd(nc, [arrays], core_ids=[0])
    return result.results[0]["out"]
```

```python
from contextlib import ExitStack

import concourse.bass as bass
from concourse import mybir

ALU = mybir.AluOpType
ACT = mybir.ActivationFunctionType
AX = mybir.AxisListType
F32 = mybir.dt.float32
BF16 = mybir.dt.bfloat16
I32 = mybir.dt.int32
U32 = mybir.dt.uint32

P = 128
BATCH, SEQ, D = 64, 64, 128
TOK = BATCH * SEQ
NT = TOK // P
HEADS, DH = 16, 8
EPS = 1e-5
QK_SCALE = DH ** -0.5
MAGIC = 1.5 * 2.0 ** 23


class Memory:

    def __init__(self, nc, stack):
        self.nc, self.stack, self.part, self.sems = nc, stack, "", []
        sb = self.kept
        self.X = sb("X", [P, NT, D], F32)
        self.ctxT = sb("ctxT", [P, TOK], F32)
        self.xT = sb("xT", [P, TOK], F32)
        self.ident = sb("ident", [P, P], F32)
        self.identb = sb("identb", [P, P], BF16)
        self.fold = sb("fold", [P, SEQ], F32)
        self.head_mask = sb("head_mask", [P, 4], F32)
        self.half_mask = sb("half_mask", [P, 2], F32)
        self.mean = sb("mean", [P, NT], F32)
        self.rstd = sb("rstd", [P, NT], F32)
        self.stats = sb("stats", [P, NT, 6], F32)

        self.ctx_in = stack.enter_context(nc.semaphore("ctx_in"))

    def kept(self, name, shape, dt):
        return self.stack.enter_context(self.nc.sbuf_tensor("kept_" + name, shape, dt))

    def sem(self, name):
        self.sems.append(self.nc.alloc_semaphore(name=f"{self.part}_{name}"))
        return self.sems[-1]

    def free_sems(self):
        self.nc.clear_and_free_semaphores(self.sems)
        self.nc.all_engine_barrier()
        self.sems = []


class Chain:

    def __init__(self, eng, sem, base=0):
        self.eng, self.sem, self.base, self.n = eng, sem, base, 0

    def link(self, instruction):
        self.n += 1
        instruction.then_inc(self.sem, 1)
        self.eng.wait_ge(self.sem, self.base + self.n)


def wait_past(eng, sem, value):
    if not isinstance(value, int) or value > 0:
        eng.wait_ge(sem, value)


def in_pairs(eng, first, end, step):
    assert first % 2 == 0 and end % 2 == 0
    with eng.Fori(0, (end - first) // 2) as k:
        for u in range(2):
            step(2 * k + (first + u), u, k + first // 2)


def peeled(eng, end, step):
    step(0, 0, 0)
    step(1, 1, 0)
    in_pairs(eng, 2, end, step)


def pipelined(eng, units, stages, period=2):
    stages = [(lead, stage, *(more or (0,))) for lead, stage, *more in stages]
    leads = [lead for lead, _, _ in stages]
    first = -(-(period - min(leads)) // period) * period
    end = (units - max(leads)) // period * period
    def plain(start, stop):
        for s in range(start, stop):
            for lead, stage, beyond in stages:
                if 0 <= s + lead < units + beyond:
                    stage(s + lead, (s + lead) % period, (s + lead) // period)

    if first >= end:
        plain(-max(leads), units - min(leads))
        return
    plain(-max(leads), first)
    with eng.Fori(0, (end - first) // period) as k:
        for s in range(first, first + period):
            for lead, stage, _ in stages:
                stage(period * k + (s + lead), (s + lead) % period, k + (s + lead) // period)
    plain(end, units - min(leads))


def load_all(nc, m, t):
    m.part = "load"
    loaded, built = m.sem("loaded"), m.sem("built")
    with nc.Block() as block:
        @block.sync
        def _(sp):
            x = t["x"].rearrange("(b e) s d -> (e s) b d", e=P // SEQ)
            sp.dma_start(m.X[:, 0:NT // 2, :], x[:, 0:NT // 2, :]).then_inc(loaded, 16)
            sp.dma_start(m.ctxT[:, :], t["ctxT"]).then_inc(m.ctx_in, 16)
            sp.wait_ge(loaded, 80)

        @block.scalar
        def _(act):
            x = t["x"].rearrange("(b e) s d -> (e s) b d", e=P // SEQ)
            act.dma_start(m.ident[:, :], t["c_ident"]).then_inc(loaded, 16)
            act.dma_start(m.X[:, NT // 2:NT, :], x[:, NT // 2:NT, :]).then_inc(loaded, 16)
            act.dma_start(m.head_mask[:, :], t["c_head_mask"]).then_inc(loaded, 16)
            act.dma_start(m.fold[:, :], t["c_fold"]).then_inc(loaded, 16)

        @block.vector
        def _(dve):
            for h in range(2):
                dve.memset(m.half_mask[64 * h:64 * h + 64, h:h + 1], 1.0).then_inc(built, 1)
                dve.memset(m.half_mask[64 * h:64 * h + 64, 1 - h:2 - h], 0.0).then_inc(built, 1)
            dve.wait_ge(loaded, 80)
            dve.tensor_copy(m.identb[:, :], m.ident[:, :]).then_inc(built, 1)
            dve.wait_ge(built, 5)


def layer_norm(nc, m, part, to_xT=True, router=None, rows=None, also=None, measured=True):
    m.part = part
    with ExitStack() as own:
        stats = m.stats
        a = own.enter_context(nc.sbuf_tensor(part + "a", [P, NT], F32))
        diff = own.enter_context(nc.sbuf_tensor(part + "diff", [P, NT], F32))
        var = own.enter_context(nc.sbuf_tensor(part + "var", [P, NT], F32))
        xh = own.enter_context(nc.sbuf_tensor(part + "xh", [P, 2, 4, D], F32))
        psT = own.enter_context(nc.psum_tensor(part + "psT", [P, 2, 512], F32))
        if router:
            wr, logits = router
            E = logits.shape[2]
            Wr = own.enter_context(nc.sbuf_tensor(part + "Wr", [P, E], F32))
            hatT = own.enter_context(nc.sbuf_tensor(part + "hatT", [P, 2, 512], F32))
            psL = own.enter_context(nc.psum_tensor(part + "psL", [P, 2, 512], F32))
            wr_loaded, routed, hatT_copied = m.sem("wr_loaded"), m.sem("routed"), m.sem("hatT_copied")
        rows_out = [m.sem(f"rows_out{u}") for u in range(2)] if rows is not None else None
        chained, var_ready, std_ready = m.sem("chained"), m.sem("var_ready"), m.sem("std_ready")
        hat_ready, hatT_ready, hatT_taken = m.sem("hat_ready"), m.sem("hatT_ready"), m.sem("hatT_taken")
        groups = NT // 4

        with nc.Block() as block:
            @block.sync
            def _(sp):
                if router:
                    sp.dma_start(Wr[:, :], wr).then_inc(wr_loaded, 16)
                if also:
                    also(sp)
                if rows is not None:
                    def write(g, u, n):
                        sp.wait_ge(hat_ready, g + 1)
                        sp.dma_start(rows[bass.ds(4 * g, 4), :, :].rearrange("j p d -> p j d"), xh[:, u, :, :]).then_inc(rows_out[u], 16)
                    peeled(sp, groups, write)
                    for u in range(2):
                        sp.wait_ge(rows_out[u], 16 * groups // 2)

            @block.vector
            def _(dve):
                chain = Chain(dve, chained)
                if not measured:
                    with dve.Fori(0, groups) as g:
                        for j in range(4):
                            last = dve.bn_stats(stats[:, 4 * g + j, :], m.X[:, 4 * g + j, :])
                        last.then_inc(chained, 1)
                    chain.n = groups
                    dve.wait_ge(chained, groups)
                dve.tensor_tensor(a[:, :], stats[:, :, 1], stats[:, :, 4], ALU.add)
                dve.tensor_tensor(diff[:, :], stats[:, :, 1], stats[:, :, 4], ALU.subtract)
                chain.link(dve.tensor_tensor(var[:, :], stats[:, :, 2], stats[:, :, 5], ALU.add))
                dve.tensor_scalar(m.mean[:, :], a[:, :], 0.5, None, ALU.mult)
                dve.tensor_scalar(var[:, :], var[:, :], 1.0 / D, EPS, ALU.mult, ALU.add)
                chain.link(dve.scalar_tensor_tensor(diff[:, :], diff[:, :], 0.25, diff[:, :], ALU.mult, ALU.mult))
                dve.tensor_tensor(var[:, :], var[:, :], diff[:, :], ALU.add).then_inc(var_ready, 1)
                dve.wait_ge(std_ready, 1)
                chain.link(dve.reciprocal(m.rstd[:, :], a[:, :]))
                if not to_xT:
                    return

                def normalise(g, u, n):
                    wait_past(dve, hatT_ready, g - 1)
                    if rows is not None:
                        wait_past(dve, rows_out[u], 16 * n)
                    for j in range(4):
                        i = 4 * g + j
                        last = dve.tensor_scalar(xh[:, u, j, :], m.X[:, i, :], m.mean[:, bass.ds(i, 1)],
                                                 m.rstd[:, bass.ds(i, 1)], ALU.subtract, ALU.mult)
                    last.then_inc(hat_ready, 1)

                dve.wait_ge(chained, chain.n)
                if not router:
                    peeled(dve, groups, normalise)
                    return

                def take_logits(g, u, n):
                    dve.wait_ge(hatT_taken, g + 1)
                    dve.tensor_scalar(m.xT[:, bass.ds(512 * g, 512)], hatT[:, u, :], 1.0, None, ALU.mult).then_inc(hatT_copied, 1)
                    dve.wait_ge(routed, g + 1)
                    out = logits[:, bass.ds(4 * g, 4), :].rearrange("p j e -> p (j e)")
                    dve.tensor_scalar(out, psL[:, u, 0:4 * E], 1.0, None, ALU.mult).then_inc(hatT_copied, 1)

                pipelined(dve, groups, [(2, normalise), (0, take_logits)])

            @block.scalar
            def _(act):
                act.wait_ge(var_ready, 1)
                act.activation(a[:, :], var[:, :], ACT.Sqrt).then_inc(std_ready, 1)
                if not to_xT:
                    return

                def take(g, u, n):
                    act.wait_ge(hatT_ready, g + 1)
                    if router:
                        wait_past(act, hatT_copied, 2 * (g - 1))
                        act.activation(hatT[:, u, :], psT[:, u, :], ACT.Copy).then_inc(hatT_taken, 1)
                        return
                    act.activation(m.xT[:, bass.ds(512 * g, 512)], psT[:, u, :], ACT.Copy).then_inc(hatT_taken, 1)

                peeled(act, groups, take)

            @block.tensor
            def _(pe):
                if not to_xT:
                    return

                def turn(g, u, n):
                    pe.wait_ge(hat_ready, g + 1)
                    wait_past(pe, hatT_taken, g - 1)
                    for j in range(4):
                        last = pe.transpose(psT[:, u, j * D:(j + 1) * D], xh[:, u, j, :], m.ident[:, :])
                    last.then_inc(hatT_ready, 1)

                if not router:
                    peeled(pe, groups, turn)
                    return

                def route(g, u, n):
                    pe.wait_ge(hatT_taken, g + 1)
                    wait_past(pe, hatT_copied, 2 * (g - 1))
                    for j in range(4):
                        last = pe.matmul(psL[:, u, j * E:j * E + E], hatT[:, u, j * D:j * D + D], Wr[:, :], start=True, stop=True)
                    last.then_inc(routed, 1)

                pe.wait_ge(wr_loaded, 16)
                pipelined(pe, groups, [(1, turn), (0, route)])
HV = 16
LAMBDA_INIT = 0.8
WIDTH = 64
REGIONS = 8


def attention(nc, m, part, norm, wq, wk, wv, wo=None, bq=None, bk=None, bv=None, bo=None,
              keep_mask=None, add_mask=None, lams=None, Oall=None):
    m.part = part
    diff = lams is not None
    CH = 2 if diff else 1
    M = NT * CH
    VW = D // CH
    W = VW // (2 * REGIONS // 2)
    LS = 2 if diff else 1
    LP = LS + 1
    with ExitStack() as own:
        def sb(name, shape, dt=F32):
            return own.enter_context(nc.sbuf_tensor(f"{part}_{name}", shape, dt))

        def pb(name, shape, dt=F32):
            return own.enter_context(nc.psum_tensor(f"{part}_{name}", shape, dt))

        Wq, Wk, Wv = sb("Wq", [P, CH * P]), sb("Wk", [P, CH * P]), sb("Wv", [P, D])
        qmask = sb("qmask", [P, 2])
        cst = sb("cst", [P, 2, 2, 2, SEQ])
        QM = sb("QM", [P, 2, 2, 2, SEQ])
        KM = sb("KM", [P, 2, 2, 2, SEQ])
        RW = 2 * (W + 1)
        WIDE = max(RW, WIDTH)
        VZ = sb("VZ", [P, 2, REGIONS * RW + WIDE - RW])
        regions = lambda par: VZ[:, par, 0:REGIONS * RW].rearrange("p (r j w) -> p r j w", j=2, w=W + 1)
        E = sb("E", [P, 2, 2, 512])
        PT = sb("PT", [P, 2, REGIONS, P])
        mx, rs, spare = sb("mx", [P, HV]), sb("rs", [P, HV]), sb("spare", [P, 1])
        On = sb("On", [P, 2 * HV // 2, W])
        if diff:
            lam, coef = sb("lam", [P, HEADS]), sb("coef", [P, CH, 2, HEADS // 2])
            lamv = sb("lamv", [P, 4, HEADS * DH])
            amask = sb("amask", [P, 4, 2, HEADS // 2, SEQ])
            Z = sb("Z", [P, 2, 2, 512])
            mx2 = sb("mx2", [P, 2, HV])
        else:
            Wo, OT = sb("Wo", [P, D]), sb("OT", [P, P])
            bqc, bkc, bvc = sb("bq", [P, 1]), sb("bk", [P, 1]), sb("bv", [P, 1])
            bvm, bias = sb("bvm", [P, P]), sb("bias", [P, D])
            inv = sb("inv", [P, HV, 2])
        if keep_mask is not None:
            keep, drop, neg, carrier = sb("keep", [P, SEQ], I32), sb("drop", [P, SEQ], I32), sb("neg", [P, 1]), sb("carrier", [P, 2])

        loaded = m.sem("loaded")

        def loads(sp):
            sp.dma_start(Wq[:, :], wq).then_inc(loaded, 16)
            sp.dma_start(Wk[:, :], wk).then_inc(loaded, 16)
            sp.dma_start(Wv[:, :], wv).then_inc(loaded, 16)
            if not diff:
                sp.dma_start(Wo[:, :], wo).then_inc(loaded, 16)
                for column, b in ((bqc, bq), (bkc, bk), (bvc, bv)):
                    sp.dma_start(column[:, :], b.rearrange("(p a) -> p a", a=1)).then_inc(loaded, 16)
                sp.dma_start(bias[:, :], bo.partition_broadcast(P)).then_inc(loaded, 16)
            if keep_mask is not None:
                for h in range(2):
                    sp.dma_start(keep[64 * h:64 * h + 64, :], keep_mask[0, 0]).then_inc(loaded, 16)
            if diff:
                for n, v in enumerate(lams):
                    sp.dma_start(lamv[:, n, :], v.rearrange("h d -> (h d)").partition_broadcast(P)).then_inc(loaded, 16)

        layer_norm(nc, m, norm, also=loads, measured=not diff)
        m.part = part
        psS = pb("psS", [P, 4, 512])
        psT = pb("psT", [P, 2, 512])
        psP = pb("psP", [P, 512])
        psO = pb("psO", [P, 512])
        SUMS = (REGIONS - 1) * RW + WIDE
        O_ = psO[:, 0:REGIONS * RW].rearrange("p (r w) -> p r w", w=W + 1)
        OTP = slice(SUMS, SUMS + P) if not diff else slice(SUMS, SUMS + VW)
        chained, prepared = m.sem("chained"), m.sem("prepared")
        staged, carried, qk_done, qk_taken, v_done, v_taken = (m.sem(n) for n in (
            "staged", "carried", "qk_done", "qk_taken", "v_done", "v_taken"))
        scored, s_taken, shifted, exped, turned, pt_ready = (m.sem(n) for n in (
            "scored", "s_taken", "shifted", "exped", "turned", "pt_ready"))
        maxed, summed, inverted, normed, folded, ot_taken = (m.sem(n) for n in (
            "maxed", "summed", "inverted", "normed", "folded", "ot_taken"))
        biased, y_ready, x_added = m.sem("biased"), m.sem("y_ready"), m.sem("x_added")
        dots_ready, lam_exps, mask_in, half_in = m.sem("dots_ready"), m.sem("lam_exps"), *(
            [m.sem(f"{name}{u}") for u in range(4)] for name in ("mask_in", "half_in"))
        o_free = ot_taken if diff else x_added
        s_free = s_taken if diff else shifted
        LOADS = 16 * (7 if diff else 8 + (2 if keep_mask is not None else 0))
        PERIOD = 4
        run = lambda eng, stages: pipelined(eng, M, stages, period=PERIOD)
        at_most = lambda v: min(v, M) if isinstance(v, int) else v

        def tile_of(s, n):
            return PERIOD // CH * n + s // CH

        with nc.Block() as block:
            @block.sync
            def _(sp):
                if diff:
                    def load_masks(i, s, n):
                        wait_past(sp, s_taken, 2 * (i - 3))
                        c = s % 2
                        for b in range(2):
                            src = add_mask[bass.ds(2 * tile_of(s, n) + b, 1), 8 * c:8 * c + 8, :, :]
                            sp.dma_start(amask[0:SEQ, s, b, :, :], src.rearrange("a h q k -> (a q) h k")).then_inc(half_in[s], 16)

                    def repeat_masks(i, s, n):
                        sp.wait_ge(half_in[s], 32 * n + 32)
                        sp.dma_start(amask[SEQ:P, s, :, :, :], amask[0:SEQ, s, :, :, :]).then_inc(mask_in[s], 16)

                    run(sp, [(2, load_masks), (0, repeat_masks)])

            @block.gpsimd
            def _(pool):
                pool.memset(spare[:, :], 0.0).then_inc(carried, 1)
                pool.wait_ge(carried, 1)
                pool.wait_ge(prepared, 2)
                pool.wait_ge(m.ctx_in, 16)

                def stage_ctx(i, s, n):
                    wait_past(pool, v_done, i - 1)
                    wait_past(pool, carried, i + 1)
                    pool.tensor_tensor(spare[:, :], spare[:, :], spare[:, :], ALU.add).then_inc(carried, 1)
                    tokens = m.ctxT[:, bass.ds(P * tile_of(s, n), P)].rearrange("p (b k) -> p b k", b=2)
                    pool.tensor_copy(cst[:, s % 2, :, :, :], tokens.unsqueeze(2).broadcast_to([P, 2, 2, SEQ])).then_inc(staged, 1)
                    if not diff:
                        mine = m.X[:, bass.ds(i, 1), :].rearrange("p a d -> p (a d)")
                        pool.tensor_tensor(mine, mine, bias[:, :], ALU.add).then_inc(biased, 1)

                def shift_masked(i, s, n):
                    for a in range(2):
                        pool.wait_ge(maxed, 2 * i + a + 1)
                        wait_past(pool, turned, 2 * i - 3 + a)
                        pool.tensor_tensor(E[:, s % 2, a, :].rearrange("p (v k) -> p v k", k=SEQ), Z[:, s % 2, a, :].rearrange("p (v k) -> p v k", k=SEQ),
                                           mx2[:, s % 2, 8 * a:8 * a + 8].unsqueeze(2).broadcast_to([P, 8, SEQ]), ALU.subtract).then_inc(shifted, 1)

                run(pool, [(1, stage_ctx)] + ([(1, shift_masked)] if diff else []))

            @block.tensor
            def _(pe):
                if not diff:
                    pe.wait_ge(prepared, 1)
                    pe.matmul(psO[:, 0:D], bvm[:, :], Wo[:, :], start=True, stop=True).then_inc(dots_ready, 1)
                pe.wait_ge(prepared, 2)
                pe.wait_ge(m.ctx_in, 16)

                def project_qk(i, s, n):
                    wait_past(pe, qk_taken, i)
                    wait_past(pe, v_taken, i - LP)
                    c = s % CH
                    x, ctx = m.xT[:, bass.ds(P * tile_of(s, n), P)], m.ctxT[:, bass.ds(P * tile_of(s, n), P)]
                    pe.matmul(psP[:, 0:P], Wq[:, c * P:c * P + P], x, start=True, stop=True)
                    pe.matmul(psP[:, P:2 * P], Wk[:, c * P:c * P + P], ctx, start=True, stop=True).then_inc(qk_done, 1)

                def project_v(i, s, n):
                    pe.wait_ge(staged, i + 1)
                    wait_past(pe, v_taken, i)
                    wait_past(pe, qk_taken, at_most(i + LP))
                    c = s % CH
                    for b in range(2):
                        last = pe.matmul(psP[:, 2 * P + b * VW:2 * P + b * VW + VW],
                                         cst[:, s % 2, b, :, :].rearrange("p t k -> p (t k)"), Wv[:, c * VW:c * VW + VW],
                                         start=True, stop=True)
                    last.then_inc(v_done, 1)

                def score(i, s, n):
                    pe.wait_ge(qk_taken, i + 1)
                    for a in range(2):
                        wait_past(pe, s_free, 2 * i - 1 + a)
                        for g in (2 * a, 2 * a + 1):
                            rows = slice(32 * g, 32 * g + 32)
                            for b in range(2):
                                last = pe.matmul(psS[:, g, b * P:b * P + P], QM[rows, s % 2, b, :, :].rearrange("p h q -> p (h q)"),
                                                 KM[rows, s % 2, b, :, :].rearrange("p j k -> p (j k)"), start=True, stop=True)
                        last.then_inc(scored, 1)

                def turn(i, s, n):
                    for a in range(2):
                        pe.wait_ge(exped, 2 * i + a + 1)
                        wait_past(pe, pt_ready, 2 * i - 1 + a)
                        for r in range(4):
                            last = pe.transpose(psT[:, a, r * P:r * P + P], E[:, s % 2, a, r * P:r * P + P], m.ident[:, :])
                        last.then_inc(turned, 1)

                def weigh(i, s, n):
                    pe.wait_ge(pt_ready, 2 * i + 2)
                    pe.wait_ge(v_taken, i + 1)
                    wait_past(pe, o_free, i)
                    for r in range(REGIONS):
                        last = pe.matmul(psO[:, r * RW:r * RW + WIDE], PT[:, s % 2, 2 * (r % 4) + r // 4, :],
                                         VZ[:, s % 2, r * RW:r * RW + WIDE], start=True, stop=True)
                    last.then_inc(summed, 1)

                def fold(i, s, n):
                    pe.wait_ge(normed, i + 1)
                    for b in range(2):
                        mine = On[:, 8 * b:8 * b + 8, :].rearrange("p r w -> p (r w)")
                        if diff:
                            last = pe.matmul(psO[64 * b:64 * b + 64, OTP], m.fold[:, :], mine, start=True, stop=True)
                        else:
                            last = pe.matmul(psO[:, SUMS + 64 * b:SUMS + 64 * b + 64], mine, m.fold[:, :], start=True, stop=True)
                    last.then_inc(folded, 1)

                def project_out(i, s, n):
                    pe.wait_ge(ot_taken, i + 1)
                    pe.matmul(psO[:, 0:D], OT[:, :], Wo[:, :], start=True, stop=True).then_inc(y_ready, 1)

                if diff:
                    run(pe, [(LS, score), (-2, fold), (LP, project_qk), (0, project_v), (0, turn), (-1, weigh)])
                else:
                    run(pe, [(LS, score), (LP, project_qk), (-2, fold), (0, project_v), (-2, project_out), (0, turn), (-1, weigh)])

            @block.scalar
            def _(act):
                if diff:
                    act.wait_ge(dots_ready, 1)
                    act.activation(lamv[:, 0, 0:HEADS], lamv[:, 1, 0:HEADS], ACT.Exp)
                    act.activation(lamv[:, 2, 0:HEADS], lamv[:, 3, 0:HEADS], ACT.Exp).then_inc(lam_exps, 1)

                def take_v(i, s, n):
                    act.wait_ge(v_done, i + 1)
                    act.wait_ge(qk_taken, at_most(i + LP + 1))
                    wait_past(act, summed, i - 1)
                    v = psP[:, 2 * P:2 * P + 2 * VW].rearrange("p (r j w) -> p r j w", r=REGIONS, w=W)
                    for j in range(2):
                        last = act.activation(regions(s % 2)[:, :, j, 0:W], v[:, :, j, :], ACT.Copy, scale=m.half_mask[:, j:j + 1])
                    last.then_inc(v_taken, 1)

                def exponent(i, s, n):
                    for a in range(2):
                        act.wait_ge(shifted, 2 * i + a + 1)
                        act.activation(E[:, s % 2, a, :], E[:, s % 2, a, :], ACT.Exp,
                                       scale=1.0 if diff else QK_SCALE).then_inc(exped, 1)

                def take_pt(i, s, n):
                    wait_past(act, summed, i - 1)
                    for a in range(2):
                        act.wait_ge(turned, 2 * i + a + 1)
                        act.activation(PT[:, s % 2, 4 * a:4 * a + 4, :].rearrange("p r q -> p (r q)"), psT[:, a, :], ACT.Copy).then_inc(pt_ready, 1)

                def take_o(i, s, n):
                    act.wait_ge(folded, i + 1)
                    if diff:
                        c = s % 2
                        act.activation(Oall[:, bass.ds(tile_of(s, n), 1), VW * c:VW * c + VW].rearrange("p a d -> p (a d)"), psO[:, OTP],
                                       ACT.Copy).then_inc(ot_taken, 1)
                        return
                    wait_past(act, y_ready, i)
                    act.activation(OT[:, :], psO[:, OTP], ACT.Copy).then_inc(ot_taken, 1)

                run(act, [(-2, take_o), (1, exponent), (0, take_pt), (0, take_v)])

            @block.vector
            def _(dve):
                chain = Chain(dve, chained)
                chain.link(dve.memset(VZ[:, :, :], 1.0))
                for par in range(2):
                    for j in range(2):
                        sums = regions(par)[:, :, j, W:W + 1]
                        dve.tensor_scalar(sums, sums, m.half_mask[:, j:j + 1], None, ALU.mult)
                if keep_mask is not None:
                    dve.memset(neg[:, :], -1e6 / QK_SCALE)
                chain.link(dve.tensor_scalar(qmask[:, :], m.head_mask[:, 0:2], QK_SCALE if diff else 1.0, None, ALU.mult))
                dve.wait_ge(loaded, LOADS)
                if keep_mask is not None:
                    chain.link(dve.tensor_scalar(drop[:, :], keep[:, :], 0, None, ALU.is_equal))
                if diff:
                    l0 = lamv[:, 0, :], lamv[:, 1, :], lamv[:, 2, :], lamv[:, 3, :]
                    dve.tensor_tensor(l0[0], l0[0], l0[1], ALU.mult)
                    chain.link(dve.tensor_tensor(l0[2], l0[2], l0[3], ALU.mult))
                    for n in (0, 2):
                        last = dve.tensor_reduce(lamv[:, n + 1, 0:HEADS], l0[n].rearrange("p (h d) -> p h d", d=DH), AX.X, ALU.add)
                    last.then_inc(dots_ready, 1)
                    dve.wait_ge(lam_exps, 1)
                    chain.link(dve.tensor_tensor(lam[:, :], lamv[:, 0, 0:HEADS], lamv[:, 2, 0:HEADS], ALU.subtract))
                    chain.link(dve.tensor_scalar(lam[:, :], lam[:, :], LAMBDA_INIT, -1.0, ALU.add, ALU.mult))
                    chain.link(dve.tensor_scalar(lam[:, :], lam[:, :], m.half_mask[:, 1:2], m.half_mask[:, 0:1], ALU.mult, ALU.add))
                    for b in range(2):
                        last = dve.tensor_copy(coef[:, :, b, :], lam[:, :].rearrange("p (c r) -> p c r", c=CH))
                    chain.link(last)
                    dve.memset(rs[:, :], 0.0).then_inc(prepared, 2)
                else:
                    chain.link(dve.memset(bvm[:, :], 1.0))
                    dve.tensor_scalar(bvm[:, :], bvm[:, :], bvc[:, 0:1], None, ALU.mult).then_inc(prepared, 1)
                    dve.wait_ge(dots_ready, 1)
                    dve.tensor_tensor(bias[:, :], bias[:, :], psO[:, 0:D], ALU.add).then_inc(prepared, 1)

                def take_qk(i, s, n):
                    dve.wait_ge(qk_done, i + 1)
                    wait_past(dve, v_done, i - LP + 1)
                    wait_past(dve, scored, 2 * (i - 1))
                    for out, src, mask, bc in ((QM, psP[:, 0:P], qmask[:, :], 0 if diff else bqc), (KM, psP[:, P:2 * P], m.head_mask[:, 2:4], 0 if diff else bkc)):
                        src = src.rearrange("p (b q) -> p b q", b=2)
                        for h in range(2):
                            if diff:
                                last = dve.tensor_scalar(out[:, s % 2, :, h, :], src, mask[:, h:h + 1], None, ALU.mult)
                            else:
                                last = dve.tensor_scalar(out[:, s % 2, :, h, :], src, bc[:, 0:1], mask[:, h:h + 1], ALU.add, ALU.mult)
                    last.then_inc(qk_taken, 1)

                def add_masks(i, s, n):
                    dve.wait_ge(mask_in[s], 16 * n + 16)
                    wait_past(dve, shifted, 2 * (i - 1))
                    for a in range(2):
                        dve.wait_ge(scored, 2 * i + a + 1)
                        by_batch = lambda v: v.rearrange("p g (b w) -> p g b w", b=2)
                        dve.tensor_tensor(by_batch(Z[:, s % 2, a, :].rearrange("p (g w) -> p g w", g=2)), by_batch(psS[:, 2 * a:2 * a + 2, 0:256]),
                                          amask[:, s, :, 4 * a:4 * a + 4, :].rearrange("p b (g j) k -> p g b (j k)", j=2),
                                          ALU.add).then_inc(s_taken, 1)
                    for a in range(2):
                        dve.wait_ge(s_taken, 2 * i + a + 1)
                        dve.tensor_reduce(mx2[:, s % 2, 8 * a:8 * a + 8], Z[:, s % 2, a, :].rearrange("p (v k) -> p v k", k=SEQ),
                                          AX.X, ALU.max).then_inc(maxed, 1)

                def shift(i, s, n):
                    banks = [psS[:, 2 * a:2 * a + 2, 0:256].rearrange("p g (v k) -> p g v k", k=SEQ) for a in range(2)]
                    tops = [mx[:, 8 * a:8 * a + 8].rearrange("p (g v) -> p g v", g=2) for a in range(2)]
                    passes = 4 if keep_mask is not None else 2
                    if keep_mask is not None:
                        m3 = drop[:, :].unsqueeze(1).unsqueeze(1).broadcast_to([P, 2, 4, SEQ])
                        n3 = neg[:, :].unsqueeze(1).unsqueeze(1).broadcast_to([P, 2, 4, SEQ])
                        for a in range(2):
                            dve.wait_ge(scored, 2 * i + a + 1)
                            dve.memset(carrier[:, a:a + 1], 0.0)
                            dve.copy_predicated(banks[a], m3, n3).then_inc(maxed, 1)
                    for a in range(2):
                        if keep_mask is not None:
                            dve.wait_ge(maxed, passes * i + a + 1)
                        else:
                            dve.wait_ge(scored, 2 * i + a + 1)
                            wait_past(dve, shifted, 2 * i)
                        dve.tensor_reduce(tops[a], banks[a], AX.X, ALU.max).then_inc(maxed, 1)
                    for a in range(2):
                        dve.wait_ge(maxed, passes * i + passes - 1 + a)
                        wait_past(dve, turned, 2 * i - 3 + a)
                        last = dve.tensor_tensor(E[:, s % 2, a, :].rearrange("p (g v k) -> p g v k", g=2, k=SEQ), banks[a],
                                                 tops[a].unsqueeze(3).broadcast_to([P, 2, 4, SEQ]), ALU.subtract)
                        last.then_inc(shifted, 1)

                def norm(i, s, n):
                    dve.wait_ge(summed, i + 1)
                    wait_past(dve, folded, i)
                    dve.reciprocal(rs[:, :], O_[:, :, W]).then_inc(inverted, 1)
                    dve.wait_ge(inverted, 2 * i + 1)
                    if diff:
                        dve.tensor_tensor(rs[:, :], rs[:, :], coef[:, s % 2, :, :].rearrange("p b r -> p (b r)"), ALU.mult).then_inc(inverted, 1)
                        dve.wait_ge(inverted, 2 * i + 2)
                        dve.tensor_tensor(On[:, :, :], O_[:, :, 0:W], rs[:, :].unsqueeze(2).broadcast_to([P, HV, W]), ALU.mult).then_inc(normed, 1)
                        return
                    dve.tensor_tensor(inv[:, :, :], rs[:, :].unsqueeze(2).broadcast_to([P, HV, 2]),
                                      m.half_mask[:, :].unsqueeze(1).broadcast_to([P, HV, 2]), ALU.mult).then_inc(inverted, 1)
                    dve.wait_ge(inverted, 2 * i + 2)
                    dve.tensor_tensor(On[:, :, :].rearrange("p r (h d) -> p r h d", d=DH), O_[:, :, 0:W].rearrange("p r (h d) -> p r h d", d=DH),
                                      inv[:, :, :].unsqueeze(3).broadcast_to([P, HV, 2, DH]), ALU.mult).then_inc(normed, 1)

                def residual(i, s, n):
                    dve.wait_ge(y_ready, i + 1)
                    dve.wait_ge(biased, i + 1)
                    dve.tensor_tensor(m.X[:, i, :], m.X[:, i, :], psO[:, 0:D], ALU.add).then_inc(x_added, 1)

                def measure(i, s, n):
                    dve.wait_ge(x_added, i + 1)
                    dve.bn_stats(m.stats[:, i, :], m.X[:, i, :])

                if diff:
                    run(dve, [(-2, norm), (LS, add_masks), (LP, take_qk)])
                else:
                    run(dve, [(-2, norm), (1, shift), (-2, residual), (LP, take_qk), (-3, measure)])


def differential_out(nc, m, part, Oall, wo, rms_scale):
    m.part = part
    with ExitStack() as own:
        def sb(name, shape, dt=F32):
            return own.enter_context(nc.sbuf_tensor(f"{part}_{name}", shape, dt))

        Wo, sc = sb("Wo", [P, D]), sb("sc", [P, 1])
        sq, inv = sb("sq", [P, NT * D]), sb("inv", [P, NT * HEADS])
        On, OT = sb("On", [P, 2, HEADS, DH]), sb("OT", [P, 2, P])
        psT = own.enter_context(nc.psum_tensor(part + "_psT", [P, 2, 512], F32))
        psY = own.enter_context(nc.psum_tensor(part + "_psY", [P, 2, 512], F32))
        loaded, chained, ms_ready, rms_ready = m.sem("loaded"), m.sem("chained"), m.sem("ms_ready"), m.sem("rms_ready")
        normed, turned, ot_ready, y_ready, x_added = (m.sem(n) for n in ("normed", "turned", "ot_ready", "y_ready", "x_added"))
        wo_scaled = m.sem("wo_scaled")

        with nc.Block() as block:
            @block.sync
            def _(sp):
                sp.dma_start(Wo[:, :], wo).then_inc(loaded, 16)
                sp.dma_start(sc[:, :], rms_scale).then_inc(loaded, 16)

            @block.vector
            def _(dve):
                chain = Chain(dve, chained)
                flat = Oall[:, :, :].rearrange("p n d -> p (n d)")
                chain.link(dve.tensor_tensor(sq[:, :], flat, flat, ALU.mult))
                chain.link(dve.tensor_reduce(inv[:, :], sq[:, :].rearrange("p (n d) -> p n d", d=DH), AX.X, ALU.add))
                dve.tensor_scalar(inv[:, :], inv[:, :], 1.0 / DH, EPS, ALU.mult, ALU.add).then_inc(ms_ready, 1)
                dve.wait_ge(loaded, 32)
                dve.tensor_scalar(Wo[:, :], Wo[:, :], sc[:, 0:1], 1.0 - LAMBDA_INIT, ALU.mult, ALU.mult).then_inc(wo_scaled, 1)
                dve.wait_ge(rms_ready, 1)
                chain.link(dve.reciprocal(inv[:, :], sq[:, 0:NT * HEADS]))

                def norm(i, u, n=None):
                    wait_past(dve, turned, i - 1)
                    dve.tensor_tensor(On[:, u, :, :], Oall[:, bass.ds(i, 1), :].rearrange("p a (h w) -> p (a h) w", w=DH),
                                      inv[:, bass.ds(HEADS * i, HEADS)].unsqueeze(2).broadcast_to([P, HEADS, DH]),
                                      ALU.mult).then_inc(normed, 1)

                def measure(i):
                    dve.wait_ge(x_added, i + 1)
                    dve.bn_stats(m.stats[:, i, :], m.X[:, i, :])

                def residual(i, u, n=None):
                    dve.wait_ge(y_ready, i + 1)
                    dve.tensor_tensor(m.X[:, i, :], m.X[:, i, :], psY[:, u, 0:D], ALU.add).then_inc(x_added, 1)

                def step(i, u, n=None):
                    norm(i, u)
                    residual(i - 1, 1 - u)
                    if not isinstance(i, int) or i > 1:
                        measure(i - 2)

                norm(0, 0)
                step(1, 1)
                in_pairs(dve, 2, NT, step)
                residual(NT - 1, 1)
                measure(NT - 2)
                measure(NT - 1)

            @block.scalar
            def _(act):
                act.wait_ge(ms_ready, 1)
                act.activation(sq[:, 0:NT * HEADS], inv[:, :], ACT.Sqrt).then_inc(rms_ready, 1)

                def take(i, u, n=None):
                    act.wait_ge(turned, i + 1)
                    wait_past(act, y_ready, i - 1)
                    act.activation(OT[:, u, :], psT[:, u, 0:P], ACT.Copy).then_inc(ot_ready, 1)
                peeled(act, NT, take)

            @block.tensor
            def _(pe):
                pe.wait_ge(wo_scaled, 1)

                def turn(i, u, n=None):
                    pe.wait_ge(normed, i + 1)
                    wait_past(pe, ot_ready, i - 1)
                    pe.transpose(psT[:, u, 0:P], On[:, u, :, :].rearrange("p h w -> p (h w)"), m.ident[:, :]).then_inc(turned, 1)

                def project(i, u, n=None):
                    pe.wait_ge(ot_ready, i + 1)
                    wait_past(pe, x_added, i - 1)
                    pe.matmul(psY[:, u, 0:D], OT[:, u, :], Wo[:, :], start=True, stop=True).then_inc(y_ready, 1)

                def step(i, u, n=None):
                    turn(i, u)
                    project(i - 1, 1 - u)
                turn(0, 0)
                step(1, 1)
                in_pairs(pe, 2, NT, step)
                project(NT - 1, 1)


def norm_of_stats(dve, chain, stats, width, mean, var_eps, tmp):
    dve.tensor_tensor(mean, stats[:, :, 1], stats[:, :, 4], ALU.add)
    dve.tensor_tensor(tmp, stats[:, :, 1], stats[:, :, 4], ALU.subtract)
    chain.link(dve.tensor_tensor(var_eps, stats[:, :, 2], stats[:, :, 5], ALU.add))
    dve.tensor_scalar(mean, mean, 0.5, None, ALU.mult)
    dve.tensor_scalar(var_eps, var_eps, 1.0 / width, EPS, ALU.mult, ALU.add)
    chain.link(dve.scalar_tensor_tensor(tmp, tmp, 0.25, tmp, ALU.mult, ALU.mult))
    return dve.tensor_tensor(var_eps, var_eps, tmp, ALU.add)


HID0 = 512


def bit_ffn(nc, m, t):
    m.part = "bit"
    C = HID0 // P
    G = NT // 4
    with ExitStack() as own:
        def sb(name, shape, dt=F32):
            return own.enter_context(nc.sbuf_tensor(f"bit_{name}", shape, dt))

        def pb(name, shape, dt=F32):
            return own.enter_context(nc.psum_tensor(f"bit_{name}", shape, dt))

        w1, w2 = sb("w1", [P, C, D]), sb("w2", [P, HID0])
        w1q, w2q = sb("w1q", [P, C, D], BF16), sb("w2q", [P, HID0], BF16)
        w1T, w2T = sb("w1T", [P, HID0], BF16), sb("w2T", [P, C, D], BF16)
        ones = sb("ones", [P, P])
        wsum, wmean, winv = sb("wsum", [P, 2]), sb("wmean", [P, 2]), sb("winv", [P, 2])
        g1, b1n, b2 = sb("g1", [P, D]), sb("b1n", [P, D]), sb("b2", [P, D])
        b1, g2, b2n = sb("b1", [P, HID0]), sb("g2", [P, HID0]), sb("b2n", [P, HID0])
        R, tmp = sb("R", [P, NT]), sb("tmp", [P, NT])
        mean2, rstd2, shift2 = sb("mean2", [P, NT]), sb("rstd2", [P, NT]), sb("shift2", [P, NT])
        stats = sb("stats", [P, NT, 6])
        H = sb("H", [P, NT, HID0])
        xh, xq, xqT = sb("xh", [P, 2, 4, D]), sb("xq", [P, 2, 4 * D], BF16), sb("xqT", [P, 2, 4 * D], BF16)
        amax, scale, undo = sb("amax", [P, 4]), sb("scale", [P, 4]), sb("undo", [P, 2, 4])
        hn = sb("hn", [P, 4, 2, HID0])
        hq, hqT = sb("hq", [P, 2, 2 * HID0], BF16), sb("hqT", [P, 2, 2 * HID0], BF16)
        top2, scale2, undo2, minus = sb("top2", [P, 2]), sb("scale2", [P, 2]), sb("undo2", [P, 4, 2]), sb("minus", [P, 1])
        y = sb("y", [P, 2, D])
        loaded = m.sem("loaded")

        def loads(sp):
            sp.dma_start(w1[:, :, :], t["L0_ffn_w1"].rearrange("(c p) d -> p c d", p=P)).then_inc(loaded, 16)
            sp.dma_start(w2[:, :], t["L0_ffn_w2"]).then_inc(loaded, 16)
            for dst, name in ((g1, "ln1_g"), (b1n, "ln1_b"), (b2, "b2"), (b1, "b1"), (g2, "ln2_g"), (b2n, "ln2_b")):
                sp.dma_start(dst[:, :], t["L0_ffn_" + name].partition_broadcast(P)).then_inc(loaded, 16)

        layer_norm(nc, m, "ln1", to_xT=False, also=loads)
        m.part = "bit"
        psT = pb("psT", [P, 2, 1024], BF16)
        psH = pb("psH", [P, 4, HID0])
        psY = pb("psY", [P, 2, 512])
        chained, wsum_ready, wtot_ready, wq_ready, wT_turned, wT_ready = (m.sem(n) for n in (
            "chained", "wsum_ready", "wtot_ready", "wq_ready", "wT_turned", "wT_ready"))
        r_in, r_out = m.sem("r_in"), m.sem("r_out")
        xq_ready, xq_turned, xqT_ready, up_ready, biased, gelued = (m.sem(n) for n in (
            "xq_ready", "xq_turned", "xqT_ready", "up_ready", "biased", "gelued"))
        n_ready, hq_ready, hq_turned, hqT_ready, down_ready, x_added = (m.sem(n) for n in (
            "n_ready", "hq_ready", "hq_turned", "hqT_ready", "down_ready", "x_added"))
        affined, rounded, xn_ready, x_affined = m.sem("affined"), m.sem("rounded"), m.sem("xn_ready"), m.sem("x_affined")
        PAIRS = NT // 2
        LOADS = 16 * 8

        with nc.Block() as block:
            @block.vector
            def _(dve):
                chain = Chain(dve, chained)
                dve.memset(ones[:, :], 1.0)
                dve.memset(minus[:, :], -MAGIC)
                chain.link(dve.tensor_tensor(tmp[:, :], m.rstd[:, :], m.rstd[:, :], ALU.mult))
                dve.tensor_scalar(tmp[:, :], tmp[:, :], -EPS, 1.0 + EPS, ALU.mult, ALU.add).then_inc(r_in, 1)
                dve.wait_ge(loaded, LOADS)
                dve.tensor_reduce(wsum[:, 0:1], w1[:, :, :], AX.XY, ALU.add, apply_absolute_value=True)
                dve.tensor_reduce(wsum[:, 1:2], w2[:, :], AX.X, ALU.add, apply_absolute_value=True).then_inc(wsum_ready, 1)
                dve.wait_ge(r_out, 1)
                chain.link(dve.reciprocal(tmp[:, :], R[:, :]))
                chain.link(dve.tensor_tensor(R[:, :], m.rstd[:, :], tmp[:, :], ALU.mult))
                dve.wait_ge(wtot_ready, 1)
                chain.link(dve.tensor_scalar(wmean[:, :], psY[:, 0, 0:2], 1.0 / (HID0 * D), EPS, ALU.mult, ALU.max))
                chain.link(dve.reciprocal(winv[:, :], wmean[:, :]))
                dve.tensor_scalar(w1[:, :, :], w1[:, :, :], winv[:, 0:1], 1.0, ALU.mult, ALU.min)
                chain.link(dve.tensor_scalar(w2[:, :], w2[:, :], winv[:, 1:2], 1.0, ALU.mult, ALU.min))
                dve.tensor_scalar(w1[:, :, :], w1[:, :, :], -1.0, MAGIC, ALU.max, ALU.add)
                chain.link(dve.tensor_scalar(w2[:, :], w2[:, :], -1.0, MAGIC, ALU.max, ALU.add))
                dve.tensor_scalar(w1q[:, :, :], w1[:, :, :], MAGIC, None, ALU.subtract)
                dve.tensor_scalar(w2q[:, :], w2[:, :], MAGIC, None, ALU.subtract).then_inc(wq_ready, 1)
                dve.wait_ge(wT_turned, 1)
                dve.tensor_copy(w1T[:, :], psT[:, 0, 0:HID0])
                dve.tensor_copy(w2T[:, :, :], psT[:, 1, 0:HID0].rearrange("p (c d) -> p c d", c=C)).then_inc(wT_ready, 1)
                before = chain.n
                A_LINKS = 5

                def normalise_x(g, u, n):
                    wait_past(dve, xq_ready, g - 1)
                    for j in range(4):
                        i = 4 * g + j
                        last = dve.tensor_scalar(xh[:, u, j, :], m.X[:, i, :], m.mean[:, bass.ds(i, 1)],
                                                 R[:, bass.ds(i, 1)], ALU.subtract, ALU.mult)
                    last.then_inc(xn_ready, 1)

                def quantise(g, u, n):
                    wait_past(dve, xq_turned, g - 1)
                    wait_past(dve, xq_ready, g)
                    dve.wait_ge(x_affined, 2 * g + 2)
                    c = Chain(dve, chained, before + A_LINKS * g)
                    x = xh[:, u, :, :]
                    c.link(dve.tensor_reduce(amax[:, :], x, AX.X, ALU.max, apply_absolute_value=True))
                    c.link(dve.tensor_scalar(amax[:, :], amax[:, :], EPS, 1.0 / 127.0, ALU.max, ALU.mult))
                    dve.tensor_scalar(undo[:, u, :], amax[:, :], wmean[:, 0:1], None, ALU.mult)
                    c.link(dve.reciprocal(scale[:, :], amax[:, :]))
                    for j in range(4):
                        last = dve.tensor_scalar(xh[:, u, j, :], xh[:, u, j, :], scale[:, j:j + 1], 127.0, ALU.mult, ALU.min)
                    c.link(last)
                    c.link(dve.tensor_scalar(x, x, -128.0, MAGIC, ALU.max, ALU.add))
                    assert c.n == A_LINKS
                    dve.tensor_scalar(xq[:, u, :], x.rearrange("p j d -> p (j d)"), MAGIC, None, ALU.subtract).then_inc(xq_ready, 1)

                def bias(g, u, n):
                    for j in range(4):
                        i = 4 * g + j
                        dve.wait_ge(up_ready, i + 1)
                        dve.scalar_tensor_tensor(H[:, bass.ds(i, 1), :].rearrange("p a h -> p (a h)"), psH[:, j, :], undo[:, u, j:j + 1], b1[:, :],
                                                 ALU.mult, ALU.add).then_inc(biased, 1)

                def measure(g, u, n):
                    dve.wait_ge(gelued, 4 * g + 4)
                    for j in range(4):
                        dve.bn_stats(stats[:, 4 * g + j, :], H[:, 4 * g + j, :])

                pipelined(dve, G, [(1, quantise), (2, normalise_x), (0, bias), (-1, measure)])
                c = Chain(dve, chained, before + A_LINKS * G)
                c.link(dve.memset(y[:, 0, 0:1], 0.0))
                norm_of_stats(dve, c, stats, HID0, mean2[:, :], R[:, :], tmp[:, :]).then_inc(r_in, 1)
                dve.wait_ge(r_out, 2)
                c.link(dve.reciprocal(rstd2[:, :], tmp[:, :]))
                c.link(dve.scalar_tensor_tensor(shift2[:, :], mean2[:, :], -1.0, rstd2[:, :], ALU.mult, ALU.mult))
                dve.memset(y[:, 0, 0:1], 0.0).then_inc(r_in, 1)
                before_b = c.base + c.n
                B_LINKS = 5

                def quantise_h(k, s, n):
                    dve.wait_ge(affined, 2 * k + 2)
                    wait_past(dve, rounded, k)
                    c = Chain(dve, chained, before_b + B_LINKS * k)
                    h = hn[:, s, :, :]
                    c.link(dve.tensor_reduce(top2[:, :], h, AX.X, ALU.max, apply_absolute_value=True))
                    c.link(dve.tensor_scalar(top2[:, :], top2[:, :], EPS, 1.0 / 127.0, ALU.max, ALU.mult))
                    dve.tensor_scalar(undo2[:, s, :], top2[:, :], wmean[:, 1:2], None, ALU.mult)
                    c.link(dve.reciprocal(scale2[:, :], top2[:, :]))
                    c.link(dve.tensor_scalar(hn[:, s, 0, :], hn[:, s, 0, :], scale2[:, 0:1], 127.0, ALU.mult, ALU.min))
                    c.link(dve.tensor_scalar(hn[:, s, 1, :], hn[:, s, 1, :], scale2[:, 1:2], 127.0, ALU.mult, ALU.min))
                    dve.tensor_scalar(h, h, -128.0, MAGIC, ALU.max, ALU.add).then_inc(rounded, 1)

                def residual(k, s, n):
                    dve.wait_ge(down_ready, k + 1)
                    wait_past(dve, x_added, 2 * k)
                    for j in range(2):
                        last = dve.scalar_tensor_tensor(y[:, j, :], psY[:, s % 2, j * D:j * D + D], undo2[:, s, j:j + 1], b2[:, :], ALU.mult, ALU.add)
                    last.then_inc(x_added, 1)
                    dve.wait_ge(x_added, 2 * k + 1)
                    tiles = m.X[:, bass.ds(2 * k, 2), :]
                    dve.tensor_tensor(tiles, tiles, y[:, :, :], ALU.add).then_inc(x_added, 1)

                def measure_x(k, s, n):
                    dve.wait_ge(x_added, 2 * k + 2)
                    for j in range(2):
                        dve.bn_stats(m.stats[:, 2 * k + j, :], m.X[:, 2 * k + j, :])

                pipelined(dve, PAIRS, [(-2, residual), (0, quantise_h), (-3, measure_x)], period=4)

            @block.gpsimd
            def _(pool):
                def affine_x(g, u, n):
                    row = lambda v: v[:, :].unsqueeze(1).broadcast_to([P, 4, D])
                    pool.wait_ge(xn_ready, g + 1)
                    pool.tensor_tensor(xh[:, u, :, :], xh[:, u, :, :], row(g1), ALU.mult).then_inc(x_affined, 1)
                    pool.wait_ge(x_affined, 2 * g + 1)
                    pool.tensor_tensor(xh[:, u, :, :], xh[:, u, :, :], row(b1n), ALU.add).then_inc(x_affined, 1)

                peeled(pool, G, affine_x)

                def affine(k, s, n):
                    row = lambda v: v[:, :].unsqueeze(1).broadcast_to([P, 2, HID0])
                    pool.wait_ge(n_ready, k + 1)
                    pool.tensor_tensor(hn[:, s, :, :], hn[:, s, :, :], row(g2), ALU.mult).then_inc(affined, 1)
                    pool.wait_ge(affined, 2 * k + 1)
                    pool.tensor_tensor(hn[:, s, :, :], hn[:, s, :, :], row(b2n), ALU.add).then_inc(affined, 1)

                pipelined(pool, PAIRS, [(0, affine)], period=4)

            @block.scalar
            def _(act):
                act.wait_ge(r_in, 1)
                act.activation(R[:, :], tmp[:, :], ACT.Sqrt).then_inc(r_out, 1)

                def take(g, u, n):
                    act.wait_ge(xq_turned, g + 1)
                    wait_past(act, up_ready, 4 * (g - 1))
                    act.activation(xqT[:, u, :], psT[:, u, 0:4 * D], ACT.Copy).then_inc(xqT_ready, 1)

                def gelu(g, u, n):
                    for j in range(4):
                        i = 4 * g + j
                        act.wait_ge(biased, i + 1)
                        act.activation(H[:, i, :], H[:, i, :], ACT.Gelu).then_inc(gelued, 1)

                act.wait_ge(wT_ready, 1)
                pipelined(act, G, [(1, take), (0, gelu)])
                act.wait_ge(r_in, 2)
                act.activation(tmp[:, :], R[:, :], ACT.Sqrt).then_inc(r_out, 1)
                act.wait_ge(r_in, 3)

                def normalise(k, s, n):
                    wait_past(act, hq_ready, k - 3)
                    for j in range(2):
                        last = act.activation(hn[:, s, j, :], H[:, bass.ds(2 * k + j, 1), :].rearrange("p a h -> p (a h)"), ACT.Identity,
                                              bias=shift2[:, bass.ds(2 * k + j, 1)], scale=rstd2[:, bass.ds(2 * k + j, 1)])
                    last.then_inc(n_ready, 1)

                def to_integers(k, s, n):
                    act.wait_ge(rounded, k + 1)
                    wait_past(act, hq_turned, k - 1)
                    act.activation(hq[:, s % 2, :], hn[:, s, :, :].rearrange("p j h -> p (j h)"), ACT.Identity, bias=minus[:, 0:1]).then_inc(hq_ready, 1)

                def take_h(k, s, n):
                    act.wait_ge(hq_turned, k + 1)
                    wait_past(act, down_ready, k - 1)
                    act.activation(hqT[:, s % 2, :], psT[:, s % 2, :], ACT.Copy).then_inc(hqT_ready, 1)

                pipelined(act, PAIRS, [(-1, take_h), (2, normalise), (0, to_integers)], period=4)

            @block.tensor
            def _(pe):
                pe.wait_ge(wsum_ready, 1)
                pe.matmul(psY[:, 0, 0:2], ones[:, :], wsum[:, :], start=True, stop=True).then_inc(wtot_ready, 1)
                pe.wait_ge(wq_ready, 1)
                for c in range(C):
                    pe.transpose(psT[:, 0, c * P:c * P + P], w1q[:, c, :], m.identb[:, :])
                for c in range(C):
                    last = pe.transpose(psT[:, 1, c * P:c * P + P], w2q[:, c * P:c * P + P], m.identb[:, :])
                last.then_inc(wT_turned, 1)
                pe.wait_ge(wT_ready, 1)

                def turn(g, u, n):
                    pe.wait_ge(xq_ready, g + 1)
                    wait_past(pe, xqT_ready, g - 1)
                    for j in range(4):
                        last = pe.transpose(psT[:, u, j * D:j * D + D], xq[:, u, j * D:j * D + D], m.identb[:, :])
                    last.then_inc(xq_turned, 1)

                def up(g, u, n):
                    pe.wait_ge(xqT_ready, g + 1)
                    for j in range(4):
                        wait_past(pe, biased, 4 * g + (j - 3))
                        pe.matmul(psH[:, j, :], xqT[:, u, j * D:j * D + D], w1T[:, :], start=True, stop=True).then_inc(up_ready, 1)

                pipelined(pe, G, [(0, up), (1, turn)])

                def turn_h(k, s, n):
                    pe.wait_ge(hq_ready, k + 1)
                    wait_past(pe, hqT_ready, k - 1)
                    for c in range(2 * C):
                        last = pe.transpose(psT[:, s % 2, c * P:c * P + P], hq[:, s % 2, c * P:c * P + P], m.identb[:, :])
                    last.then_inc(hq_turned, 1)

                def down(k, s, n):
                    pe.wait_ge(hqT_ready, k + 1)
                    wait_past(pe, x_added, 2 * (k - 1))
                    for j in range(2):
                        for c in range(C):
                            last = pe.matmul(psY[:, s % 2, j * D:j * D + D], hqT[:, s % 2, (j * C + c) * P:(j * C + c) * P + P], w2T[:, c, :],
                                             start=(c == 0), stop=(c == C - 1))
                    last.then_inc(down_ready, 1)

                pipelined(pe, PAIRS, [(-1, down), (0, turn_h)], period=4)


HID1, EXP1 = 512, 8
TOP1_SCALE = 2.0
BLOCKS = (TOK + EXP1 * (P - 1)) // P


def expert_ffn(nc, m, t):
    C, G = HID1 // P, NT // 4
    EARLY = 5
    xs = nc.dram_tensor("ex_xs", (BLOCKS * P, D), F32, kind="Internal").ap()
    ys = nc.dram_tensor("ex_ys", (BLOCKS * P, D), F32, kind="Internal").ap()
    with ExitStack() as own:
        def sb(name, shape, dt=F32):
            return own.enter_context(nc.sbuf_tensor(f"ex_{name}", shape, dt))

        def pb(name, shape, dt=F32):
            return own.enter_context(nc.psum_tensor(f"ex_{name}", shape, dt))

        prob = sb("prob", [P, NT, EXP1])
        m.part = "ex"
        wu, wg = sb("wu", [P, EXP1, HID1]), sb("wg", [P, EXP1, HID1])
        wd = sb("wd", [P, EXP1, C, D])
        order = sb("order", [P, EXP1])
        upto, uptob, onesb = sb("upto", [P, P]), sb("uptob", [P, P], BF16), sb("onesb", [P, P], BF16)
        number = sb("number", [1, BLOCKS])
        eq = sb("eq", [P, NT, EXP1])
        M, inc, fresh = (sb(n, [P, EXP1, NT]) for n in ("M", "inc", "fresh"))
        Mb, incb, excb = (sb(n, [P, EXP1, NT], BF16) for n in ("Mb", "incb", "excb"))
        top, total, weight = sb("top", [P, NT]), sb("total", [P, NT]), sb("weight", [P, NT])
        count, whole, ends, one8 = (sb(n, [P, EXP1]) for n in ("count", "whole", "ends", "one8"))
        pos = sb("pos", [P, NT], I32)
        over = sb("over", [1, BLOCKS, EXP1 - 1])
        ids = sb("ids", [1, BLOCKS], I32)
        sg, h, upc = sb("sg", [P, 2, 512]), sb("h", [P, 2, 512]), sb("upc", [P, 2, 512])
        S = sb("S", [P, NT, D])
        idx = sb("idx", [P, 4], I32)
        row = sb("row", [P, 4, D])
        out = sb("out", [P, 4, D])
        GT, hT = sb("GT", [P, 2, P]), sb("hT", [P, 2, 512])
        zero, spare = sb("zero", [P, D]), sb("spare", [P, 1])
        loaded, w_loaded = m.sem("loaded"), m.sem("w_loaded")

        def loads(sp):
            sp.dma_start(wu[:, EXP1 - 1, :], t["L1_ffn_ws_up"]).then_inc(w_loaded, 16)
            sp.dma_start(wg[:, EXP1 - 1, :], t["L1_ffn_ws_gate"]).then_inc(w_loaded, 16)
            sp.dma_start(wd[:, EXP1 - 1, :, :], t["L1_ffn_ws_down"].rearrange("(c p) d -> p c d", p=P)).then_inc(w_loaded, 16)
            sp.dma_start(order[:, :], t["c_order"].partition_broadcast(P)).then_inc(loaded, 16)
            sp.dma_start(upto[:, :], t["c_upto"]).then_inc(loaded, 16)
            sp.dma_start(number[:, :], t["c_blocks"].rearrange("(a b) -> a b", a=1)).then_inc(loaded, 16)

        layer_norm(nc, m, "ln3", router=(t["L1_ffn_w_router"], prob), also=loads)
        m.part = "ex"
        psU, psG, psH = pb("psU", [P, 2, 512]), pb("psG", [P, 2, 512]), pb("psH", [P, 2, 512])
        psX, psY = pb("psX", [P, 512]), pb("psY", [P, 512])
        chained, shifted, exped = (m.sem(n) for n in ("chained", "shifted", "exped"))
        zeroed, z_out, counting, counted, given, carried = (m.sem(n) for n in (
            "zeroed", "z_out", "counting", "counted", "given", "carried"))
        up_ready, gated, h_ready, down_done, s_written = (m.sem(n) for n in ("up_ready", "gated", "h_ready", "down_done", "s_written"))
        experts_in, up_taken = m.sem("experts_in"), m.sem("up_taken")
        scattered = [m.sem(f"scattered{s}") for s in range(4)]

        def shared_up(pe, q, c, g):
            wait_past(pe, h_ready, q - 1)
            x = m.xT[:, bass.ds(512 * g, 512)]
            pe.matmul(psU[:, c % 2, :], wu[:, EXP1 - 1, c * P:c * P + P], x, start=True, stop=True)
            pe.matmul(psG[:, c % 2, :], wg[:, EXP1 - 1, c * P:c * P + P], x, start=True, stop=True).then_inc(up_ready, 1)

        def shared_down(pe, q, c, g, half):
            pe.wait_ge(h_ready, q + 1)
            if c == 0:
                wait_past(pe, s_written, g - 1)
            for j in range(4):
                last = pe.matmul(psH[:, half, j * D:j * D + D], h[:, c % 2, j * P:j * P + P], wd[:, EXP1 - 1, c, :],
                                 start=(c == 0 and j == 0), stop=(c == C - 1), skip_group_check=True)
            last.then_inc(down_done, 1)

        def shared_silu(act, q, u):
            act.wait_ge(up_ready, q + 1)
            wait_past(act, h_ready, q - 1)
            act.activation(sg[:, u, :], psG[:, u, :], ACT.Silu).then_inc(gated, 1)

        def shared_take(act, g, half):
            act.wait_ge(down_done, C * g + C)
            act.activation(S[:, bass.ds(4 * g, 4), :].rearrange("p j d -> p (j d)"), psH[:, half, :], ACT.Copy).then_inc(s_written, 1)

        def shared_product(eng, q, u, up=psU):
            eng.wait_ge(gated, q + 1)
            wait_past(eng, down_done, q - 1)
            eng.tensor_tensor(h[:, u, :], up[:, u, :], sg[:, u, :], ALU.mult).then_inc(h_ready, 1)

        ON_POOL = 4
        UNITS = EARLY * C
        with nc.Block() as block:
            @block.sync
            def _(sp):
                sp.wait_ge(zeroed, 1)
                sp.dma_start(xs.rearrange("(b p) d -> p b d", p=P), zero[:, :].unsqueeze(1).broadcast_to([P, BLOCKS, D])).then_inc(z_out, 16)
                sp.dma_start(wu[:, 0:EXP1 - 1, :], t["L1_ffn_w_up"].rearrange("e d h -> d e h")).then_inc(experts_in, 16)
                sp.dma_start(wg[:, 0:EXP1 - 1, :], t["L1_ffn_w_gate"].rearrange("e d h -> d e h")).then_inc(experts_in, 16)
                sp.dma_start(wd[:, 0:EXP1 - 1, :, :], t["L1_ffn_w_down"].rearrange("e (c p) d -> p e c d", p=P)).then_inc(experts_in, 16)
                sp.wait_ge(experts_in, 48)

            @block.gpsimd
            def _(pool):
                pool.memset(zero[:, :], 0.0).then_inc(zeroed, 1)
                for q in range(ON_POOL):
                    pool.wait_ge(up_taken, q + 1)
                    shared_product(pool, q, q % 2, up=upc)
                pool.wait_ge(z_out, 16)

                def scatter(i, s, n):
                    pool.wait_ge(given, i + 1)
                    wait_past(pool, carried, i)
                    pool.tensor_tensor(spare[:, :], zero[:, 0:1], zero[:, 0:1], ALU.add).then_inc(carried, 1)
                    pool.indirect_dma_start(xs, bass.IndirectOffsetOnAxis(ap=idx[:, s:s + 1], axis=0), row[:, s, :], None).then_inc(scattered[s], 16)

                pipelined(pool, NT, [(0, scatter)], period=4)
                for s in range(4):
                    pool.wait_ge(scattered[s], 16 * NT // 4)

            @block.scalar
            def _(act):
                act.wait_ge(shifted, 1)
                act.activation(prob[:, :, :], prob[:, :, :], ACT.Exp).then_inc(exped, 1)

                def silu(q, s, n):
                    if isinstance(q, int) and q < ON_POOL:
                        act.wait_ge(up_ready, q + 1)
                        wait_past(act, h_ready, q - 1)
                        act.activation(upc[:, s % 2, :], psU[:, s % 2, :], ACT.Copy).then_inc(up_taken, 1)
                    shared_silu(act, q, s % 2)

                def take(q, s, n):
                    if s % C == C - 1:
                        shared_take(act, 2 * n + s // C, s // C)

                pipelined(act, UNITS, [(0, silu), (-1, take)], period=2 * C)

            @block.tensor
            def _(pe):
                def up(q, s, n):
                    shared_up(pe, q, s % C, 2 * n + s // C)

                def down(q, s, n):
                    shared_down(pe, q, s % C, 2 * n + s // C, s // C)

                pe.wait_ge(w_loaded, 48)
                for q in range(UNITS):
                    up(q, q % (2 * C), q // (2 * C))
                    if q:
                        down(q - 1, (q - 1) % (2 * C), (q - 1) // (2 * C))
                    if q == 2:
                        pe.wait_ge(counting, 1)
                        flat = lambda v: v[:, :, :].rearrange("p e n -> p (e n)")
                        pe.matmul(psX[:, 0:EXP1 * NT], uptob[:, :], flat(Mb), start=True, stop=False)
                        pe.matmul(psX[:, 0:EXP1 * NT], onesb[:, :], flat(excb), start=False, stop=True)
                        pe.matmul(psY[:, 0:EXP1], onesb[:, :], incb[:, :, NT - 1], start=True, stop=True).then_inc(counted, 1)
                down(UNITS - 1, (UNITS - 1) % (2 * C), (UNITS - 1) // (2 * C))

            @block.vector
            def _(dve):
                chain = Chain(dve, chained)
                wide = lambda v: v[:, :].unsqueeze(2).broadcast_to([P, NT, EXP1])
                flat = lambda v: v[:, :, :].rearrange("p e n -> p (e n)")
                chain.link(dve.tensor_reduce(top[:, :], prob[:, :, :], AX.X, ALU.max))
                dve.tensor_tensor(prob[:, :, :], prob[:, :, :], wide(top), ALU.subtract).then_inc(shifted, 1)
                dve.memset(onesb[:, :], 1.0)
                dve.memset(one8[:, :], 1.0)
                chain.link(dve.memset(fresh[:, :, :], 1.0))
                dve.memset(fresh[:, :, 0:1], 0.0)
                dve.wait_ge(loaded, 48)
                dve.tensor_copy(uptob[:, :], upto[:, :])
                dve.wait_ge(exped, 1)
                chain.link(dve.tensor_reduce(total[:, :], prob[:, :, :], AX.X, ALU.add))
                chain.link(dve.reciprocal(total[:, :], total[:, :]))
                chain.link(dve.tensor_tensor(prob[:, :, :], prob[:, :, :], wide(total), ALU.mult))
                chain.link(dve.tensor_reduce(top[:, :], prob[:, :, :], AX.X, ALU.max))
                chain.link(dve.tensor_tensor(eq[:, :, :], prob[:, :, :], wide(top), ALU.is_equal))
                chain.link(dve.tensor_tensor(eq[:, :, :], eq[:, :, :], order[:, :].unsqueeze(1).broadcast_to([P, NT, EXP1]), ALU.mult))
                chain.link(dve.tensor_reduce(total[:, :], eq[:, :, :], AX.X, ALU.max))
                by_token = M[:, :, :].rearrange("p e n -> p n e")
                chain.link(dve.tensor_tensor(by_token, eq[:, :, :], wide(total), ALU.is_equal))
                dve.tensor_copy(Mb[:, :, :], M[:, :, :])
                chain.link(dve.tensor_tensor_scan(flat(inc), flat(fresh), flat(M), 0.0, ALU.mult, ALU.add))
                dve.tensor_copy(incb[:, :, :], inc[:, :, :])
                dve.tensor_tensor(excb[:, :, :], inc[:, :, :], M[:, :, :], ALU.subtract).then_inc(counting, 1)
                chain.link(dve.tensor_scalar(weight[:, :], M[:, EXP1 - 1, :], -TOP1_SCALE, TOP1_SCALE, ALU.mult, ALU.add))
                dve.tensor_tensor(weight[:, :], weight[:, :], top[:, :], ALU.mult)
                dve.wait_ge(counted, 1)
                chain.link(dve.tensor_scalar(count[:, :], psY[:, 0:EXP1], (P - 1) / 2, 1.0 / P, ALU.add, ALU.mult))
                chain.link(dve.tensor_scalar(whole[:, :], count[:, :], MAGIC, -MAGIC, ALU.add, ALU.add))
                chain.link(dve.tensor_tensor_scan(ends[:, :], one8[:, :], whole[:, :], 0.0, ALU.mult, ALU.add))
                chain.link(dve.tensor_tensor(count[:, :], ends[:, :], whole[:, :], ALU.subtract))
                chain.link(dve.tensor_scalar(count[:, :], count[:, :], float(P), -1.0, ALU.mult, ALU.add))
                chain.link(dve.tensor_tensor(inc[:, :, :], psX[:, 0:EXP1 * NT].rearrange("p (e n) -> p e n", n=NT),
                                             count[:, :].unsqueeze(2).broadcast_to([P, EXP1, NT]), ALU.add))
                chain.link(dve.tensor_tensor(inc[:, :, :], inc[:, :, :], M[:, :, :], ALU.mult))
                chain.link(dve.tensor_reduce(total[:, :], inc[:, :, :].rearrange("p e n -> p n e"), AX.X, ALU.add))
                dve.tensor_copy(pos[:, :], total[:, :])
                full = [1, BLOCKS, EXP1 - 1]
                chain.link(dve.tensor_tensor(over[:, :, :], ends[0:1, 0:EXP1 - 1].unsqueeze(1).broadcast_to(full),
                                             number[:, :].unsqueeze(2).broadcast_to(full), ALU.is_le))
                chain.link(dve.tensor_reduce(inc[0:1, 0:2, :].rearrange("p e n -> p (e n)")[:, 0:BLOCKS], over[:, :, :], AX.X, ALU.add))
                chain.link(dve.tensor_copy(ids[:, :], inc[0:1, 0:2, :].rearrange("p e n -> p (e n)")[:, 0:BLOCKS]))
                dve.wait_ge(h_ready, ON_POOL)

                def give(i, s, n):
                    wait_past(dve, scattered[s % 4], 16 * (2 * n + s // 4))
                    dve.tensor_copy(idx[:, s % 4:s % 4 + 1], pos[:, bass.ds(i, 1)])
                    dve.tensor_scalar(row[:, s % 4, :], m.X[:, bass.ds(i, 1), :].rearrange("p a d -> p (a d)"), m.mean[:, bass.ds(i, 1)],
                                      m.rstd[:, bass.ds(i, 1)], ALU.subtract, ALU.mult).then_inc(given, 1)

                def step(k, i0, q0):
                    for s in range(8):
                        give(i0 + s, s, k)
                        if s % 2:
                            shared_product(dve, q0 + s // 2, s // 2 % 2)
                step(0, 0, ON_POOL)
                with dve.Fori(1, NT // 8) as k:
                    step(k, 8 * k, ON_POOL + 4 * k)

        m.part = "exb"
        x_in, y_out = ([m.sem(f"{n}{s}") for s in range(4)] for n in ("x_in", "y_out"))
        turned, gt_ready, ug_ready, silued, hb_ready = (m.sem(n) for n in ("turned", "gt_ready", "ug_ready", "silued", "hb_ready"))
        h_turned, ht_ready, y_ready, y_taken = (m.sem(n) for n in ("h_turned", "ht_ready", "y_ready", "y_taken"))
        run = lambda eng, stages: pipelined(eng, BLOCKS, stages, period=4)
        with nc.Block() as block:
            @block.sync
            def _(sp):
                def load(b, s, n):
                    wait_past(sp, turned, b - 3)
                    sp.dma_start(row[:, s, :], xs[bass.ds(P * b, P), :]).then_inc(x_in[s], 16)

                def store(b, s, n):
                    sp.wait_ge(y_taken, b + 1)
                    sp.dma_start(ys[bass.ds(P * b, P), :], out[:, s, :]).then_inc(y_out[s], 16)

                run(sp, [(4, load), (-2, store)])
                for s in range(4):
                    sp.wait_ge(y_out[s], 16 * len(range(s, BLOCKS, 4)))

            @block.tensor
            def _(pe):
                def turn(b, s, n):
                    pe.wait_ge(x_in[s], 16 * n + 16)
                    wait_past(pe, gt_ready, b)
                    pe.transpose(psX[:, 0:P], row[:, s, :], m.ident[:, :]).then_inc(turned, 1)

                def expert_of(b):
                    return pe.value_load(ids[0:1, bass.ds(b, 1)], min_val=0, max_val=EXP1 - 1)

                def up(b, s, n):
                    e = expert_of(b)
                    pe.wait_ge(gt_ready, b + 1)
                    wait_past(pe, hb_ready, b - 1)
                    pe.matmul(psU[:, s % 2, :], GT[:, s % 2, :], wu[:, bass.ds(e, 1), :].rearrange("p a h -> p (a h)"), start=True, stop=True)
                    pe.matmul(psG[:, s % 2, :], GT[:, s % 2, :], wg[:, bass.ds(e, 1), :].rearrange("p a h -> p (a h)"), start=True, stop=True).then_inc(ug_ready, 1)

                def turn_h(b, s, n):
                    pe.wait_ge(hb_ready, b + 1)
                    wait_past(pe, ht_ready, b - 1)
                    for c in range(C):
                        last = pe.transpose(psH[:, s % 2, c * P:c * P + P], h[:, s % 2, c * P:c * P + P], m.ident[:, :])
                    last.then_inc(h_turned, 1)

                def down(b, s, n):
                    e = expert_of(b)
                    pe.wait_ge(ht_ready, b + 1)
                    wait_past(pe, y_taken, b)
                    for c in range(C):
                        last = pe.matmul(psY[:, 0:D], hT[:, s % 2, c * P:c * P + P], wd[:, bass.ds(e, 1), c, :].rearrange("p a d -> p (a d)"),
                                         start=(c == 0), stop=(c == C - 1))
                    last.then_inc(y_ready, 1)

                run(pe, [(1, turn), (0, up), (-1, turn_h), (-2, down)])

            @block.scalar
            def _(act):
                def take_x(b, s, n):
                    act.wait_ge(turned, b + 1)
                    wait_past(act, ug_ready, b - 1)
                    act.activation(GT[:, s % 2, :], psX[:, 0:P], ACT.Copy).then_inc(gt_ready, 1)

                def silu(b, s, n):
                    act.wait_ge(ug_ready, b + 1)
                    wait_past(act, hb_ready, b - 1)
                    act.activation(sg[:, s % 2, :], psG[:, s % 2, :], ACT.Silu).then_inc(silued, 1)

                def take_y(b, s, n):
                    act.wait_ge(y_ready, b + 1)
                    wait_past(act, y_out[s], 16 * n)
                    act.activation(out[:, s, :], psY[:, 0:D], ACT.Copy).then_inc(y_taken, 1)

                run(act, [(1, take_x), (0, silu), (-2, take_y)])

            @block.vector
            def _(dve):
                def product(b, s, n):
                    dve.wait_ge(silued, b + 1)
                    wait_past(dve, h_turned, b - 1)
                    dve.tensor_tensor(h[:, s % 2, :], psU[:, s % 2, :], sg[:, s % 2, :], ALU.mult).then_inc(hb_ready, 1)

                def take_h(b, s, n):
                    dve.wait_ge(h_turned, b + 1)
                    wait_past(dve, y_ready, b - 1)
                    dve.tensor_scalar(hT[:, s % 2, :], psH[:, s % 2, :], 1.0, None, ALU.mult).then_inc(ht_ready, 1)

                run(dve, [(0, product), (-1, take_h)])

        m.part = "exg"
        asked, gathered, carried, combined, x_added = m.sem("asked"), [m.sem(f"gathered{s}") for s in range(4)], *(
            m.sem(n) for n in ("carried", "combined", "x_added"))
        LATE = range(UNITS, G * C)
        with nc.Block() as block:
            @block.gpsimd
            def _(pool):
                def gather(i, s, n):
                    pool.wait_ge(asked, i + 1)
                    wait_past(pool, combined, i - 3)
                    wait_past(pool, carried, i)
                    pool.tensor_tensor(spare[:, :], zero[:, 0:1], zero[:, 0:1], ALU.add).then_inc(carried, 1)
                    pool.indirect_dma_start(row[:, s, :], None, ys, bass.IndirectOffsetOnAxis(ap=idx[:, s:s + 1], axis=0)).then_inc(gathered[s], 16)

                pipelined(pool, NT, [(0, gather)], period=4)

            @block.tensor
            def _(pe):
                for q in LATE:
                    shared_up(pe, q, q % C, q // C)
                    if q > UNITS:
                        shared_down(pe, q - 1, (q - 1) % C, (q - 1) // C, (q - 1) // C % 2)
                shared_down(pe, LATE[-1], C - 1, G - 1, (G - 1) % 2)

            @block.scalar
            def _(act):
                for q in LATE:
                    shared_silu(act, q, q % 2)
                    if q % C == 0 and q > UNITS:
                        shared_take(act, q // C - 1, (q // C - 1) % 2)
                shared_take(act, G - 1, (G - 1) % 2)

            @block.vector
            def _(dve):
                def ask(i, s, n):
                    wait_past(dve, gathered[s % 4], 16 * (2 * n + s // 4))
                    dve.tensor_copy(idx[:, s % 4:s % 4 + 1], pos[:, bass.ds(i, 1)]).then_inc(asked, 1)

                def product(i, s, n):
                    if s % 2 == 0 and not (isinstance(i, int) and i >= 2 * len(LATE)):
                        shared_product(dve, UNITS + 4 * n + s // 2, s // 2 % 2)

                def combine(i, s, n):
                    dve.wait_ge(gathered[s % 4], 16 * (2 * n + s // 4) + 16)
                    dve.wait_ge(s_written, 2 * n + s // 4 + 1)
                    mine = S[:, bass.ds(i, 1), :].rearrange("p a d -> p (a d)")
                    dve.scalar_tensor_tensor(mine, row[:, s % 4, :], weight[:, bass.ds(i, 1)], mine, ALU.mult, ALU.add).then_inc(combined, 1)

                def residual(i, s, n):
                    dve.wait_ge(combined, i + 1)
                    mine = m.X[:, bass.ds(i, 1), :]
                    dve.tensor_tensor(mine, mine, S[:, bass.ds(i, 1), :], ALU.add).then_inc(x_added, 1)

                def measure(i, s, n):
                    dve.wait_ge(x_added, i + 1)
                    dve.bn_stats(m.stats[:, i, :], m.X[:, i, :])

                pipelined(dve, NT, [(3, ask), (0, product), (0, combine), (-1, residual), (-2, measure)], period=8)


HID2, EXP2 = 32, 64
GROUP = 64
BUDGET = TOK // GROUP * 16
HALF = TOK // 2
NG = HALF // GROUP


def sort_levels():
    run = 2
    while run <= HALF:
        dist = run // 2
        while dist:
            yield run, dist
            dist //= 2
        run *= 2


def compare(dve, src, dst, run, dist):
    if run >= HALF:
        s = src.rearrange("p (b two d) -> p b two d", two=2, d=dist)
        o = dst.rearrange("p (b two d) -> p b two d", two=2, d=dist)
        dve.tensor_tensor(o[:, :, 0, :], s[:, :, 0, :], s[:, :, 1, :], ALU.max)
        return dve.tensor_tensor(o[:, :, 1, :], s[:, :, 0, :], s[:, :, 1, :], ALU.min)
    s = src.rearrange("p (r way b two d) -> p r way b two d", way=2, b=run // 2 // dist, two=2, d=dist)
    o = dst.rearrange("p (r way b two d) -> p r way b two d", way=2, b=run // 2 // dist, two=2, d=dist)
    for way in range(2):
        a, b = s[:, :, way, :, 0, :], s[:, :, way, :, 1, :]
        dve.tensor_tensor(o[:, :, way, :, way, :], a, b, ALU.max)
        last = dve.tensor_tensor(o[:, :, way, :, 1 - way, :], a, b, ALU.min)
    return last


def grouped_ffn(nc, m, t):
    C = EXP2 * HID2 // P
    EC = EXP2 // C
    with ExitStack() as own:
        def sb(name, shape, dt=F32, on=own):
            return on.enter_context(nc.sbuf_tensor(f"gr_{name}", shape, dt))

        def pb(name, shape, dt=F32, on=own):
            return on.enter_context(nc.psum_tensor(f"gr_{name}", shape, dt))

        V = sb("V", [P, HALF])
        wu, wg, wd = sb("wu", [P, EXP2, HID2]), sb("wg", [P, EXP2, HID2]), sb("wd", [P, C, D])
        bu, bg = sb("bu", [P, C]), sb("bg", [P, C])
        bd = sb("bd", [EXP2, D])
        SOME = EXP2 // 2
        pick = sb("pick", [3 * SOME, SOME, HID2], BF16)
        with ExitStack() as routing:
            S = sb("S", [P, NT, EXP2], on=routing)
            m.part = "gr"
            w_loaded = m.sem("w_loaded")
            A, B = sb("A", [P, HALF], on=routing), sb("B", [P, HALF], on=routing)
            br = sb("br", [P, EXP2], on=routing)
            sgn = sb("sgn", [P, 1], on=routing)
            mats = sb("mats", [P, 7, P], on=routing)
            ALL, SAME_HALF, SAME_EXP, LOW_UP, EARLIER, SWAP, LOW_UP_EXP = range(7)
            top, total = sb("top", [P, NT], on=routing), sb("total", [P, NT], on=routing)
            gsum, gmin = sb("gsum", [P, NG], on=routing), sb("gmin", [P, NG], on=routing)
            eq, sel, rank, excl = (sb(n, [P, NG], on=routing) for n in ("eq", "sel", "rank", "excl"))
            ones = sb("ones", [P, HALF], on=routing)
            count, cols = sb("count", [P, 4], on=routing), sb("cols", [P, 8], on=routing)
            cur, bit = (sb(n, [P, 1], I32, on=routing) for n in ("cur", "bit"))
            loaded = m.sem("loaded")

            def loads(sp):
                sp.dma_start(br[:, :], t["L2_ffn_br"].partition_broadcast(P)).then_inc(loaded, 16)
                sp.dma_start(mats[:, :, :], t["c_mats"]).then_inc(loaded, 16)
                sp.dma_start(sgn[:, :], t["c_sign"]).then_inc(loaded, 16)
                sp.dma_start(wu[:, :, :], t["L2_ffn_Wup"].rearrange("e d h -> d e h")).then_inc(w_loaded, 16)
                sp.dma_start(wg[:, :, :], t["L2_ffn_Wgate"].rearrange("e d h -> d e h")).then_inc(w_loaded, 16)
                sp.dma_start(wd[:, :, :], t["L2_ffn_Wdown"].rearrange("(c e) h d -> (e h) c d", e=EC)).then_inc(w_loaded, 16)
                sp.dma_start(bu[:, :], t["bup_cols"]).then_inc(w_loaded, 16)
                sp.dma_start(bg[:, :], t["bgate_cols"]).then_inc(w_loaded, 16)
                sp.dma_start(bd[:, :], t["L2_ffn_bdown"]).then_inc(w_loaded, 16)

            layer_norm(nc, m, "ln5", router=(t["L2_ffn_Wr"], S), also=loads)
            m.part = "gr"
            psV = pb("psV", [P, 4, 512], on=routing)
            psC = pb("psC", [P, 512], on=routing)
            psR = pb("psR", [P, 512], on=routing)
            chained, shifted, exped, s_ready, turned, v_taken, swapped, swap_in = (m.sem(n) for n in (
                "chained", "shifted", "exped", "s_ready", "turned", "v_taken", "swapped", "swap_in"))
            picked, counted, total_ready, asked, answered, kept, summed = (m.sem(n) for n in (
                "picked", "counted", "total_ready", "asked", "answered", "kept", "summed"))
            BITS, STEP = 30, 3
            TRIED = 2 ** STEP - 1
            of_expert = sb("of_expert", [3 * SOME, SOME], on=routing)
            reach, tried = sb("reach", [P, TRIED, NG], on=routing), sb("tried", [P, TRIED], on=routing)
            more, cand, flag = (sb(n, [P, TRIED], I32, on=routing) for n in ("more", "cand", "flag"))

            with nc.Block() as block:
                @block.sync
                def _(sp):
                    sp.wait_ge(swapped, 1)
                    for hf in range(2):
                        sp.dma_start(B[EXP2 * hf:EXP2 * hf + EXP2, :], A[EXP2 * (1 - hf):EXP2 * (1 - hf) + EXP2, :]).then_inc(swap_in, 16)
                    sp.wait_ge(w_loaded, 16 * 6)

                @block.gpsimd
                def _(pool):
                    pool.tensor_tensor(of_expert[:, :], m.fold[0:3 * SOME, 0:SOME], m.fold[0:3 * SOME, SOME:EXP2], ALU.add).then_inc(picked, 1)
                    pool.wait_ge(picked, 1)
                    pool.tensor_copy(pick[:, :, :], of_expert[:, :].unsqueeze(2).broadcast_to([3 * SOME, SOME, HID2])).then_inc(picked, 1)
                    pool.wait_ge(picked, 2)

                @block.scalar
                def _(act):
                    act.wait_ge(shifted, 1)
                    act.activation(S[:, :, :], S[:, :, :], ACT.Exp).then_inc(exped, 1)
                    act.wait_ge(turned, 1)
                    act.activation(V[:, :], psV[:, :, :].rearrange("p a b -> p (a b)"), ACT.Copy).then_inc(v_taken, 1)

                @block.vector
                def _(dve):
                    chain = Chain(dve, chained)
                    dve.memset(ones[:, :], 1.0)
                    dve.memset(cur[:, :], 0)
                    chain.link(dve.memset(more[:, :], 0x7F7FFFFF))
                    dve.memset(more[:, 0:1], 1 << BITS)
                    wide = lambda v: v[:, :].unsqueeze(2).broadcast_to([P, NT, EXP2])
                    dve.wait_ge(loaded, 48)
                    chain.link(dve.tensor_tensor(S[:, :, :], S[:, :, :], br[:, :].unsqueeze(1).broadcast_to([P, NT, EXP2]), ALU.add))
                    chain.link(dve.tensor_reduce(top[:, :], S[:, :, :], AX.X, ALU.max))
                    dve.tensor_tensor(S[:, :, :], S[:, :, :], wide(top), ALU.subtract).then_inc(shifted, 1)
                    dve.wait_ge(exped, 1)
                    chain.link(dve.tensor_reduce(total[:, :], S[:, :, :], AX.X, ALU.add))
                    chain.link(dve.reciprocal(total[:, :], total[:, :]))
                    dve.tensor_tensor(B[:, :].rearrange("p (i h e) -> p h i e", h=2, e=EXP2), S[:, :, :].rearrange("p (h i) e -> p h i e", h=2),
                                      wide(total).rearrange("p (h i) e -> p h i e", h=2), ALU.mult).then_inc(s_ready, 1)
                    dve.wait_ge(v_taken, 1)
                    chain.link(dve.tensor_scalar(A[:, :], V[:, :], sgn[:, 0:1], None, ALU.mult))
                    here, there = A, B
                    for run, dist in sort_levels():
                        last = compare(dve, here[:, :], there[:, :], run, dist)
                        here, there = there, here
                        if (run, dist) != (HALF, 1):
                            chain.link(last)
                    assert here is A
                    last.then_inc(swapped, 1)
                    dve.wait_ge(swap_in, 32)
                    chain.link(dve.scalar_tensor_tensor(B[:, :], B[:, :], -1.0, A[:, :], ALU.mult, ALU.max))
                    chain.link(dve.tensor_scalar(A[:, :], B[:, :], sgn[:, 0:1], None, ALU.mult))
                    here, there = A, B
                    dist = HALF // 2
                    while dist >= GROUP:
                        chain.link(compare(dve, here[:, :], there[:, :], HALF, dist))
                        here, there = there, here
                        dist //= 2
                    by_group = here[:, :].rearrange("p (c g) -> p c g", g=GROUP)
                    dve.tensor_reduce(gmin[:, :], by_group, AX.X, ALU.min)
                    chain.link(dve.tensor_reduce(gsum[:, :], by_group, AX.X, ALU.add))
                    before, LINKS = chain.n, 6
                    full = [P, TRIED, NG]

                    def try_bits(k):
                        c = Chain(dve, chained, before + LINKS * k)
                        c.link(dve.tensor_scalar(cand[:, :], more[:, :], cur[:, 0:1], None, ALU.bitwise_or))
                        c.link(dve.tensor_tensor(reach[:, :, :], gsum[:, :].unsqueeze(1).broadcast_to(full),
                                                 cand[:, :].bitcast(F32).unsqueeze(2).broadcast_to(full), ALU.is_ge))
                        dve.tensor_reduce(tried[:, :], reach[:, :, :], AX.X, ALU.add).then_inc(counted, 1)
                        dve.wait_ge(total_ready, k + 1)
                        c.link(dve.tensor_scalar(flag[:, :], psC[:, 0:TRIED], float(BUDGET), -1.0, ALU.is_ge, ALU.mult))
                        c.link(dve.tensor_tensor(flag[:, :], flag[:, :], more[:, :], ALU.bitwise_and))
                        dve.tensor_scalar(more[:, :], more[:, :], STEP, None, ALU.logical_shift_right)
                        c.link(dve.tensor_reduce(bit[:, :], flag[:, :], AX.X, ALU.max))
                        c.link(dve.tensor_tensor(cur[:, :], cur[:, :], bit[:, :], ALU.bitwise_or))
                        assert c.n == LINKS

                    try_bits(0)
                    for n in range(TRIED):
                        last = dve.memset(more[:, n:n + 1], (n + 1) << (BITS - STEP))
                    chain.n = before + LINKS
                    chain.link(last)
                    before += 1
                    with dve.Fori(1, BITS // STEP + 1) as k:
                        try_bits(k)
                    chain.n = before + LINKS * (BITS // STEP + 1)
                    tau = cur[:, :].bitcast(F32)
                    dve.tensor_scalar(sel[:, :], gsum[:, :], tau, None, ALU.is_gt, ALU.add, accum_out=cols[:, 0:1])
                    dve.tensor_scalar(eq[:, :], gsum[:, :], tau, None, ALU.is_equal, ALU.add, accum_out=cols[:, 1:2]).then_inc(asked, 1)
                    dve.wait_ge(answered, 1)
                    dve.tensor_scalar(cols[:, 2:3], psR[:, 0:1], -1.0, float(BUDGET), ALU.mult, ALU.add)
                    chain.link(dve.tensor_copy(excl[:, :], psR[:, 64:64 + NG]))
                    chain.link(dve.tensor_tensor_scan(rank[:, :], ones[:, 0:NG], excl[:, :], 0.0, ALU.mult, ALU.add))
                    chain.link(dve.tensor_tensor(rank[:, :], rank[:, :], excl[:, :], ALU.subtract))
                    chain.link(dve.tensor_tensor(rank[:, :], rank[:, :], psR[:, 128:128 + NG], ALU.add))
                    chain.link(dve.tensor_scalar(rank[:, :], rank[:, :], psR[:, 1:2], None, ALU.add))
                    chain.link(dve.tensor_scalar(rank[:, :], rank[:, :], cols[:, 2:3], None, ALU.is_lt))
                    chain.link(dve.tensor_tensor(rank[:, :], rank[:, :], eq[:, :], ALU.mult))
                    chain.link(dve.tensor_tensor(sel[:, :], sel[:, :], rank[:, :], ALU.add))
                    dve.tensor_reduce(cols[:, 3:4], sel[:, :], AX.X, ALU.add)
                    dve.tensor_scalar(eq[:, :], sel[:, :], -2.0, 2.0, ALU.mult, ALU.add)
                    chain.link(dve.tensor_tensor(gmin[:, :], gmin[:, :], sel[:, :], ALU.mult))
                    chain.link(dve.tensor_tensor(gmin[:, :], gmin[:, :], eq[:, :], ALU.add))
                    dve.tensor_reduce(cols[:, 4:5], gmin[:, :], AX.X, ALU.min).then_inc(asked, 1)
                    dve.wait_ge(answered, 2)
                    dve.tensor_scalar(cols[:, 5:6], psR[:, 2:3], float(GROUP), None, ALU.mult)
                    chain.link(dve.tensor_tensor(cols[:, 6:7], psR[:, 3:4], cols[:, 4:5], ALU.min))
                    chain.link(dve.tensor_scalar(A[:, :], V[:, :], cols[:, 6:7], None, ALU.is_gt, ALU.add, accum_out=count[:, 0:1]))
                    dve.tensor_scalar(B[:, :], V[:, :], cols[:, 6:7], None, ALU.is_equal, ALU.add, accum_out=count[:, 1:2]).then_inc(asked, 1)
                    dve.wait_ge(answered, 3)
                    chain.link(dve.tensor_tensor(cols[:, 7:8], cols[:, 5:6], psR[:, 4:5], ALU.subtract))
                    chain.link(dve.tensor_tensor(cols[:, 7:8], cols[:, 7:8], psR[:, 5:6], ALU.subtract))
                    T = S[:, :, :].rearrange("p n e -> p (n e)")
                    chain.link(dve.tensor_tensor_scan(T, ones[:, :], B[:, :], 0.0, ALU.mult, ALU.add))
                    chain.link(dve.scalar_tensor_tensor(B[:, :], T, cols[:, 7:8], B[:, :], ALU.is_le, ALU.mult))
                    chain.link(dve.tensor_tensor(A[:, :], A[:, :], B[:, :], ALU.add))
                    dve.tensor_tensor(V[:, :], V[:, :], A[:, :], ALU.mult).then_inc(kept, 1)
                    dve.wait_ge(summed, 1)
                    chain.link(dve.tensor_scalar(A[:, :], psV[:, :, :].rearrange("p a b -> p (a b)"), 1e-6, None, ALU.add))
                    chain.link(dve.reciprocal(A[:, :], A[:, :]))
                    chain.link(dve.tensor_tensor(V[:, :], V[:, :], A[:, :], ALU.mult))

                @block.tensor
                def _(pe):
                    pe.wait_ge(s_ready, 1)
                    for i in range(NT // 2):
                        last = pe.transpose(psV[:, i // 4, i % 4 * P:i % 4 * P + P], B[:, i * P:i * P + P], m.ident[:, :])
                    last.then_inc(turned, 1)
                    with pe.Fori(0, BITS // STEP + 1) as k:
                        pe.wait_ge(counted, k + 1)
                        pe.matmul(psC[:, 0:TRIED], mats[:, ALL, :], tried[:, :], start=True, stop=True).then_inc(total_ready, 1)
                    pe.wait_ge(asked, 1)
                    pe.matmul(psR[:, 0:1], mats[:, ALL, :], cols[:, 0:1], start=True, stop=True)
                    pe.matmul(psR[:, 1:2], mats[:, LOW_UP, :], cols[:, 1:2], start=True, stop=True)
                    pe.matmul(psR[:, 64:64 + NG], mats[:, SAME_HALF, :], eq[:, :], start=True, stop=True)
                    pe.matmul(psR[:, 128:128 + NG], mats[:, EARLIER, :], eq[:, :], start=True, stop=True).then_inc(answered, 1)
                    pe.wait_ge(asked, 2)
                    pe.matmul(psR[:, 2:3], mats[:, SAME_EXP, :], cols[:, 3:4], start=True, stop=True)
                    pe.matmul(psR[:, 3:4], mats[:, SWAP, :], cols[:, 4:5], start=True, stop=True).then_inc(answered, 1)
                    pe.wait_ge(asked, 3)
                    pe.matmul(psR[:, 4:5], mats[:, SAME_EXP, :], count[:, 0:1], start=True, stop=True)
                    pe.matmul(psR[:, 5:6], mats[:, LOW_UP_EXP, :], count[:, 1:2], start=True, stop=True).then_inc(answered, 1)
                    pe.wait_ge(kept, 1)
                    for b in range(4):
                        last = pe.matmul(psV[:, b, :], mats[:, SAME_HALF, :], V[:, 512 * b:512 * b + 512], start=True, stop=True)
                    last.then_inc(summed, 1)

        m.part = "gf"
        with ExitStack() as second:
            fs = sb("fs", [EXP2, TOK], on=second)
            parts = sb("parts", [3 * SOME, 2, TOK], BF16, on=second)
            part = sb("part", [P, 3, HALF], BF16, on=second)
            rest = sb("rest", [P, HALF], on=second)
            fst = sb("fst", [EXP2, 512], on=second)
            su, tg, h = sb("su", [P, 2, 512], on=second), sb("tg", [P, 2, 512], on=second), sb("h", [P, 2, 512], on=second)
            psU, psG, psF = (pb(n, [P, 2, 512], on=second) for n in ("psU", "psG", "psF"))
            psY = pb("psY", [P, 4, D], on=second)
            chained, part_ready, fs_in, parts_in = (m.sem(n) for n in ("chained", "part_ready", "fs_in", "parts_in"))
            staged, up_ready, silued, gated, h_ready, down_done, x_added = (m.sem(n) for n in (
                "staged", "up_ready", "silued", "gated", "h_ready", "down_done", "x_added"))
            run = lambda eng, stages: pipelined(eng, NT // 4 * C, stages, period=C)

            with nc.Block() as block:
                @block.sync
                def _(sp):
                    lower, upper = slice(0, EXP2), slice(EXP2, P)
                    for hf, rows in enumerate((lower, upper)):
                        sp.dma_start(fs[:, HALF * hf:HALF * hf + HALF], V[rows, :]).then_inc(fs_in, 16)
                    for n in range(3):
                        sp.wait_ge(part_ready, n + 1)
                        for hf in range(2):
                            for k in range(2):
                                rows = slice(EXP2 * hf + SOME * k, EXP2 * hf + SOME * k + SOME)
                                sp.dma_start(parts[SOME * n:SOME * n + SOME, k, HALF * hf:HALF * hf + HALF], part[rows, n, :]).then_inc(parts_in, 16)

                @block.scalar
                def _(act):
                    def silu(q, s, g):
                        act.wait_ge(up_ready, q + 1)
                        wait_past(act, gated, q - 1)
                        act.activation(su[:, s % 2, :], psU[:, s % 2, :], ACT.Silu, bias=bu[:, s:s + 1]).then_inc(silued, 1)
                    run(act, [(0, silu)])

                @block.vector
                def _(dve):
                    chain = Chain(dve, chained)
                    dve.tensor_copy(part[:, 0, :], V[:, :]).then_inc(part_ready, 1)
                    dve.wait_ge(part_ready, 1)
                    chain.link(dve.tensor_tensor(rest[:, :], V[:, :], part[:, 0, :], ALU.subtract))
                    dve.tensor_copy(part[:, 1, :], rest[:, :]).then_inc(part_ready, 1)
                    dve.wait_ge(part_ready, 2)
                    dve.tensor_tensor(part[:, 2, :], rest[:, :], part[:, 1, :], ALU.subtract).then_inc(part_ready, 1)
                    dve.wait_ge(fs_in, 32)

                    def product(q, s, g):
                        if s == 0:
                            wait_past(dve, down_done, q - C + 1)
                            dve.tensor_scalar(fst[:, :], fs[:, bass.ds(512 * g, 512)], 1.0, None, ALU.mult).then_inc(staged, 1)
                        dve.wait_ge(silued, q + 1)
                        dve.scalar_tensor_tensor(tg[:, s % 2, :], psG[:, s % 2, :], bg[:, s:s + 1], su[:, s % 2, :],
                                                 ALU.add, ALU.mult).then_inc(gated, 1)
                        dve.wait_ge(gated, q + 1)
                        wait_past(dve, down_done, q - 1)
                        dve.tensor_tensor(h[:, s % 2, :], psF[:, s % 2, :], tg[:, s % 2, :], ALU.mult).then_inc(h_ready, 1)

                    def residual(q, s, g):
                        if s == C - 1:
                            dve.wait_ge(down_done, q + 1)
                            tiles = m.X[:, bass.ds(4 * g, 4), :]
                            dve.tensor_tensor(tiles, tiles, psY[:, :, :], ALU.add).then_inc(x_added, 1)

                    def measure(q, s, g):
                        if s == C - 1:
                            dve.wait_ge(x_added, g + 1)
                            for j in range(4):
                                dve.bn_stats(m.stats[:, 4 * g + j, :], m.X[:, 4 * g + j, :])

                    run(dve, [(0, product), (-1, residual), (-2, measure)])

                @block.tensor
                def _(pe):
                    def up(q, s, g):
                        wait_past(pe, h_ready, q - 1)
                        x = m.xT[:, bass.ds(512 * g, 512)]
                        pe.matmul(psU[:, s % 2, :], wu[:, EC * s:EC * s + EC, :].rearrange("p e h -> p (e h)"), x, start=True, stop=True)
                        pe.matmul(psG[:, s % 2, :], wg[:, EC * s:EC * s + EC, :].rearrange("p e h -> p (e h)"), x, start=True, stop=True)
                        if isinstance(q, int) and q == 0:
                            pe.wait_ge(parts_in, 16 * 12)
                        k, e = divmod(EC * s, SOME)
                        pe.matmul(psF[:, s % 2, :], pick[:, e:e + EC, :].rearrange("p e h -> p (e h)"),
                                  parts[:, k, bass.ds(512 * g, 512)], start=True, stop=True).then_inc(up_ready, 1)

                    def down(q, s, g):
                        if s == 0:
                            pe.wait_ge(staged, g + 1)
                            wait_past(pe, x_added, g)
                            for j in range(4):
                                pe.matmul(psY[:, j, :], fst[:, j * P:j * P + P], bd[:, :],
                                          start=(j == 0), stop=False, skip_group_check=True)
                        pe.wait_ge(h_ready, q + 1)
                        for j in range(4):
                            last = pe.matmul(psY[:, j, :], h[:, s % 2, j * P:j * P + P], wd[:, s, :],
                                             start=False, stop=(s == C - 1), skip_group_check=True)
                        last.then_inc(down_done, 1)

                    run(pe, [(0, up), (-1, down)])


HID3, EXP3 = 64, 64
GROUPS3, TOP_GROUPS = 8, 4
TOP3, CAP = 8, 128
OUT_SCALE = 2.5
ROW = D + EXP3
ACCS = 2
FAR = -1e30


def capacity_ffn(nc, m, t):
    GE = EXP3 // GROUPS3
    rows = nc.dram_tensor("cap_rows", (TOK + P, ROW), F32, kind="Internal").ap()
    accs = [nc.dram_tensor(f"cap_acc{n}", (TOK + P, D), F32, kind="Internal").ap() for n in range(ACCS)]
    tiles_of = lambda table: table[0:TOK, :].rearrange("(n p) d -> n p d", p=P)
    with ExitStack() as own:
        def sb(name, shape, dt=F32, on=own):
            return on.enter_context(nc.sbuf_tensor(f"cap_{name}", shape, dt))

        def pb(name, shape, dt=F32, on=own):
            return on.enter_context(nc.psum_tensor(f"cap_{name}", shape, dt))

        slot = sb("slot", [P, 1])
        base = sb("base", [P, EXP3])
        DT = sb("DT", [P, EXP3 // 4, P])
        ends = sb("ends", [P, EXP3 // 4])
        with ExitStack() as first:
            L = sb("L", [P, NT, EXP3], on=first)
            layer_norm(nc, m, "ln7", router=(t["gate_wT"], L), rows=tiles_of(rows)[:, :, 0:D])
            m.part = "cap"
            F = sb("F", [P, NT, EXP3], on=first)
            bias, tri = sb("bias", [P, EXP3], on=first), sb("tri", [P, GROUPS3, GROUPS3], on=first)
            hi, lo, a = (sb(n, [P, NT, GROUPS3, GE // 2], on=first) for n in ("hi", "lo", "a"))
            gt, eq = (sb(n, [P, NT, GROUPS3, GROUPS3], on=first) for n in ("gt", "eq"))
            score, pen = sb("score", [P, NT, GROUPS3], on=first), sb("pen", [P, NT, GROUPS3], on=first)
            st, rp, t8 = sb("st", [P, 4, EXP3], on=first), sb("rp", [P, 4, EXP3], on=first), sb("t8", [P, 4, 8], on=first)
            M = sb("M", [P, EXP3, NT], on=first)
            fresh = sb("fresh", [P, EXP3, NT], on=first)
            inc = sb("inc", [P, EXP3, NT], on=first)
            Mb, incb, excb = (sb(n, [P, EXP3, NT], BF16, on=first) for n in ("Mb", "incb", "excb"))
            upto, onesb = sb("upto", [P, P], on=first), sb("onesb", [P, P], BF16, on=first)
            uptob = sb("uptob", [P, P], BF16, on=first)
            total, spare = sb("total", [P, NT], on=first), sb("spare", [P, 1], on=first)
            zero = sb("zero", [P, (NT + 1) * D], on=first)
            dif, inner = sb("dif", [P, EXP3, NT], on=first), sb("inner", [P, 1], on=first)
            psC, psE = pb("psC", [P, 4, 512], on=first), pb("psE", [P, 4, 512], on=first)
            loaded, zeroed, chained, sigmoided, w_ready, w_out, z_out = (m.sem(n) for n in (
                "loaded", "zeroed", "chained", "sigmoided", "w_ready", "w_out", "z_out"))
            bits_ready, counted, ends_ready, inc_ready, dif_ready, dif_turned, dif_taken = (m.sem(n) for n in (
                "bits_ready", "counted", "ends_ready", "inc_ready", "dif_ready", "dif_turned", "dif_taken"))

            with nc.Block() as block:
                @block.sync
                def _(sp):
                    sp.dma_start(bias[:, :], t["L3_ffn_gate_bias"].partition_broadcast(P)).then_inc(loaded, 16)
                    sp.dma_start(tri[:, :, :], t["c_tri8"].partition_broadcast(P)).then_inc(loaded, 16)
                    sp.dma_start(slot[:, :], t["c_slot"]).then_inc(loaded, 16)
                    sp.dma_start(upto[:, :], t["c_upto"]).then_inc(loaded, 16)
                    sp.dma_start(inner[:, :], t["c_inner"]).then_inc(loaded, 16)
                    sp.wait_ge(zeroed, 1)
                    for acc in accs:
                        sp.dma_start(acc.rearrange("(n p) d -> p n d", p=P), zero[:, :].rearrange("p (n d) -> p n d", d=D)).then_inc(z_out, 16)
                    sp.dma_start(rows[TOK:TOK + P, :], zero[:, 0:ROW]).then_inc(z_out, 16)
                    sp.wait_ge(w_ready, 1)
                    sp.dma_start(tiles_of(rows)[:, :, D:ROW].rearrange("n p e -> p n e"), L[:, :, :]).then_inc(w_out, 16)
                    sp.wait_ge(z_out, 16 * (ACCS + 1))
                    sp.wait_ge(w_out, 16)

                @block.gpsimd
                def _(pool):
                    pool.memset(zero[:, :], 0.0).then_inc(zeroed, 1)

                @block.scalar
                def _(act):
                    act.activation(L[:, :, :], L[:, :, :], ACT.Sigmoid).then_inc(sigmoided, 1)
                    for half in range(2):
                        act.wait_ge(dif_turned, half + 1)
                        act.activation(DT[:, 8 * half:8 * half + 8, :], psE[:, 2 * half:2 * half + 2, :].rearrange("p a (b q) -> p (a b) q", q=P),
                                       ACT.Copy).then_inc(dif_taken, 1)

                @block.vector
                def _(dve):
                    chain = Chain(dve, chained)
                    dve.memset(fresh[:, :, :], 1.0)
                    chain.link(dve.memset(onesb[:, :], 1.0))
                    dve.memset(fresh[:, :, 0:1], 0.0)
                    dve.wait_ge(loaded, 80)
                    dve.tensor_copy(uptob[:, :], upto[:, :])
                    dve.wait_ge(sigmoided, 1)
                    chain.link(dve.tensor_tensor(F[:, :, :], L[:, :, :], bias[:, :].unsqueeze(1).broadcast_to([P, NT, EXP3]), ALU.add))
                    by_group = F[:, :, :].rearrange("p n (g e) -> p n g e", e=GE)
                    w = GE // 2
                    dve.tensor_tensor(hi[:, :, :, :], by_group[:, :, :, 0:w], by_group[:, :, :, w:GE], ALU.max)
                    chain.link(dve.tensor_tensor(lo[:, :, :, :], by_group[:, :, :, 0:w], by_group[:, :, :, w:GE], ALU.min))
                    while w > 1:
                        v = w // 2
                        chain.link(dve.tensor_tensor(a[:, :, :, 0:v], hi[:, :, :, 0:v], hi[:, :, :, v:w], ALU.min))
                        dve.tensor_tensor(a[:, :, :, v:w], lo[:, :, :, 0:v], lo[:, :, :, v:w], ALU.max)
                        chain.link(dve.tensor_tensor(hi[:, :, :, 0:v], hi[:, :, :, 0:v], hi[:, :, :, v:w], ALU.max))
                        chain.link(dve.tensor_tensor(lo[:, :, :, 0:v], a[:, :, :, 0:v], a[:, :, :, v:w], ALU.max))
                        w = v
                    chain.link(dve.tensor_tensor(score[:, :, :], hi[:, :, :, 0], lo[:, :, :, 0], ALU.add))
                    full = [P, NT, GROUPS3, GROUPS3]
                    own_score = score[:, :, :].unsqueeze(3).broadcast_to(full)
                    others = score[:, :, :].unsqueeze(2).broadcast_to(full)
                    dve.tensor_tensor(gt[:, :, :, :], others, own_score, ALU.is_gt)
                    chain.link(dve.tensor_tensor(eq[:, :, :, :], others, own_score, ALU.is_equal))
                    eqf = eq[:, :, :, :].rearrange("p n g h -> p n (g h)")
                    earlier = tri[:, :, :].rearrange("p g h -> p (g h)").unsqueeze(1).broadcast_to([P, NT, GROUPS3 * GROUPS3])
                    chain.link(dve.tensor_tensor(eqf, eqf, earlier, ALU.mult))
                    chain.link(dve.tensor_tensor(gt[:, :, :, :], gt[:, :, :, :], eq[:, :, :, :], ALU.add))
                    chain.link(dve.tensor_reduce(score[:, :, :], gt[:, :, :, :], AX.X, ALU.add))
                    chain.link(dve.tensor_scalar(pen[:, :, :], score[:, :, :], float(TOP_GROUPS), FAR, ALU.is_ge, ALU.mult))
                    before, LINKS = chain.n, 4
                    with dve.Fori(0, NT // 4) as k:
                        c = Chain(dve, chained, before + LINKS * k)
                        c.link(dve.tensor_tensor(st[:, :, :].rearrange("p j (g e) -> p j g e", e=GE),
                                                 F[:, bass.ds(4 * k, 4), :].rearrange("p j (g e) -> p j g e", e=GE),
                                                 pen[:, bass.ds(4 * k, 4), :].unsqueeze(3).broadcast_to([P, 4, GROUPS3, GE]), ALU.add))
                        dve.memset(spare[:, :], 0.0)
                        for j in range(4):
                            last = dve.max(t8[:, j, :], st[:, j, :])
                        c.link(last)
                        dve.memset(spare[:, :], 0.0)
                        for j in range(4):
                            last = dve.match_replace(rp[:, j, :], t8[:, j, :], st[:, j, :], 3 * FAR)
                        c.link(last)
                        c.link(dve.tensor_tensor(M[:, :, bass.ds(4 * k, 4)].rearrange("p e j -> p j e"), rp[:, :, :], st[:, :, :], ALU.not_equal))
                    chain.n = before + LINKS * (NT // 4)
                    dve.tensor_copy(Mb[:, :, :], M[:, :, :])
                    flat = lambda v: v[:, :, :].rearrange("p e n -> p (e n)")
                    chain.link(dve.tensor_tensor_scan(flat(inc), flat(fresh), flat(M), 0.0, ALU.mult, ALU.add))
                    dve.tensor_copy(incb[:, :, :], inc[:, :, :])
                    dve.tensor_tensor(excb[:, :, :], inc[:, :, :], M[:, :, :], ALU.subtract).then_inc(bits_ready, 1)
                    Mt = M[:, :, :].rearrange("p e n -> p n e")
                    chain.link(dve.tensor_tensor(L[:, :, :], L[:, :, :], Mt, ALU.mult))
                    chain.link(dve.tensor_reduce(total[:, :], L[:, :, :], AX.X, ALU.add))
                    chain.link(dve.tensor_scalar(total[:, :], total[:, :], 1e-20, None, ALU.add))
                    chain.link(dve.reciprocal(total[:, :], total[:, :]))
                    chain.link(dve.tensor_scalar(total[:, :], total[:, :], OUT_SCALE, None, ALU.mult))
                    dve.tensor_tensor(L[:, :, :], L[:, :, :], total[:, :].unsqueeze(2).broadcast_to([P, NT, EXP3]), ALU.mult).then_inc(w_ready, 1)
                    dve.wait_ge(counted, 1)
                    dve.tensor_copy(flat(inc), psC[:, :, :].rearrange("p a b -> p (a b)")).then_inc(inc_ready, 1)
                    dve.wait_ge(ends_ready, 1)
                    flatF = F[:, :, :].rearrange("p n e -> p (n e)")
                    dve.tensor_scalar(flatF, psE[:, :, :].rearrange("p a b -> p (a b)"), slot[:, 0:1], None, ALU.is_le).then_inc(inc_ready, 1)
                    dve.wait_ge(inc_ready, 2)
                    dve.tensor_tensor(dif[:, :, 0:NT - 1], inc[:, :, 1:NT], inc[:, :, 0:NT - 1], ALU.subtract)
                    dve.tensor_copy(dif[:, :, NT - 1:NT], inc[:, :, 0:1]).then_inc(dif_ready, 1)
                    chain.link(dve.tensor_reduce(base[:, :], flatF.rearrange("p (e n) -> p e n", n=NT), AX.X, ALU.add))
                    dve.tensor_scalar(base[:, :], base[:, :], float(NT - 1), float(P), ALU.min, ALU.mult)
                    dve.wait_ge(ends_ready, 2)
                    dve.tensor_scalar(ends[:, :], psC[:, 0, 0:EXP3 // 4], inner[:, 0:1], None, ALU.mult)

                @block.tensor
                def _(pe):
                    pe.wait_ge(bits_ready, 1)
                    fl = lambda v: v[:, :, :].rearrange("p e n -> p (e n)")
                    for b in range(4):
                        cols = slice(512 * b, 512 * b + 512)
                        pe.matmul(psC[:, b, :], uptob[:, :], fl(Mb)[:, cols], start=True, stop=False)
                        last = pe.matmul(psC[:, b, :], onesb[:, :], fl(excb)[:, cols], start=False, stop=True)
                    last.then_inc(counted, 1)
                    for b in range(4):
                        last = pe.matmul(psE[:, b, :], onesb[:, :], fl(incb)[:, 512 * b:512 * b + 512], start=True, stop=True)
                    last.then_inc(ends_ready, 1)
                    pe.wait_ge(inc_ready, 2)
                    for b in range(EXP3 // 4):
                        last = pe.matmul(psC[:, 0, b:b + 1], fl(inc)[:, b * P:b * P + P], m.ident[:, P - 1:P], start=True, stop=True)
                    last.then_inc(ends_ready, 1)
                    pe.wait_ge(dif_ready, 1)
                    for b in range(EXP3 // 4):
                        last = pe.transpose(psE[:, b // 4, b % 4 * P:b % 4 * P + P], fl(dif)[:, b * P:b * P + P], m.ident[:, :])
                        if b % 8 == 7:
                            last.then_inc(dif_turned, 1)

        m.part = "capx"
        with ExitStack() as second:
            GX = sb("GX", [P, 4, ROW], on=second)
            past_end, more = sb("past_end", [P, 2, P], on=second), sb("more", [P, 2, P], on=second)
            slots = sb("slots", [P, P], on=second)
            idx2 = sb("idx2", [P, 8], I32, on=second)
            spare, nought = sb("spare2", [P, 2], on=second), sb("nought", [P, 1], on=second)
            le, cnt, tok, past = sb("le", [P, P], on=second), sb("cnt", [P, 1], on=second), sb("tok", [P, 1], on=second), sb("past", [P, 1], on=second)
            wgu, wdn = sb("wgu", [P, 4, 2, HID3], on=second), sb("wdn", [HID3, 4, D], on=second)
            GT, sg, h = sb("GT", [P, 2, P], on=second), sb("sg", [HID3, 2, P], on=second), sb("h", [HID3, 2, P], on=second)
            Y = sb("Y", [P, 4, D], on=second)
            psQ, psT, psU, psY = (pb(n, [P, 2, 512], on=second) for n in ("psQ", "psT", "psU", "psY"))
            slots_in, prepared, picked, found, chained, turned, gt_ready, up_ready, silued, h_ready, down_ready, y_ready = (m.sem(n) for n in (
                "slots_in", "prepared", "picked", "found", "chained", "turned", "gt_ready", "up_ready", "silued", "h_ready", "down_ready", "y_ready"))
            cleared, carried = m.sem("cleared"), [m.sem(f"carried{k}") for k in range(2)]
            gx_in, w_in, added = ([m.sem(f"{n}{u}") for u in range(4)] for n in ("gx_in", "w_in", "added"))
            turn_of = lambda s, n: 2 * n + s // 4
            run = lambda eng, stages: pipelined(eng, EXP3, stages, period=8)

            with nc.Block() as block:
                @block.sync
                def _(sp):
                    sp.dma_start(slots[:, :], t["c_slots"].partition_broadcast(P)).then_inc(slots_in, 16)

                    def weights(e, s, n):
                        q = s % 4
                        wait_past(sp, down_ready, e - 3)
                        sp.dma_start(wgu[:, q, 0, :], t["L3_ffn_w_gate"][bass.ds(e, 1), :, :].rearrange("a d i -> (a d) i")).then_inc(w_in[q], 16)
                        sp.dma_start(wgu[:, q, 1, :], t["L3_ffn_w_up"][bass.ds(e, 1), :, :].rearrange("a d i -> (a d) i")).then_inc(w_in[q], 16)
                        sp.dma_start(wdn[:, q, :], t["L3_ffn_w_down"][bass.ds(e, 1), :, :].rearrange("a i d -> (a i) d")).then_inc(w_in[q], 16)
                    run(sp, [(0, weights)])

                @block.gpsimd
                def _(pool):
                    def carry(k, e):
                        wait_past(pool, carried[k], e)
                        pool.tensor_tensor(spare[:, k:k + 1], nought[:, :], nought[:, :], ALU.add).then_inc(carried[k], 1)

                    def gather_rows(e, s, n):
                        pool.wait_ge(found, e + 1)
                        wait_past(pool, y_ready, e - 3)
                        carry(0, e)
                        pool.indirect_dma_start(GX[:, s % 4, :], None, rows, bass.IndirectOffsetOnAxis(ap=idx2[:, s:s + 1], axis=0)).then_inc(gx_in[s % 4], 16)

                    def add(e, s, n):
                        pool.wait_ge(y_ready, e + 1)
                        wait_past(pool, added[(s - ACCS) % 4], 16 * (2 * n + (s + 4 - ACCS) // 4))
                        carry(1, e)
                        pool.indirect_dma_start(accs[s % ACCS], bass.IndirectOffsetOnAxis(ap=idx2[:, s:s + 1], axis=0), Y[:, s % 4, :], None,
                                                compute_op=ALU.add).then_inc(added[s % 4], 16)

                    pool.memset(nought[:, :], 0.0).then_inc(cleared, 1)
                    pool.wait_ge(cleared, 1)
                    run(pool, [(3, gather_rows), (-1, add)])
                    for s in range(4):
                        pool.wait_ge(added[s], 16 * EXP3 // 4)

                @block.vector
                def _(dve):
                    dve.wait_ge(slots_in, 16)

                    def prepare(e, s, n):
                        if s % 4 == 0:
                            wait_past(dve, picked, e - 4)
                            four = bass.ds(2 * n + s // 4, 1)
                            dve.tensor_scalar(past_end[:, s // 4, :], slots[:, :], ends[:, four], None, ALU.is_ge)
                            dve.tensor_scalar(more[:, s // 4, :], DT[:, four, :].rearrange("p a q -> p (a q)"), 1.0, None, ALU.mult).then_inc(prepared, 1)

                    def find(e, s, n):
                        dve.wait_ge(picked, e + 1)
                        wait_past(dve, added[s % 4], 16 * (turn_of(s, n) - 1))
                        wait_past(dve, found, e)
                        c = Chain(dve, chained, 3 * e)
                        c.link(dve.tensor_scalar(le[:, :], psQ[:, s % 2, 0:P], slot[:, 0:1], None, ALU.is_le, ALU.add, accum_out=cnt[:, :]))
                        c.link(dve.tensor_tensor(tok[:, :], cnt[:, :], base[:, bass.ds(e, 1)], ALU.add))
                        c.link(dve.scalar_tensor_tensor(past[:, :], tok[:, :], float(TOK), slot[:, :], ALU.is_ge, ALU.mult))
                        dve.tensor_tensor(idx2[:, s:s + 1], tok[:, :], past[:, :], ALU.add).then_inc(found, 1)

                    def product(e, s, n):
                        u = s % 2
                        dve.wait_ge(silued, e + 1)
                        wait_past(dve, down_ready, e - 1)
                        dve.tensor_tensor(h[:, u, :], psU[0:HID3, u, P:2 * P], sg[:, u, :], ALU.mult).then_inc(h_ready, 1)

                    run(dve, [(5, prepare), (3, find), (0, product)])

                @block.scalar
                def _(act):
                    def take(e, s, n):
                        act.wait_ge(turned, e + 1)
                        wait_past(act, up_ready, e - 1)
                        act.activation(GT[:, s % 2, :], psT[:, s % 2, 0:P], ACT.Copy).then_inc(gt_ready, 1)

                    def silu(e, s, n):
                        act.wait_ge(up_ready, e + 1)
                        wait_past(act, h_ready, e - 1)
                        act.activation(sg[:, s % 2, :], psU[0:HID3, s % 2, 0:P], ACT.Silu).then_inc(silued, 1)

                    def weigh(e, s, n):
                        act.wait_ge(down_ready, e + 1)
                        wait_past(act, added[s % 4], 16 * turn_of(s, n))
                        act.activation(Y[:, s % 4, :], psY[:, s % 2, 0:D], ACT.Copy, scale=GX[:, s % 4, bass.ds(D + e, 1)]).then_inc(y_ready, 1)

                    run(act, [(1, take), (0, silu), (-1, weigh)])

                @block.tensor
                def _(pe):
                    def pick(e, s, n):
                        pe.wait_ge(prepared, turn_of(s, n) + 1)
                        wait_past(pe, found, e - 1)
                        rows = slice(32 * (s % 4), 32 * (s % 4) + 32)
                        pe.matmul(psQ[:, s % 2, 0:P], past_end[rows, s // 4, :], more[rows, s // 4, :], start=True, stop=True).then_inc(picked, 1)

                    def turn(e, s, n):
                        pe.wait_ge(gx_in[s % 4], 16 * turn_of(s, n) + 16)
                        wait_past(pe, gt_ready, e - 1)
                        pe.transpose(psT[:, s % 2, 0:P], GX[:, s % 4, 0:D], m.ident[:, :]).then_inc(turned, 1)

                    def up(e, s, n):
                        pe.wait_ge(gt_ready, e + 1)
                        pe.wait_ge(w_in[s % 4], 48 * turn_of(s, n) + 48)
                        wait_past(pe, h_ready, e - 1)
                        pe.matmul(psU[0:HID3, s % 2, 0:P], wgu[:, s % 4, 0, :], GT[:, s % 2, :], start=True, stop=True)
                        pe.matmul(psU[0:HID3, s % 2, P:2 * P], wgu[:, s % 4, 1, :], GT[:, s % 2, :], start=True, stop=True).then_inc(up_ready, 1)

                    def down(e, s, n):
                        pe.wait_ge(h_ready, e + 1)
                        wait_past(pe, y_ready, e - 1)
                        pe.matmul(psY[:, s % 2, 0:D], h[:, s % 2, :], wdn[:, s % 4, :], start=True, stop=True).then_inc(down_ready, 1)

                    run(pe, [(4, pick), (1, turn), (0, up), (-1, down)])

        m.part = "capy"
        with ExitStack() as third:
            PARTS = 4
            S = sb("sums", [P, ACCS, NT, D], on=third)
            in_ = [m.sem(f"in{q}") for q in range(PARTS)]
            x_added, stored = m.sem("x_added"), m.sem("stored")
            tiles = [slice(NT // PARTS * q, NT // PARTS * (q + 1)) for q in range(PARTS)]
            with nc.Block() as block:
                @block.sync
                def _(sp):
                    for q in range(PARTS):
                        for n in range(ACCS):
                            sp.dma_start(S[:, n, tiles[q], :], tiles_of(accs[n])[tiles[q], :, :].rearrange("n p d -> p n d")).then_inc(in_[q], 16)
                    sp.wait_ge(stored, 16 * PARTS)

                @block.vector
                def _(dve):
                    for q in range(PARTS):
                        dve.wait_ge(in_[q], 16 * ACCS)
                        for n in range(ACCS):
                            if n:
                                dve.wait_ge(x_added, ACCS * q + n)
                            mine = m.X[:, tiles[q], :]
                            dve.tensor_tensor(mine, mine, S[:, n, tiles[q], :], ALU.add).then_inc(x_added, 1)

                @block.scalar
                def _(act):
                    out = t["out"].rearrange("(b e) s d -> (e s) b d", e=P // SEQ)
                    for q in range(PARTS):
                        act.wait_ge(x_added, ACCS * (q + 1))
                        act.dma_start(out[:, tiles[q], :], m.X[:, tiles[q], :]).then_inc(stored, 16)


def program(nc, t):
    with ExitStack() as stack:
        m = Memory(nc, stack)
        load_all(nc, m, t)
        with nc.sbuf_tensor("kept_Oall", [P, NT, D], F32) as Oall:
            attention(nc, m, "at0", "ln0", t["L0_xattn_W_q"], t["L0_xattn_W_k"], t["L0_xattn_W_v"],
                      add_mask=t["mask_Bx16xSxS2_ff0"], Oall=Oall,
                      lams=[t["L0_xattn_lambda_" + n] for n in ("q1", "k1", "q2", "k2")])
            differential_out(nc, m, "do0", Oall, t["L0_xattn_W_o"], t["rms_scale_col"])
        m.free_sems()
        bit_ffn(nc, m, t)
        m.free_sems()
        attention(nc, m, "at1", "ln2", *(t["L1_xattn_" + n] for n in ("wq", "wk", "wv", "wo", "bq", "bk", "bv", "bo")),
                  keep_mask=t["mask_1x1xSxS2_ik1"])
        m.free_sems()
        expert_ffn(nc, m, t)
        m.free_sems()
        attention(nc, m, "at2", "ln4", *(t["L2_xattn_" + n] for n in ("WqT", "WkT", "WvT", "WoT", "Wq_b", "Wk_b", "Wv_b", "Wo_b")))
        m.free_sems()
        grouped_ffn(nc, m, t)
        m.free_sems()
        attention(nc, m, "at3", "ln6", *(t["L3_xattn_" + n] for n in ("Wq", "Wk", "Wv", "Wo", "bq", "bk", "bv", "bo")))
        m.free_sems()
        capacity_ffn(nc, m, t)


def lay_out(inputs):
    import numpy as np

    t = {k: np.asarray(v) for k, v in inputs.items() if k != "itok_BxS2_0_2047"}
    t["ctxT"] = np.ascontiguousarray(t.pop("ctx_1024").reshape(TOK, D).T)
    for n in "qkvo":
        t[f"L2_xattn_W{n}T"] = np.ascontiguousarray(t.pop(f"L2_xattn_W{n}_w").T)
    t["rms_scale_col"] = np.ascontiguousarray(np.tile(t.pop("L0_xattn_rms_scale"), HEADS).reshape(P, 1))
    t["c_ident"] = np.eye(P, dtype=np.float32)
    t["c_order"] = np.arange(EXP1, 0, -1).astype(np.float32)
    t["bup_cols"] = np.ascontiguousarray(t.pop("L2_ffn_bup").reshape(-1, P).T)
    t["bgate_cols"] = np.ascontiguousarray(t.pop("L2_ffn_bgate").reshape(-1, P).T)
    p = np.arange(P)
    half, exp = p // EXP2, p % EXP2
    pairs = [np.ones((P, P), bool), half[:, None] == half, exp[:, None] == exp, half[:, None] < half,
             (half[:, None] == half) & (exp[:, None] < exp), (half[:, None] != half) & (exp[:, None] == exp),
             (half[:, None] < half) & (exp[:, None] == exp)]
    t["c_mats"] = np.ascontiguousarray(np.stack(pairs, 1).astype(np.float32))
    t["c_sign"] = (1.0 - 2.0 * half[:, None]).astype(np.float32)
    t["c_head_mask"] = np.stack([p // DH % 2 == 0, p // DH % 2 == 1, p // DH % 4 < 2, p // DH % 4 > 1], 1).astype(np.float32)
    t["c_fold"] = (p[:, None] % SEQ == np.arange(SEQ)).astype(np.float32)
    t["gate_wT"] = np.ascontiguousarray(t.pop("L3_ffn_gate_w").T)
    g = np.arange(GROUPS3)
    t["c_tri8"] = (g[None, :] < g[:, None]).astype(np.float32)
    t["c_slot"] = p.astype(np.float32)[:, None]
    t["c_blocks"] = np.arange(BLOCKS).astype(np.float32)
    t["c_upto"] = (p[:, None] <= p[None, :]).astype(np.float32)
    t["c_inner"] = (p % NT != NT - 1).astype(np.float32)[:, None]
    t["c_slots"] = p.astype(np.float32)
    return t


def kernel(**inputs):
    import concourse.bacc as bacc
    from concourse.bass_utils import run_bass_kernel_spmd

    nc = bacc.Bacc("TRN2", target_bir_lowering=False, num_devices=1)
    arrays = lay_out(inputs)
    t = {name: nc.dram_tensor(name, a.shape, mybir.dt.from_np(a.dtype), kind="ExternalInput").ap() for name, a in arrays.items()}
    t["out"] = nc.dram_tensor("out", (BATCH, SEQ, D), F32, kind="ExternalOutput").ap()
    program(nc, t)
    result = run_bass_kernel_spmd(nc, [arrays], core_ids=[0])
    return result.results[0]["out"]
```
